# Optimizing a Trainium2 kernel written in Bass

```python
import numpy as np
import jax
import jax.numpy as jnp

def _softmax(x, axis=-1):
    return jax.nn.softmax(x, axis=axis)

def _gelu(x):
    return jax.nn.gelu(x, approximate=True)

def _silu(x):
    return jax.nn.silu(x)

def _sigmoid(x):
    return jax.nn.sigmoid(x)

def _layernorm(x, axis=-1, eps=1e-05):
    m = jnp.mean(x, axis=axis, keepdims=True)
    v = jnp.var(x, axis=axis, keepdims=True)
    return (x - m) / jnp.sqrt(v + eps)

def _scatter_add(tgt, idx, src, axis=0):
    return tgt.at[idx].add(src)

def _segment_sum(src, seg, n):
    return jax.ops.segment_sum(src, seg, n)
kernel_name = 'mk_gnn_preln_d4_gnn_r32_197a06'

def setup_inputs(seed: int=0):
    np.random.seed(seed)
    _w = jnp.asarray

    def _rec_inputs():
        import jax
        import jax.numpy as jnp
        _gk = jax.random.key(seed)
        x = -0.000202 + 1 * jax.random.normal(jax.random.fold_in(_gk, 1), (3125, 64), jnp.float32)
        _s = jax.random.randint(jax.random.fold_in(_gk, 2), (50000,), 0, 3125, jnp.int32)
        _d = jax.random.randint(jax.random.fold_in(_gk, 3), (50000,), 0, 3125, jnp.int32)
        _loop = jnp.arange(3125, dtype=jnp.int32)
        src = jnp.concatenate([_s, _d, _loop])
        dst = jnp.concatenate([_d, _s, _loop])
        _o = jnp.argsort(dst, stable=True)
        src = src[_o]
        dst = dst[_o]
        edge_attr_16 = 0.000254156 + 0.999948 * jax.random.normal(jax.random.fold_in(_gk, 12), (103125, 16), jnp.float32)
        edge_attr_8 = 0.000398945 + 1.00003 * jax.random.normal(jax.random.fold_in(_gk, 13), (103125, 8), jnp.float32)
        return (x, src, dst, edge_attr_16, edge_attr_8)
    x, src, dst, edge_attr_16, edge_attr_8 = _rec_inputs()

    def _L0_gnn_setup():
        import jax, jax.numpy as jnp
        import numpy as np
        N_NODES = 3125
        N_EDGES = 50000
        D_IN = 64
        D_HID = 64
        D_OUT = 64

        def _glorot(key, fan_in, fan_out):
            lim = np.sqrt(6.0 / (fan_in + fan_out)).astype(np.float32)
            return jax.random.uniform(key, (fan_in, fan_out), jnp.float32, -lim, lim)

        def _sage_conv(x, src, dst, Wl, Wr, b):
            msg_sum = jax.ops.segment_sum(x[src], dst, num_segments=N_NODES)
            deg = jax.ops.segment_sum(jnp.ones((src.shape[0], 1), x.dtype), dst, num_segments=N_NODES)
            agg = msg_sum / jnp.maximum(deg, 1.0)
            return agg @ Wl + x @ Wr + b
        key = jax.random.key(seed)
        ks = jax.random.split(key, 8)
        x = jax.random.normal(ks[0], (N_NODES, D_IN), jnp.float32)
        edge_index = jax.random.randint(ks[1], (2, N_EDGES), 0, N_NODES, jnp.int64)
        Wl0 = _glorot(ks[2], D_IN, D_HID)
        Wr0 = _glorot(ks[3], D_IN, D_HID)
        Wl1 = _glorot(ks[4], D_HID, D_HID)
        Wr1 = _glorot(ks[5], D_HID, D_HID)
        Wl2 = _glorot(ks[6], D_HID, D_OUT)
        Wr2 = _glorot(ks[7], D_HID, D_OUT)
        b0 = jnp.zeros((D_HID,), jnp.float32)
        b1 = jnp.zeros((D_HID,), jnp.float32)
        b2 = jnp.zeros((D_OUT,), jnp.float32)
        return {'x': x, 'edge_index': edge_index, 'Wl0': Wl0, 'Wr0': Wr0, 'b0': b0, 'Wl1': Wl1, 'Wr1': Wr1, 'b1': b1, 'Wl2': Wl2, 'Wr2': Wr2, 'b2': b2}
    _L0_gnn_all = _L0_gnn_setup()
    _L0_gnn_in = {k: v for k, v in _L0_gnn_all.items() if k in ('Wl0', 'Wr0', 'b0', 'Wl1', 'Wr1', 'b1', 'Wl2', 'Wr2', 'b2')}
    del _L0_gnn_all

    def _L1_gnn_setup():
        import jax, jax.numpy as jnp
        import numpy as np
        NEG_SLOPE = 0.2
        BN_EPS = 1e-05
        key = jax.random.key(seed)
        ks = jax.random.split(key, 8)
        N, E, D_IN, D_OUT, D_EDGE = (50000, 25000, 64, 64, 8)
        x = jax.random.normal(ks[0], (N, D_IN), dtype=jnp.float32)
        edge_index = jax.random.randint(ks[1], (2, E), 0, N, dtype=jnp.int64)
        edge_attr = jax.random.normal(ks[2], (E, D_EDGE), dtype=jnp.float32)
        scale = 1.0 / np.sqrt(D_IN)
        W_l = jax.random.normal(ks[3], (D_IN, D_OUT), dtype=jnp.float32) * scale
        W_r = jax.random.normal(ks[4], (D_IN, D_OUT), dtype=jnp.float32) * scale
        b_l = jnp.zeros((D_OUT,), dtype=jnp.float32)
        b_r = jnp.zeros((D_OUT,), dtype=jnp.float32)
        att = jax.random.normal(ks[5], (D_OUT,), dtype=jnp.float32) * scale
        bias = jnp.zeros((D_OUT,), dtype=jnp.float32)
        gamma = jnp.ones((D_OUT,), dtype=jnp.float32)
        beta = jnp.zeros((D_OUT,), dtype=jnp.float32)
        return {'x': x, 'edge_index': edge_index, 'edge_attr': edge_attr, 'W_l': W_l, 'b_l': b_l, 'W_r': W_r, 'b_r': b_r, 'att': att, 'bias': bias, 'gamma': gamma, 'beta': beta}
    _L1_gnn_all = _L1_gnn_setup()
    _L1_gnn_in = {k: v for k, v in _L1_gnn_all.items() if k in ('W_l', 'b_l', 'W_r', 'b_r', 'att', 'bias', 'gamma', 'beta')}
    del _L1_gnn_all

    def _L2_gnn_setup():
        import jax, jax.numpy as jnp
        import numpy as np
        N_NODES = 3125
        N_EDGES = 50000
        D = 64
        K = 10
        ALPHA = 0.1
        key = jax.random.key(seed)
        kx, kw, kb, ks, kd = jax.random.split(key, 5)
        x = jax.random.normal(kx, (N_NODES, D), dtype=jnp.float32)
        lim = 1.0 / np.sqrt(D)
        W = jax.random.uniform(kw, (D, D), minval=-lim, maxval=lim, dtype=jnp.float32)
        b = jax.random.uniform(kb, (D,), minval=-lim, maxval=lim, dtype=jnp.float32)
        src = jax.random.randint(ks, (N_EDGES,), 0, N_NODES, dtype=jnp.int32)
        dst = jax.random.randint(kd, (N_EDGES,), 0, N_NODES, dtype=jnp.int32)
        return {'x': x, 'W': W, 'b': b, 'src': src, 'dst': dst}
    _L2_gnn_all = _L2_gnn_setup()
    _L2_gnn_in = {k: v for k, v in _L2_gnn_all.items() if k in ('W', 'b')}
    del _L2_gnn_all

    def _L3_gnn_setup():
        import jax, jax.numpy as jnp
        import numpy as np
        N, E = (50000, 25000)
        EMB, HEADS, EDGE_DIM = (64, 4, 16)
        NEG_SLOPE = 0.2
        LN_EPS = 1e-05
        key = jax.random.key(seed)
        ks = jax.random.split(key, 12)
        HC = HEADS * EMB
        inp = {'x': jax.random.normal(ks[0], (N, EMB), jnp.float32), 'edge_index': jax.random.randint(ks[1], (2, E), 0, N, jnp.int32), 'edge_attr': jax.random.normal(ks[2], (E, EDGE_DIM), jnp.float32), 'W': jax.random.normal(ks[3], (EMB, HC), jnp.float32) * 0.1, 'W_edge': jax.random.normal(ks[4], (EDGE_DIM, HC), jnp.float32) * 0.1, 'att_src': jax.random.normal(ks[5], (HEADS, EMB), jnp.float32) * 0.1, 'att_dst': jax.random.normal(ks[6], (HEADS, EMB), jnp.float32) * 0.1, 'att_edge': jax.random.normal(ks[7], (HEADS, EMB), jnp.float32) * 0.1, 'bias': jnp.zeros((HC,), jnp.float32), 'Wp': jax.random.normal(ks[8], (HC, EMB), jnp.float32) * 0.05, 'bp': jnp.zeros((EMB,), jnp.float32), 'gamma': jnp.ones((EMB,), jnp.float32), 'beta': jnp.zeros((EMB,), jnp.float32)}
        return inp
    _L3_gnn_all = _L3_gnn_setup()
    _L3_gnn_in = {k: v for k, v in _L3_gnn_all.items() if k in ('W', 'W_edge', 'att_src', 'att_dst', 'att_edge', 'bias', 'Wp', 'bp', 'gamma', 'beta')}
    del _L3_gnn_all
    return {'x': x, 'src': src, 'dst': dst, 'edge_attr_16': edge_attr_16, 'edge_attr_8': edge_attr_8, 'L0_gnn_Wl0': _L0_gnn_in['Wl0'], 'L0_gnn_Wr0': _L0_gnn_in['Wr0'], 'L0_gnn_b0': _L0_gnn_in['b0'], 'L0_gnn_Wl1': _L0_gnn_in['Wl1'], 'L0_gnn_Wr1': _L0_gnn_in['Wr1'], 'L0_gnn_b1': _L0_gnn_in['b1'], 'L0_gnn_Wl2': _L0_gnn_in['Wl2'], 'L0_gnn_Wr2': _L0_gnn_in['Wr2'], 'L0_gnn_b2': _L0_gnn_in['b2'], 'L1_gnn_W_l': _L1_gnn_in['W_l'], 'L1_gnn_b_l': _L1_gnn_in['b_l'], 'L1_gnn_W_r': _L1_gnn_in['W_r'], 'L1_gnn_b_r': _L1_gnn_in['b_r'], 'L1_gnn_att': _L1_gnn_in['att'], 'L1_gnn_bias': _L1_gnn_in['bias'], 'L1_gnn_gamma': _L1_gnn_in['gamma'], 'L1_gnn_beta': _L1_gnn_in['beta'], 'L2_gnn_W': _L2_gnn_in['W'], 'L2_gnn_b': _L2_gnn_in['b'], 'L3_gnn_W': _L3_gnn_in['W'], 'L3_gnn_W_edge': _L3_gnn_in['W_edge'], 'L3_gnn_att_src': _L3_gnn_in['att_src'], 'L3_gnn_att_dst': _L3_gnn_in['att_dst'], 'L3_gnn_att_edge': _L3_gnn_in['att_edge'], 'L3_gnn_bias': _L3_gnn_in['bias'], 'L3_gnn_Wp': _L3_gnn_in['Wp'], 'L3_gnn_bp': _L3_gnn_in['bp'], 'L3_gnn_gamma': _L3_gnn_in['gamma'], 'L3_gnn_beta': _L3_gnn_in['beta']}

def reference(x, src, dst, edge_attr_16, edge_attr_8, L0_gnn_Wl0, L0_gnn_Wr0, L0_gnn_b0, L0_gnn_Wl1, L0_gnn_Wr1, L0_gnn_b1, L0_gnn_Wl2, L0_gnn_Wr2, L0_gnn_b2, L1_gnn_W_l, L1_gnn_b_l, L1_gnn_W_r, L1_gnn_b_r, L1_gnn_att, L1_gnn_bias, L1_gnn_gamma, L1_gnn_beta, L2_gnn_W, L2_gnn_b, L3_gnn_W, L3_gnn_W_edge, L3_gnn_att_src, L3_gnn_att_dst, L3_gnn_att_edge, L3_gnn_bias, L3_gnn_Wp, L3_gnn_bp, L3_gnn_gamma, L3_gnn_beta):
    import jax
    import jax.numpy as jnp

    def _L0_gnn_ref(x, edge_index, Wl0, Wr0, b0, Wl1, Wr1, b1, Wl2, Wr2, b2):
        import jax, jax.numpy as jnp
        import numpy as np
        N_NODES = 3125
        N_EDGES = 50000
        D_IN = 64
        D_HID = 64
        D_OUT = 64

        def _glorot(key, fan_in, fan_out):
            lim = np.sqrt(6.0 / (fan_in + fan_out)).astype(np.float32)
            return jax.random.uniform(key, (fan_in, fan_out), jnp.float32, -lim, lim)

        def _sage_conv(x, src, dst, Wl, Wr, b):
            msg_sum = jax.ops.segment_sum(x[src], dst, num_segments=N_NODES)
            deg = jax.ops.segment_sum(jnp.ones((src.shape[0], 1), x.dtype), dst, num_segments=N_NODES)
            agg = msg_sum / jnp.maximum(deg, 1.0)
            return agg @ Wl + x @ Wr + b
        src, dst = (edge_index[0], edge_index[1])
        h = jax.nn.relu(_sage_conv(x, src, dst, Wl0, Wr0, b0))
        h = jax.nn.relu(_sage_conv(h, src, dst, Wl1, Wr1, b1))
        out = _sage_conv(h, src, dst, Wl2, Wr2, b2)
        return out

    def _L1_gnn_ref(x, edge_index, edge_attr, W_l, b_l, W_r, b_r, att, bias, gamma, beta):
        import jax, jax.numpy as jnp
        import numpy as np
        NEG_SLOPE = 0.2
        BN_EPS = 1e-05
        N = x.shape[0]
        xl = x @ W_l + b_l
        xr = x @ W_r + b_r
        loops = jnp.arange(N, dtype=edge_index.dtype)
        src = jnp.concatenate([edge_index[0], loops])
        dst = jnp.concatenate([edge_index[1], loops])
        pre = xl[src] + xr[dst]
        act = jnp.where(pre >= 0, pre, NEG_SLOPE * pre)
        scores = act @ att
        smax = jax.ops.segment_max(scores, dst, num_segments=N)
        ex = jnp.exp(scores - smax[dst])
        denom = jax.ops.segment_sum(ex, dst, num_segments=N)
        alpha = ex / denom[dst]
        out = jax.ops.segment_sum(alpha[:, None] * xl[src], dst, num_segments=N)
        out = out + bias
        mean = out.mean(axis=0)
        var = out.var(axis=0)
        out = (out - mean) * jax.lax.rsqrt(var + BN_EPS) * gamma + beta
        return out

    def _L2_gnn_ref(x, W, b, src, dst):
        import jax, jax.numpy as jnp
        import numpy as np
        N_NODES = 3125
        N_EDGES = 50000
        D = 64
        K = 10
        ALPHA = 0.1
        h0 = x @ W + b
        ones = jnp.ones((src.shape[0],), dtype=x.dtype)
        deg_out = jax.ops.segment_sum(ones, src, num_segments=N_NODES)
        deg_in = jax.ops.segment_sum(ones, dst, num_segments=N_NODES)
        norm_src = jnp.where(deg_out > 0, jax.lax.rsqrt(jnp.maximum(deg_out, 1.0)), 0.0)[:, None]
        norm_dst = jnp.where(deg_in > 0, jax.lax.rsqrt(jnp.maximum(deg_in, 1.0)), 0.0)[:, None]
        h = h0
        for _ in range(K):
            msg = (h * norm_src)[src]
            agg = jax.ops.segment_sum(msg, dst, num_segments=N_NODES)
            h = (1.0 - ALPHA) * (agg * norm_dst) + ALPHA * h0
        return h

    def _L3_gnn_ref(x, edge_index, edge_attr, W, W_edge, att_src, att_dst, att_edge, bias, Wp, bp, gamma, beta):
        import jax, jax.numpy as jnp
        import numpy as np
        N, E = (50000, 25000)
        EMB, HEADS, EDGE_DIM = (64, 4, 16)
        NEG_SLOPE = 0.2
        LN_EPS = 1e-05
        n = x.shape[0]
        H, C = att_src.shape
        xw = (x @ W).reshape(n, H, C)
        a_src_n = jnp.einsum('nhc,hc->nh', xw, att_src)
        a_dst_n = jnp.einsum('nhc,hc->nh', xw, att_dst)
        src, dst = (edge_index[0], edge_index[1])
        loop = jnp.arange(n, dtype=edge_index.dtype)
        cnt = jax.ops.segment_sum(jnp.ones_like(dst, jnp.float32), dst, num_segments=n)
        loop_attr = jax.ops.segment_sum(edge_attr, dst, num_segments=n) / jnp.maximum(cnt, 1.0)[:, None]
        src2 = jnp.concatenate([src, loop])
        dst2 = jnp.concatenate([dst, loop])
        ea = jnp.concatenate([edge_attr, loop_attr], axis=0)
        ew = (ea @ W_edge).reshape(-1, H, C)
        a_edge = jnp.einsum('ehc,hc->eh', ew, att_edge)
        alpha = a_src_n[src2] + a_dst_n[dst2] + a_edge
        alpha = jnp.where(alpha >= 0, alpha, NEG_SLOPE * alpha)
        amax = jax.ops.segment_max(alpha, dst2, num_segments=n)
        ae = jnp.exp(alpha - amax[dst2])
        denom = jax.ops.segment_sum(ae, dst2, num_segments=n)
        attn = ae / denom[dst2]
        msg = xw[src2] * attn[:, :, None]
        agg = jax.ops.segment_sum(msg, dst2, num_segments=n)
        gat_out = agg.reshape(n, H * C) + bias
        proj = gat_out @ Wp + bp
        h = x + jax.nn.elu(proj)
        mu = jnp.mean(h, axis=-1, keepdims=True)
        var = jnp.mean((h - mu) ** 2, axis=-1, keepdims=True)
        out = (h - mu) * jax.lax.rsqrt(var + LN_EPS) * gamma + beta
        return out
    edge_index = jnp.stack([src, dst])
    h = jnp.maximum(_layernorm(x, axis=-1), 0.0)
    x = x + _L0_gnn_ref(h, edge_index, L0_gnn_Wl0, L0_gnn_Wr0, L0_gnn_b0, L0_gnn_Wl1, L0_gnn_Wr1, L0_gnn_b1, L0_gnn_Wl2, L0_gnn_Wr2, L0_gnn_b2)
    h = jnp.maximum(_layernorm(x, axis=-1), 0.0)
    x = x + _L1_gnn_ref(h, edge_index, edge_attr_8, L1_gnn_W_l, L1_gnn_b_l, L1_gnn_W_r, L1_gnn_b_r, L1_gnn_att, L1_gnn_bias, L1_gnn_gamma, L1_gnn_beta)
    h = jnp.maximum(_layernorm(x, axis=-1), 0.0)
    x = x + _L2_gnn_ref(h, L2_gnn_W, L2_gnn_b, src, dst)
    h = jnp.maximum(_layernorm(x, axis=-1), 0.0)
    x = x + _L3_gnn_ref(h, edge_index, edge_attr_16, L3_gnn_W, L3_gnn_W_edge, L3_gnn_att_src, L3_gnn_att_dst, L3_gnn_att_edge, L3_gnn_bias, L3_gnn_Wp, L3_gnn_bp, L3_gnn_gamma, L3_gnn_beta)
    return x

_drawn_inputs = setup_inputs


def setup_inputs(seed=0):
    import zlib

    import numpy as np

    out = dict(_drawn_inputs(seed))
    spreads = {'L0_gnn_b0': (0.0, 0.1),
     'L0_gnn_b1': (0.0, 0.1),
     'L0_gnn_b2': (0.0, 0.1),
     'L1_gnn_b_l': (0.0, 0.333),
     'L1_gnn_b_r': (0.0, 0.36),
     'L1_gnn_bias': (0.0, 2.0),
     'L1_gnn_gamma': (1.0, 0.2),
     'L1_gnn_beta': (0.0, 0.1),
     'L3_gnn_bias': (0.0, 0.1),
     'L3_gnn_bp': (0.0, 0.1),
     'L3_gnn_gamma': (1.0, 0.2),
     'L3_gnn_beta': (0.0, 0.1)}
    factors = {'edge_attr_16': 8.0,
     'L3_gnn_W_edge': 6.501,
     'L3_gnn_att_src': 11.441,
     'L3_gnn_att_dst': 64.0,
     'L3_gnn_att_edge': 8.0}
    for name, (base, spread) in spreads.items():
        noise = np.random.default_rng([zlib.crc32(name.encode()), seed]).standard_normal(out[name].shape)
        drawn = base * np.exp(spread * noise) if base else spread * noise
        out[name] = jnp.asarray(drawn.astype(out[name].dtype))
    for name, factor in factors.items():
        out[name] = (out[name] * factor).astype(out[name].dtype)
    return out
```

```python
from contextlib import ExitStack

import concourse.bass as bass
from concourse import mybir

ALU = mybir.AluOpType
ACT = mybir.ActivationFunctionType
F32 = mybir.dt.float32
BF16 = mybir.dt.bfloat16
FP16 = mybir.dt.float16
I32 = mybir.dt.int32
U32 = mybir.dt.uint32
AX_X = mybir.AxisListType.X

NODES = 3125
CH = 25
LO = NODES // CH
D = 64
HEADS = 4
EDGES = 103125
EP = 125
ET = EDGES // EP
EPAD = 832
P = 128
U = 16
NI = 90
NT = U * NI
assert NT >= (EDGES + CH * CH * (P - 1)) // P and LO * CH == NODES and EP * ET == EDGES
REC = 6
MAGIC = 12582912.0
BIG = 1.0e30


class Chain:

    def __init__(self, eng, sem, start=0):
        self.eng, self.sem, self.n = eng, sem, start

    def __call__(self, ins):
        self.n = self.n + 1
        ins.then_inc(self.sem, 1)
        self.eng.wait_ge(self.sem, self.n)


class Stage:

    def __init__(self, nc, name):
        self.nc, self.name, self.ctx, self.sems = nc, name, ExitStack(), []

    def __enter__(self):
        return self

    def __exit__(self, *a):
        if self.sems:
            for sem in self.sems:
                self.nc.gpsimd.sem_clear(sem)
            self.nc.all_engine_barrier()
        self.ctx.close()

    def sb(self, name, shape, dt):
        return self.ctx.enter_context(self.nc.sbuf_tensor(f"{self.name}_{name}", shape, dt))

    def ps(self, name, shape, dt):
        return self.ctx.enter_context(self.nc.psum_tensor(f"{self.name}_{name}", shape, dt))

    def sem(self, name):
        self.sems.append(self.ctx.enter_context(self.nc.semaphore(f"{self.name}_{name}")))
        return self.sems[-1]


def build_constants(nc, g):
    with Stage(nc, "const") as st:
        ready = st.sem("ready")
        chain_sem = st.sem("chain")
        with nc.Block() as block:
            @block.gpsimd
            def _(pool):
                pool.iota(g.iota_free[:, :], [[1, P]], base=0, channel_multiplier=0,
                          allow_small_or_imprecise_dtypes=True).then_inc(ready, 1)
                pool.iota(g.iota_part[:, :], [[1, 1]], base=0, channel_multiplier=1,
                          allow_small_or_imprecise_dtypes=True).then_inc(ready, 1)

            @block.vector
            def _(v):
                done = Chain(v, chain_sem)
                v.wait_ge(ready, 2)
                v.tensor_scalar(g.ident[:, :], g.iota_free[:, :], g.iota_part[:, 0:1], None, ALU.is_equal)
                v.tensor_scalar(g.ident_h[:, :], g.iota_free[:, :], g.iota_part[:, 0:1], None, ALU.is_equal)
                v.tensor_scalar(g.ident_b[:, :], g.iota_free[:, :], g.iota_part[:, 0:1], None, ALU.is_equal)
                v.tensor_copy(g.iota_b[:, :], g.iota_free[:, :])
                v.tensor_scalar(g.before[:, :], g.iota_free[:, :], g.iota_part[:, 0:1], None, ALU.is_lt)
                v.tensor_scalar(g.after[:, :], g.iota_free[:, :], g.iota_part[:, 0:1], None, ALU.is_gt)
                done(v.tensor_scalar(g.off_diag[:, :], g.iota_free[:, :], g.iota_part[:, 0:1], -BIG,
                                     ALU.not_equal, ALU.mult))


def sort_edges(nc, g, src, dst, ea16, w_edge, att_edge):
    with Stage(nc, "sort") as st:
        chunk_s = st.sb("chunk_s", [EP, EPAD + 8], F32)
        chunk_d = st.sb("chunk_d", [EP, EPAD + 8], F32)
        bucket = st.sb("bucket", [EP, EPAD], F32)
        rank = st.sb("rank", [EP, EPAD], F32)
        rec = st.sb("rec", [EP, EPAD, REC], F32)

        with Stage(nc, "decode") as s2:
            src_i = s2.sb("src_i", [EP, ET], I32)
            dst_i = s2.sb("dst_i", [EP, ET], I32)
            attrs = s2.sb("attrs", [EP, ET, 16], F32)
            prod = s2.sb("prod", [EP, ET, 16], F32)
            we = s2.sb("we", [EP, 16, HEADS * D], F32)
            wp = s2.sb("wp", [EP, 16, HEADS * D], F32)
            att = s2.sb("att", [EP, HEADS * D], F32)
            wh = s2.sb("wh", [EP, 16, HEADS], F32)
            empty = s2.sb("empty", [P, U * REC], F32)
            nodes_in = s2.sem("nodes_in")
            attrs_in = s2.sem("attrs_in")
            weights_in = s2.sem("weights_in")
            empty_set = s2.sem("empty_set")
            chain_sem = s2.sem("chain")
            with nc.Block() as block:
                @block.sync
                def _(sp):
                    sp.dma_start(src_i[:, :], src.rearrange("(p t) -> p t", p=EP)).then_inc(nodes_in, 16)
                    sp.dma_start(dst_i[:, :], dst.rearrange("(p t) -> p t", p=EP)).then_inc(nodes_in, 16)
                    sp.dma_start(we[:, :, :].rearrange("p k c -> p (k c)"),
                                 w_edge.rearrange("(a k) c -> a (k c)", a=1).to_broadcast([EP, 16 * HEADS * D])
                                 ).then_inc(weights_in, 16)
                    sp.dma_start(att[:, :], att_edge.rearrange("(a h) c -> a (h c)", a=1)
                                 .to_broadcast([EP, HEADS * D])).then_inc(weights_in, 16)
                    sp.dma_start(attrs[:, :, :], ea16.rearrange("(p t) k -> p t k", p=EP)).then_inc(attrs_in, 16)

                @block.gpsimd
                def _(pool):
                    pool.memset(empty[:, :], 0.0).then_inc(empty_set, 1)
                    pool.wait_ge(empty_set, 1)
                    pool.memset(empty[:, :].rearrange("p (n r) -> p n r", r=REC)[:, :, 0:2], -1.0
                                ).then_inc(empty_set, 1)
                    pool.wait_ge(empty_set, 2)
                    slots = g.slots.rearrange("p (n u) r -> p n (u r)", u=U)
                    pool.dma_start(slots, empty[:, :].rearrange("p (a f) -> p a f", a=1)
                                   .to_broadcast([P, NI, U * REC])).then_inc(g.cleared, 16)
                    pool.wait_ge(g.cleared, 16)

                @block.vector
                def _(v):
                    done = Chain(v, chain_sem)
                    v.memset(chunk_s[:, ET:EPAD + 8], -1.0)
                    v.memset(chunk_d[:, ET:EPAD + 8], -1.0)
                    v.memset(bucket[:, ET:EPAD], -1.0)
                    v.wait_ge(nodes_in, 32)
                    for ids, chunk, field in ((src_i, chunk_s, 0), (dst_i, chunk_d, 1)):
                        done(v.tensor_copy(rank[:, 0:ET], ids[:, :]))
                        lo = rec[:, 0:ET, field]
                        done(v.tensor_scalar(lo, rank[:, 0:ET], 1.0 / CH, -0.48, ALU.mult, ALU.add))
                        done(v.tensor_scalar(lo, lo, MAGIC, MAGIC, ALU.add, ALU.subtract))
                        done(v.scalar_tensor_tensor(out=chunk[:, 0:ET], in0=lo, scalar=-float(CH),
                                                    in1=rank[:, 0:ET], op0=ALU.mult, op1=ALU.add))
                    done(v.scalar_tensor_tensor(out=bucket[:, 0:ET], in0=chunk_d[:, 0:ET], scalar=float(CH),
                                                in1=chunk_s[:, 0:ET], op0=ALU.mult, op1=ALU.add))
                    v.wait_ge(weights_in, 32)
                    done(v.tensor_tensor(wp[:, :, :], we[:, :, :],
                                         att[:, :].rearrange("p (a c) -> p a c", a=1)
                                         .to_broadcast([EP, 16, HEADS * D]), ALU.mult))
                    done(v.tensor_reduce(wh[:, :, :], wp[:, :, :].rearrange("p k (h c) -> p k h c", h=HEADS),
                                         AX_X, ALU.add))
                    v.wait_ge(attrs_in, 16)
                    for h in range(HEADS):
                        done(v.tensor_tensor(prod[:, :, :], attrs[:, :, :],
                                             wh[:, :, h].rearrange("p (a k) -> p a k", a=1)
                                             .to_broadcast([EP, ET, 16]), ALU.mult))
                        done(v.tensor_reduce(rec[:, 0:ET, 2 + h], prod[:, :, :], AX_X, ALU.add))

        pre = st.sb("pre", [CH, CH, EPAD + 1], F32)

        with Stage(nc, "count") as s2:
            GT = 16
            oh_s = [s2.sb(f"oh_s{k}", [EP, GT, CH], BF16) for k in range(2)]
            oh_d = [s2.sb(f"oh_d{k}", [EP, GT, CH], BF16) for k in range(2)]
            cnt = [s2.ps(f"cnt{k}", [CH, 512], F32) for k in range(2)]
            hot = s2.sem("hot")
            counted, copied = s2.sem("counted"), s2.sem("copied")
            n_iter = EPAD // (2 * GT)
            with nc.Block() as block:
                @block.vector
                def _(v):
                    v.memset(pre[:, :, 0:1], 0.0)
                    with v.Fori(0, n_iter) as i:
                        for k in range(2):
                            v.wait_ge(counted, i * 2 + k + 1)
                            for oh, chunk in ((oh_s[k], chunk_s), (oh_d[k], chunk_d)):
                                v.tensor_tensor(
                                    oh[:, :, :],
                                    chunk[:, bass.ds(i * 2 * GT + k * GT, GT)].rearrange("p (t a) -> p t a", a=1)
                                    .to_broadcast([EP, GT, CH]),
                                    g.iota_free[0:EP, 0:CH].rearrange("p (a c) -> p a c", a=1)
                                    .to_broadcast([EP, GT, CH]), ALU.is_equal).then_inc(hot, 1)

                @block.tensor
                def _(pe):
                    pe.sem_inc(counted, 2)
                    with pe.Fori(0, n_iter) as i:
                        for k in range(2):
                            pe.wait_ge(hot, i * 4 + 2 * k + 2)
                            pe.wait_ge(copied, i * 2 + k + 1)
                            for t in range(GT):
                                mm = pe.matmul(cnt[k][:, t * CH:(t + 1) * CH], oh_d[k][:, t, :], oh_s[k][:, t, :],
                                               start=True, stop=True)
                            mm.then_inc(counted, 1)

                @block.scalar
                def _(act):
                    act.sem_inc(copied, 2)
                    with act.Fori(0, n_iter) as i:
                        for k in range(2):
                            act.wait_ge(counted, i * 2 + k + 3)
                            act.activation(pre[:, :, bass.ds(i * 2 * GT + k * GT + 1, GT)],
                                           cnt[k][:, 0:GT * CH].rearrange("p (t c) -> p c t", c=CH),
                                           ACT.Copy).then_inc(copied, 1)

        with Stage(nc, "prefix") as s2:
            tiles = s2.sb("tiles", [CH, CH], F32)
            upto = s2.sb("upto", [CH, CH], F32)
            base = s2.sb("base", [CH, CH], F32)
            end = s2.sb("end", [CH, CH], F32)
            rows = s2.ps("rows", [CH, 1], F32)
            ends = s2.sb("ends", [NI, CH * CH], F32)
            tile_no = s2.sb("tile_no", [NI, U], F32)
            hits = s2.sb("hits", [NI, CH * CH], F32)
            tb = s2.sb("tb", [NI, U], F32)
            td = s2.sb("td", [NI, U], F32)
            ts = s2.sb("ts", [NI, U], F32)
            pairs = s2.sb("pairs", [NI, U, 2], I32)
            dsts = s2.sb("dsts", [NI, U], I32)
            cells = s2.sb("cells", [NI, U], I32)
            chain_sem = s2.sem("chain")
            summed, end_out, end_in = s2.sem("summed"), s2.sem("end_out"), s2.sem("end_in")
            row_base, numbered = s2.sem("row_base"), s2.sem("numbered")
            found, map_out = s2.sem("found"), s2.sem("map_out")
            with nc.Block() as block:
                @block.gpsimd
                def _(pool):
                    pool.iota(tile_no[:, :], [[1, U]], base=0, channel_multiplier=U,
                              allow_small_or_imprecise_dtypes=True).then_inc(numbered, 1)

                @block.tensor
                def _(pe):
                    pe.wait_ge(summed, 1)
                    pe.matmul(rows[:, :], g.after[0:CH, 0:CH], upto[:, CH - 1:CH], start=True, stop=True
                              ).then_inc(row_base, 1)

                @block.sync
                def _(sp):
                    sp.wait_ge(end_out, 1)
                    sp.dma_start(g.ends_dram, end[:, :]).then_inc(end_in, 16)
                    sp.wait_ge(end_in, 16)
                    sp.dma_start(ends[:, :], g.ends_dram.rearrange("(a d) s -> a (d s)", a=1)
                                 .to_broadcast([NI, CH * CH])).then_inc(end_in, 16)
                    sp.wait_ge(found, 1)
                    sp.dma_start(g.pairs_dram.rearrange("a (i u f) -> (a i) u f", u=U, f=2), pairs[:, :, :]).then_inc(map_out, 16)
                    sp.dma_start(g.dst_dram.rearrange("a (i u) -> (a i) u", u=U), dsts[:, :]).then_inc(map_out, 16)
                    sp.dma_start(g.cell_dram.rearrange("a (i u) -> (a i) u", u=U), cells[:, :]).then_inc(map_out, 16)
                    sp.wait_ge(map_out, 48)

                @block.vector
                def _(v):
                    done = Chain(v, chain_sem)
                    for cs in range(CH):
                        last = v.tensor_tensor_scan(pre[:, cs, :], pre[:, cs, :], pre[:, cs, :], 0.0,
                                                    ALU.add, ALU.bypass)
                        last.then_inc(chain_sem, 1)
                        done.n += 1
                    v.wait_ge(chain_sem, done.n)
                    done(v.tensor_scalar(tiles[:, :], pre[:, :, EPAD], P / 2 - 0.5, 1.0 / P, ALU.add, ALU.mult))
                    done(v.tensor_scalar(tiles[:, :], tiles[:, :], MAGIC, MAGIC, ALU.add, ALU.subtract))
                    done(v.tensor_tensor_scan(upto[:, :], tiles[:, :], tiles[:, :], 0.0, ALU.add, ALU.bypass))
                    v.sem_inc(summed, 1)
                    done(v.tensor_tensor(base[:, :], upto[:, :], tiles[:, :], ALU.subtract))
                    v.wait_ge(row_base, 1)
                    done(v.tensor_scalar(end[:, :], upto[:, :], rows[:, 0:1], None, ALU.add))
                    v.sem_inc(end_out, 1)
                    done(v.tensor_scalar(base[:, :], base[:, :], rows[:, 0:1], None, ALU.add))
                    done(v.scalar_tensor_tensor(
                        out=pre[:, :, :], in0=base[:, :].rearrange("p (c a) -> p c a", a=1)
                        .to_broadcast([CH, CH, EPAD + 1]), scalar=float(P), in1=pre[:, :, :],
                        op0=ALU.mult, op1=ALU.add))
                    v.wait_ge(end_in, 32)
                    v.wait_ge(numbered, 1)
                    for u in range(U):
                        done(v.tensor_scalar(hits[:, :], ends[:, :], tile_no[:, u:u + 1], None,
                                             ALU.is_le, ALU.add, accum_out=tb[:, u:u + 1]))
                    done(v.tensor_scalar(tb[:, :], tb[:, :], float(CH * CH - 1), None, ALU.min))
                    done(v.tensor_scalar(td[:, :], tb[:, :], 1.0 / CH, -0.48, ALU.mult, ALU.add))
                    done(v.tensor_scalar(td[:, :], td[:, :], MAGIC, MAGIC, ALU.add, ALU.subtract))
                    done(v.scalar_tensor_tensor(out=ts[:, :], in0=td[:, :], scalar=-float(CH), in1=tb[:, :],
                                                op0=ALU.mult, op1=ALU.add))
                    done(v.tensor_copy(pairs[:, :, 0], ts[:, :]))
                    done(v.tensor_copy(pairs[:, :, 1], td[:, :]))
                    done(v.tensor_copy(dsts[:, :], td[:, :]))
                    done(v.scalar_tensor_tensor(out=tb[:, :], in0=ts[:, :], scalar=float(CH), in1=td[:, :],
                                                op0=ALU.mult, op1=ALU.add))
                    done(v.tensor_copy(cells[:, :], tb[:, :]))
                    v.sem_inc(found, 1)

        KB, GT = 8, 4
        NB = EPAD // KB
        with Stage(nc, "place") as s2:
            b_t = s2.sb("b_t", [NB, KB, EP], FP16)
            oh_s = [s2.sb(f"oh_s{k}", [EP, GT, CH], F32) for k in range(2)]
            oh_d = [s2.sb(f"oh_d{k}", [EP, GT, CH], BF16) for k in range(2)]
            oh_t = [s2.sb(f"oh_t{k}", [CH, GT * EP], F32) for k in range(2)]
            same = s2.sb("same", [EP, 2 * GT, EP], F32)
            pick = [s2.sb(f"pick{k}", [EP, GT, CH], F32) for k in range(2)]
            ahead = s2.sb("ahead", [EP, EPAD], F32)
            slot_row = s2.sb("slot_row", [EP, ET], F32)
            slot_u = s2.sb("slot_u", [EP, ET], U32)
            ps_t = [s2.ps(f"ps_t{k}", [CH, 1024], BF16) for k in range(2)]
            ps_b = [s2.ps(f"ps_b{k}", [EP, 512], F32) for k in range(2)]
            ps_l = [s2.ps(f"ps_l{k}", [EP, 512], F32) for k in range(2)]
            turned, b_ready = s2.sem("turned"), s2.sem("b_ready")
            with nc.Block() as block:
                @block.tensor
                def _(pe):
                    for k in range(KB):
                        if k >= 2:
                            pe.wait_ge(b_ready, k - 1)
                        pe.transpose(ps_b[k % 2][0:NB, 0:EP], bucket[:, k::KB], g.ident[0:EP, 0:EP]
                                     ).then_inc(turned, 1)

                @block.scalar
                def _(act):
                    for k in range(KB):
                        act.wait_ge(turned, k + 1)
                        act.activation(b_t[:, k, :], ps_b[k % 2][0:NB, 0:EP], ACT.Copy).then_inc(b_ready, 1)

            hot = s2.sem("hot")
            t_ready, t_copied = s2.sem("t_ready"), s2.sem("t_copied")
            b_bcast, b_used = s2.sem("b_bcast"), s2.sem("b_used")
            looked, l_used = s2.sem("looked"), s2.sem("l_used")
            chain_sem = s2.sem("chain")
            with nc.Block() as block:
                @block.tensor
                def _(pe):
                    pe.sem_inc(looked, 2)
                    with pe.Fori(0, NB) as i:
                        for k in range(2):
                            n = i * 2 + k
                            pe.wait_ge(hot, n * 2 + 2)
                            pe.wait_ge(t_copied, n + 1)
                            for t in range(GT):
                                mm = pe.transpose(ps_t[k][:, t * P:t * P + EP], oh_d[k][:, t, :],
                                                  g.ident_b[0:EP, 0:EP])
                            mm.then_inc(t_ready, 1)
                            pe.wait_ge(b_used, n + 1)
                            pe.matmul(ps_b[k][:, 0:GT * EP], g.ident_h[0:NB, bass.ds(i, 1)].to_broadcast([NB, EP]),
                                      b_t[:, k * GT:(k + 1) * GT, :].rearrange("p t e -> p (t e)"),
                                      start=True, stop=True).then_inc(b_bcast, 1)
                            pe.wait_ge(t_copied, n + 3)
                            pe.wait_ge(l_used, n + 1)
                            for t in range(GT):
                                mm = pe.matmul(ps_l[k][:, t * CH:(t + 1) * CH], oh_t[k][:, t * EP:(t + 1) * EP],
                                               pre[:, :, bass.ds(i * KB + k * GT + t, 1)].rearrange("p c a -> p (c a)"),
                                               start=True, stop=True)
                            mm.then_inc(looked, 1)

                @block.scalar
                def _(act):
                    act.sem_inc(t_copied, 2)
                    with act.Fori(0, NB) as i:
                        for k in range(2):
                            act.wait_ge(t_ready, i * 2 + k + 1)
                            act.wait_ge(looked, i * 2 + k + 1)
                            act.activation(oh_t[k][:, :].rearrange("c (t e) -> c t e", t=GT),
                                           ps_t[k][:, 0:GT * P].rearrange("c (t e) -> c t e", t=GT)[:, :, 0:EP],
                                           ACT.Copy).then_inc(t_copied, 1)

                @block.vector
                def _(v):
                    v.sem_inc(b_used, 2)
                    v.sem_inc(l_used, 2)

                    def one_hots(k, col):
                        for oh, chunk in ((oh_s[k], chunk_s), (oh_d[k], chunk_d)):
                            v.tensor_tensor(
                                oh[:, :, :], chunk[:, col].rearrange("p (t a) -> p t a", a=1)
                                .to_broadcast([EP, GT, CH]),
                                g.iota_free[0:EP, 0:CH].rearrange("p (a c) -> p a c", a=1)
                                .to_broadcast([EP, GT, CH]), ALU.is_equal).then_inc(hot, 1)

                    one_hots(0, bass.ds(0, GT))

                    with v.Fori(0, NB) as i:
                        done = Chain(v, chain_sem, i * 4)
                        for k in range(2):
                            n = i * 2 + k
                            v.wait_ge(looked, n + 2)
                            one_hots(1 - k, bass.ds(i * KB + (k + 1) * GT, GT))
                            v.wait_ge(b_bcast, n + 1)
                            for t in range(GT):
                                col = bass.ds(i * KB + k * GT + t, 1)
                                mm = v.scalar_tensor_tensor(
                                    out=same[:, k * GT + t, :], in0=ps_b[k][:, t * EP:(t + 1) * EP], scalar=bucket[:, col],
                                    in1=g.before[0:EP, 0:EP], op0=ALU.is_equal, op1=ALU.mult,
                                    accum_out=rank[:, col])
                            mm.then_inc(b_used, 1)
                            v.wait_ge(looked, n + 3)
                            v.wait_ge(hot, n * 2 + 2)
                            done(v.tensor_tensor(pick[k][:, :, :], oh_s[k][:, :, :],
                                                 ps_l[k][:, 0:GT * CH].rearrange("p (t c) -> p t c", c=CH), ALU.mult))
                            v.sem_inc(l_used, 1)
                            done(v.tensor_reduce(ahead[:, bass.ds(i * KB + k * GT, GT)], pick[k][:, :, :],
                                                 AX_X, ALU.add))

            chain2 = s2.sem("chain2")
            with nc.Block() as block:
                @block.vector
                def _(v):
                    done = Chain(v, chain2)
                    slot, col = ahead[:, 0:ET], rank[:, 0:ET]
                    done(v.tensor_tensor(slot, slot, col, ALU.add))
                    done(v.tensor_scalar(col, slot, 1.0 / P, -0.498, ALU.mult, ALU.add))
                    done(v.tensor_scalar(col, col, MAGIC, MAGIC, ALU.add, ALU.subtract))
                    done(v.scalar_tensor_tensor(out=slot_row[:, :], in0=col, scalar=-float(P), in1=slot,
                                                op0=ALU.mult, op1=ALU.add))
                    done(v.scalar_tensor_tensor(out=slot_row[:, :], in0=slot_row[:, :], scalar=float(NT), in1=col,
                                                op0=ALU.mult, op1=ALU.add))
                    done(v.tensor_copy(slot_u[:, :], slot_row[:, :]))

            SB, NS = 25, len(g.scattered)
            stage = s2.sb("stage", [EP, NS, SB, REC], F32)
            stage_i = s2.sb("stage_i", [EP, NS, SB], U32)
            issuing = s2.sem("issuing")
            staged, scattered = s2.sem("staged"), g.scattered
            with nc.Block() as block:
                @block.vector
                def _(v):
                    def fill(k, col):
                        v.tensor_copy(stage[:, k, :, :], rec[:, col, :]).then_inc(staged, 1)
                        v.tensor_copy(stage_i[:, k, :], slot_u[:, col]).then_inc(staged, 1)

                    for k in range(NS):
                        fill(k, bass.ds(k * SB, SB))
                    with v.Fori(1, ET // (SB * NS)) as i:
                        for k in range(NS):
                            v.wait_ge(scattered[k], i * (16 * SB))
                            fill(k, bass.ds(i * SB * NS + k * SB, SB))

                @block.gpsimd
                def _(pool):
                    rows = g.slots.rearrange("p n r -> (p n) r")
                    with pool.Fori(0, ET // (SB * NS)) as i:
                        for k in range(NS):
                            pool.wait_ge(staged, i * (2 * NS) + 2 * k + 2)
                            pool.sem_inc(issuing, 1)
                            for t in range(SB):
                                pool.indirect_dma_start(
                                    out=rows, out_offset=bass.IndirectOffsetOnAxis(stage_i[:, k, t:t + 1], 0),
                                    in_=stage[:, k, t, :], in_offset=None).then_inc(scattered[k], 16)
                    for k in range(NS):
                        pool.wait_ge(scattered[k], 16 * SB * (ET // (SB * NS)))


def load_slots(nc, g, name, slots, attr=None):
    with Stage(nc, name) as st:
        recs = st.sb("recs", [P, NT, REC], F32)
        recs_in = st.sem("recs_in")
        with nc.Block() as block:
            @block.sync
            def _(sp):
                sp.dma_start(recs[:, :, :], g.slots).then_inc(recs_in, 16)

            @block.vector
            def _(v):
                v.wait_ge(recs_in, 16)
                for n in range(2):
                    v.tensor_copy(slots[:, n, :], recs[:, :, n])
                if attr is not None:
                    v.tensor_copy(attr[:, :, :], recs[:, :, 2:REC])


def turn_slots(nc, g, name, slots, row_src, row_dst):
    with Stage(nc, name) as st:
        turned = [st.ps(f"turned{k}", [P, 1024], BF16) for k in range(2)]
        transposed, copied = st.sem("transposed"), st.sem("copied")
        with nc.Block() as block:
            @block.tensor
            def _(pe):
                for n in range(2):
                    for q in range(U // 4):
                        m = n * (U // 4) + q
                        if m >= 2:
                            pe.wait_ge(copied, m - 1)
                        for k in range(4):
                            mm = pe.transpose(turned[m % 2][0:NI, k * P:(k + 1) * P], slots[:, n, q * 4 + k:NT:U],
                                              g.ident_b[:, :])
                        mm.then_inc(transposed, 1)

            @block.scalar
            def _(act):
                for n, rows in enumerate((row_src, row_dst)):
                    for q in range(U // 4):
                        m = n * (U // 4) + q
                        act.wait_ge(transposed, m + 1)
                        act.activation(rows[:, q * 4:(q + 1) * 4, :].rearrange("i u e -> i (u e)"),
                                       turned[m % 2][0:NI, 0:4 * P], ACT.Copy).then_inc(copied, 1)


def chunks_of(nc, eng, where, i, n=U, most=CH - 1):
    _, values = nc.values_load_multi_w_load_instructions(
        where[0:1, bass.ds(i * n, n)], engines=[eng.engine], min_val=0, max_val=most,
        skip_runtime_bounds_check_because="the tile map is clamped to the last bucket on chip")
    return values


def build_counts(nc, g, counts, slots):
    G = 4
    K = U // G
    with Stage(nc, "build") as st:
        where = st.sb("where", [1, NT], I32)
        cols = [st.sb(f"cols{k}", [P, 2, G], F32) for k in range(K)]
        oh_s = [st.sb(f"oh_s{k}", [P, G, P], BF16) for k in range(K)]
        oh_d = [st.sb(f"oh_d{k}", [P, G, P], BF16) for k in range(K)]
        blk = [st.ps(f"blk{k}", [LO, 512], F32) for k in range(K)]
        zeroed, where_in, hot = st.sem("zeroed"), st.sem("where_in"), st.sem("hot")
        multiplied, chain_sem = st.sem("multiplied"), st.sem("chain")
        added, staged = st.sem("added"), st.sem("staged")
        with nc.Block() as block:
            @block.sync
            def _(sp):
                sp.dma_start(where[:, :], g.cell_dram).then_inc(where_in, 16)

            @block.gpsimd
            def _(pool):
                for n in range(5):
                    pool.memset(counts[:, n * 5 * NODES:(n + 1) * 5 * NODES], 0.0).then_inc(zeroed, 1)

            @block.scalar
            def _(act):
                with act.Fori(0, NI) as i:
                    for k in range(K):
                        act.wait_ge(multiplied, i * K + k + 1)
                        act.activation(cols[k][:, :, :], slots[:, :, bass.ds(i * U + k * G, G)], ACT.Copy
                                       ).then_inc(staged, 1)

            @block.tensor
            def _(pe):
                pe.sem_inc(multiplied, K)
                with pe.Fori(0, NI) as i:
                    for k in range(K):
                        n = i * K + k
                        pe.wait_ge(hot, n * 2 * G + 2 * G)
                        pe.wait_ge(added, n + 1)
                        for t in range(G):
                            mm = pe.matmul(blk[k][:, t * LO:(t + 1) * LO], oh_s[k][:, t, 0:LO], oh_d[k][:, t, 0:LO],
                                           start=True, stop=True)
                        mm.then_inc(multiplied, 1)

            @block.vector
            def _(v):
                v.sem_inc(added, K)
                v.wait_ge(zeroed, 5)
                v.wait_ge(where_in, 16)

                def one_hot(k, t):
                    for n, oh in enumerate((oh_s[k], oh_d[k])):
                        v.tensor_scalar(oh[:, t, :], g.iota_b[:, :], cols[k][:, n, t:t + 1], None, ALU.is_equal
                                        ).then_inc(hot, 1)

                def step(i, cell, n, k, ahead):
                    done = Chain(v, chain_sem, n * G)
                    if ahead:
                        v.wait_ge(staged, n + 2)
                    for t in range(G):
                        if ahead:
                            one_hot((k + 1) % K, t)
                        if t == 0:
                            v.wait_ge(multiplied, n + K + 1)
                        cells = counts[:, bass.ds(cell[k * G + t] * LO, LO)]
                        done(v.tensor_tensor(cells, cells, blk[k][:, t * LO:(t + 1) * LO], ALU.add))
                    v.sem_inc(added, 1)

                v.wait_ge(staged, 1)
                for t in range(G):
                    one_hot(0, t)
                with v.Fori(0, NI - 1) as i:
                    cell = chunks_of(nc, v, where, i, U, CH * CH - 1)
                    for k in range(K):
                        step(i, cell, i * K + k, k, True)
                cell = chunks_of(nc, v, where, NI - 1, U, CH * CH - 1)
                for k in range(K):
                    step(NI - 1, cell, (NI - 1) * K + k, k, k < K - 1)


def split3(v, done, whole, parts, rest):
    done(v.tensor_copy(parts[:, :, 0, :], whole))
    done(v.tensor_tensor(rest, whole, parts[:, :, 0, :], ALU.subtract))
    done(v.tensor_copy(parts[:, :, 1, :], rest))
    done(v.tensor_tensor(parts[:, :, 2, :], rest, parts[:, :, 1, :], ALU.subtract))


def spmm(nc, g, name, counts, parts, out, degree=None):
    N = 3 * D + (1 if degree is not None else 0)
    B = 5
    with Stage(nc, name) as st:
        acc = [st.ps(f"acc{k}", [LO, 512], F32) for k in range(B)]
        summed, taken = st.sem("summed"), st.sem("taken")
        with nc.Block() as block:
            @block.tensor
            def _(pe):
                for cd in range(CH):
                    pe.wait_ge(taken, cd + 1)
                    for cs in range(CH):
                        mm = pe.matmul(acc[cd % B][:, 0:N], counts[:, (cs * CH + cd) * LO:(cs * CH + cd + 1) * LO],
                                       parts[:, cs, 0:N], start=(cs == 0), stop=(cs == CH - 1))
                    mm.then_inc(summed, 1)

            @block.vector
            def _(v):
                v.sem_inc(taken, B)
                with v.Fori(0, CH // B) as i:
                    for k in range(B):
                        v.wait_ge(summed, i * B + k + 1)
                        if degree is not None:
                            v.tensor_copy(degree[:, bass.ds(i * B + k, 1)], acc[k][:, 3 * D:3 * D + 1])
                        v.tensor_reduce(out[:, bass.ds(i * B + k, 1), :].rearrange("p a f -> p (a f)"),
                                        acc[k][:, 0:3 * D].rearrange("p (s f) -> p f s", s=3),
                                        AX_X, ALU.add).then_inc(taken, 1)


def linear(nc, g, name, rows, K, weights, M, bias, out):
    NW = len(weights)
    with Stage(nc, name) as st:
        turned = [st.ps(f"turned{k}", [K, 512], F32) for k in range(2)]
        prod = [st.ps(f"prod{k}", [LO, 512], F32) for k in range(2)]
        lhs = [st.sb(f"lhs{k}", [K, NW * P], F32) for k in range(2)]
        transposed, copied = st.sem("transposed"), st.sem("copied")
        multiplied, added = st.sem("multiplied"), st.sem("added")
        with nc.Block() as block:
            @block.tensor
            def _(pe):
                for c in range(CH):
                    if c >= 2:
                        pe.wait_ge(copied, c - 1)
                    for w in range(NW):
                        mm = pe.transpose(turned[c % 2][:, w * P:w * P + LO], rows[:, c, w * K:(w + 1) * K],
                                          g.ident[0:LO, 0:LO])
                    mm.then_inc(transposed, 1)
                    if c >= 2:
                        pe.wait_ge(added, c - 1)
                    pe.wait_ge(copied, c + 1)
                    for w in range(NW):
                        mm = pe.matmul(prod[c % 2][:, 0:M], lhs[c % 2][:, w * P:w * P + LO], weights[w],
                                       start=(w == 0), stop=(w == NW - 1))
                    mm.then_inc(multiplied, 1)

            @block.scalar
            def _(act):
                for c in range(CH):
                    act.wait_ge(transposed, c + 1)
                    if c >= 2:
                        act.wait_ge(multiplied, c - 1)
                    act.activation(lhs[c % 2][:, :].rearrange("k (w p) -> k w p", w=NW)[:, :, 0:LO],
                                   turned[c % 2][:, 0:NW * P].rearrange("k (w p) -> k w p", w=NW)[:, :, 0:LO],
                                   ACT.Copy).then_inc(copied, 1)

            @block.vector
            def _(v):
                for c in range(CH):
                    v.wait_ge(multiplied, c + 1)
                    v.tensor_tensor(out[:, c, :], prod[c % 2][:, 0:M], bias, ALU.add).then_inc(added, 1)


def norm_relu(nc, g, name, x, out):
    with Stage(nc, name) as st:
        mean = st.sb("mean", [LO, CH], F32)
        var = st.sb("var", [LO, CH], F32)
        dev = st.sb("dev", [LO, CH], F32)
        sq = st.sb("sq", [LO, CH, D], F32)
        chain_sem, varied, rooted = st.sem("chain"), st.sem("varied"), st.sem("rooted")

        def over_features(a):
            return a[:, :].rearrange("p (c a) -> p c a", a=1).to_broadcast([LO, CH, D])

        with nc.Block() as block:
            @block.vector
            def _(v):
                done = Chain(v, chain_sem)
                done(v.tensor_reduce(mean[:, :], x[:, :, :], AX_X, ALU.add))
                done(v.tensor_scalar(mean[:, :], mean[:, :], 1.0 / D, None, ALU.mult))
                done(v.tensor_tensor(sq[:, :, :], x[:, :, :], over_features(mean), ALU.subtract))
                done(v.tensor_tensor(out, sq[:, :, :], sq[:, :, :], ALU.mult))
                done(v.tensor_reduce(var[:, :], out, AX_X, ALU.add))
                done(v.tensor_scalar(var[:, :], var[:, :], 1.0 / D, 1e-5, ALU.mult, ALU.add))
                v.sem_inc(varied, 1)
                v.wait_ge(rooted, 1)
                done(v.reciprocal(dev[:, :], var[:, :]))
                done(v.tensor_tensor(sq[:, :, :], sq[:, :, :], over_features(dev), ALU.mult))
                done(v.tensor_scalar(out, sq[:, :, :], 0.0, None, ALU.max))

            @block.scalar
            def _(act):
                act.wait_ge(varied, 1)
                act.activation(var[:, :], var[:, :], ACT.Sqrt).then_inc(rooted, 1)


def layer_sage(nc, g, W, counts):
    with Stage(nc, "sage") as st:
        parts = st.sb("parts", [LO, CH, 3 * D + 4], BF16)
        rows = st.sb("rows", [LO, CH, 2 * D], F32)
        rest = st.sb("rest", [LO, CH, D], F32)
        inv = st.sb("inv", [LO, CH], F32)
        w = st.sb("w", [2 * D, 3, D], F32)
        bias = st.sb("bias", [LO, 3, D], F32)
        w_in = st.sem("w_in")
        norm_relu(nc, g, "sage_norm", g.x, rows[:, :, D:2 * D])
        for layer in range(3):
            chain = [st.sem(f"chain{layer}{k}") for k in range(3)]
            with nc.Block() as block:
                if layer == 0:
                    @block.sync
                    def _(sp):
                        for n in range(3):
                            sp.dma_start(w[0:D, n, :], W[f"L0_gnn_Wl{n}"]).then_inc(w_in, 16)
                            sp.dma_start(w[D:2 * D, n, :], W[f"L0_gnn_Wr{n}"]).then_inc(w_in, 16)
                            sp.dma_start(bias[:, n, :], W[f"L0_gnn_b{n}"].rearrange("(a f) -> a f", a=1)
                                         .to_broadcast([LO, D])).then_inc(w_in, 16)
                        sp.wait_ge(w_in, 16 * 9)

                @block.vector
                def _(v):
                    done = Chain(v, chain[0])
                    if layer == 0:
                        v.memset(parts[:, :, 3 * D:], 1.0)
                    split3(v, done, rows[:, :, D:2 * D], parts[:, :, 0:3 * D].rearrange("p c (s f) -> p c s f", s=3),
                           rest[:, :, :])
            spmm(nc, g, f"sage_sum{layer}", counts, parts, rows[:, :, 0:D], g.degree if layer == 0 else None)
            with nc.Block() as block:
                @block.vector
                def _(v):
                    done = Chain(v, chain[1])
                    if layer == 0:
                        done(v.tensor_scalar(inv[:, :], g.degree[:, :], 1.0, None, ALU.max))
                        done(v.reciprocal(inv[:, :], inv[:, :]))
                    done(v.tensor_tensor(rows[:, :, 0:D], rows[:, :, 0:D],
                                         inv[:, :].rearrange("p (c a) -> p c a", a=1).to_broadcast([LO, CH, D]),
                                         ALU.mult))
            linear(nc, g, f"sage_lin{layer}", rows, 2 * D, [w[:, layer, :]], D, bias[:, layer, :], rest)
            with nc.Block() as block:
                @block.vector
                def _(v):
                    done = Chain(v, chain[2])
                    if layer < 2:
                        done(v.tensor_scalar(rows[:, :, D:2 * D], rest[:, :, :], 0.0, None, ALU.max))
                    else:
                        done(v.tensor_tensor(g.x[:, :, :], g.x[:, :, :], rest[:, :, :], ALU.add))


def counts_rows(nc, g, counts, degree_out):
    with Stage(nc, "degout") as st:
        scrap = st.sb("scrap", [LO, 2, CH * LO], BF16)
        s = st.sem("s")
        with nc.Block() as block:
            @block.scalar
            def _(act):
                for cs in range(CH):
                    if cs >= 2:
                        act.wait_ge(s, cs - 1)
                    act.activation(scrap[:, cs % 2, :], counts[:, cs * CH * LO:(cs + 1) * CH * LO], ACT.Copy,
                                   accum_out=degree_out[:, cs:cs + 1]).then_inc(s, 1)


def layer_appnp(nc, g, W, counts):
    with Stage(nc, "prop") as st:
        parts = st.sb("parts", [LO, CH, 3 * D], BF16)
        h = st.sb("h", [LO, CH, D], F32)
        h0 = st.sb("h0", [LO, CH, D], F32)
        rest = st.sb("rest", [LO, CH, D], F32)
        n_src = st.sb("n_src", [LO, CH], F32)
        n_dst = st.sb("n_dst", [LO, CH], F32)
        pos = st.sb("pos", [LO, CH], F32)
        w = st.sb("w", [D, D], F32)
        bias = st.sb("bias", [LO, D], F32)
        w_in, chain_sem, chain2, rooted, lifted = (st.sem(n) for n in ("w_in", "chain", "chain2", "rooted", "lifted"))
        norm_relu(nc, g, "prop_norm", g.x, h[:, :, :])
        with nc.Block() as block:
            @block.sync
            def _(sp):
                sp.dma_start(w[:, :], W["L2_gnn_W"]).then_inc(w_in, 16)
                sp.dma_start(bias[:, :], W["L2_gnn_b"].rearrange("(a f) -> a f", a=1).to_broadcast([LO, D])
                             ).then_inc(w_in, 16)
                sp.wait_ge(w_in, 32)

            @block.vector
            def _(v):
                done = Chain(v, chain_sem)
                for n, (deg, norm) in enumerate(((g.degree_out, n_src), (g.degree, n_dst))):
                    done(v.tensor_scalar(norm[:, :], deg[:, :], 1.0, None, ALU.max))
                v.sem_inc(lifted, 1)
                v.wait_ge(rooted, 2)
                for n, (deg, norm) in enumerate(((g.degree_out, n_src), (g.degree, n_dst))):
                    done(v.reciprocal(norm[:, :], norm[:, :]))
                    done(v.tensor_scalar(pos[:, :], deg[:, :], 0.0, 1.0 if n == 0 else 0.9, ALU.is_gt, ALU.mult))
                    done(v.tensor_tensor(norm[:, :], norm[:, :], pos[:, :], ALU.mult))

            @block.scalar
            def _(act):
                act.wait_ge(lifted, 1)
                act.activation(n_src[:, :], n_src[:, :], ACT.Sqrt).then_inc(rooted, 1)
                act.activation(n_dst[:, :], n_dst[:, :], ACT.Sqrt).then_inc(rooted, 1)
        linear(nc, g, "prop_lin", h, D, [w[:, :]], D, bias[:, :], h0)

        B = 5
        STEPS = 10
        acc = [st.ps(f"acc{k}", [LO, 512], F32) for k in range(B)]
        split, summed, chain3, chain4 = st.sem("split"), st.sem("summed"), st.sem("chain3"), st.sem("chain4")
        taken, started = st.sem("taken"), st.sem("started")

        def over(a):
            return a[:, :].rearrange("p (c a) -> p c a", a=1).to_broadcast([LO, CH, D])

        with nc.Block() as block:
            @block.tensor
            def _(pe):
                with pe.Fori(0, STEPS) as step:
                    pe.wait_ge(split, step + 1)
                    pe.sem_inc(started, 1)
                    for cd in range(CH):
                        pe.wait_ge(taken, step * CH + cd + 1)
                        for cs in range(CH):
                            mm = pe.matmul(acc[cd % B][:, 0:3 * D],
                                           counts[:, (cs * CH + cd) * LO:(cs * CH + cd + 1) * LO],
                                           parts[:, cs, :], start=(cs == 0), stop=(cs == CH - 1))
                        mm.then_inc(summed, 1)

            @block.vector
            def _(v):
                v.sem_inc(taken, B)
                done = Chain(v, chain2)
                done(v.tensor_copy(h[:, :, :], h0[:, :, :]))
                done(v.tensor_scalar(h0[:, :, :], h0[:, :, :], 0.1, None, ALU.mult))
                with v.Fori(0, STEPS) as step:
                    done = Chain(v, chain3, step * 7)
                    done(v.tensor_tensor(h[:, :, :], h[:, :, :], over(n_src), ALU.mult))
                    split3(v, done, h[:, :, :], parts[:, :, :].rearrange("p c (s f) -> p c s f", s=3), rest[:, :, :])
                    v.sem_inc(split, 1)
                    with v.Fori(0, CH // B) as i:
                        for k in range(B):
                            v.wait_ge(summed, step * CH + i * B + k + 1)
                            v.tensor_reduce(rest[:, bass.ds(i * B + k, 1), :].rearrange("p a f -> p (a f)"),
                                            acc[k][:, 0:3 * D].rearrange("p (s f) -> p f s", s=3),
                                            AX_X, ALU.add).then_inc(taken, 1)
                    v.wait_ge(taken, step * CH + CH + B)
                    done(v.tensor_tensor(rest[:, :, :], rest[:, :, :], over(n_dst), ALU.mult))
                    done(v.tensor_tensor(h[:, :, :], rest[:, :, :], h0[:, :, :], ALU.add))
                done = Chain(v, chain4)
                done(v.tensor_tensor(g.x[:, :, :], g.x[:, :, :], h[:, :, :], ALU.add))


GRP = 4
KG = U // GRP
NG = NT // GRP


def turn_scores(nc, g, name, H, scores, rows):
    with Stage(nc, name) as st:
        part = [st.sb(f"part{k}", [P, NT * H], BF16) for k in range(2)]
        turned = [st.ps(f"turned{k}", [P, 1024], BF16) for k in range(2)]
        chain_sem = st.sem("chain")
        transposed, copied, split = st.sem("transposed"), st.sem("copied"), st.sem("split")
        n_mm = 2 * H * U // 4
        with nc.Block() as block:
            @block.vector
            def _(v):
                done = Chain(v, chain_sem)
                flat = scores[:, :, :].rearrange("p n h -> p (n h)")
                done(v.tensor_copy(part[0][:, :], flat))
                done(v.tensor_tensor(part[1][:, :], flat, part[0][:, :], ALU.subtract))
                v.sem_inc(split, 1)

            @block.tensor
            def _(pe):
                pe.wait_ge(split, 1)
                m = 0
                for h in range(H):
                    for q in range(2):
                        src = part[q][:, :].rearrange("p (n h) -> p n h", h=H)
                        for u in range(0, U, 4):
                            if m >= 2:
                                pe.wait_ge(copied, m - 1)
                            for k in range(4):
                                mm = pe.transpose(turned[m % 2][0:NI, k * P:(k + 1) * P], src[:, u + k:NT:U, h],
                                                  g.ident_b[:, :])
                            mm.then_inc(transposed, 1)
                            m += 1

            @block.scalar
            def _(act):
                m = 0
                for h in range(H):
                    for q in range(2):
                        for u in range(0, U, 4):
                            act.wait_ge(transposed, m + 1)
                            act.activation(rows[:, u:u + 4, h, q, :],
                                           turned[m % 2][0:NI, 0:4 * P].rearrange("i (k e) -> i k e", k=4),
                                           ACT.Copy).then_inc(copied, 1)
                            m += 1


def score_pass(nc, g, name, H, src_parts, dst_parts, W, finish, slots=None, attr=None, attr_sum=None):
    with Stage(nc, name) as st:
        WW = W if H == 1 else 3 * W
        where = st.sb("where", [1, 2 * NT], I32)
        dsts = st.sb("dsts", [1, NT], I32)
        hot_s = [st.sb(f"hot_s{k}", [LO, GRP * P], BF16) for k in range(2)]
        hot_d = [st.sb(f"hot_d{k}", [LO, GRP * P], BF16) for k in range(2)]
        ps_s = [st.ps(f"ps_s{k}", [P, 512], F32) for k in range(2)]
        ps_d = [st.ps(f"ps_d{k}", [P, 512], F32) for k in range(2)]
        ps_x = [st.ps(f"ps_x{k}", [P, 512], F32) for k in range(2)]
        if attr is not None:
            oh = [st.sb(f"oh{k}", [P, GRP, P], F32) for k in range(2)]
            cols = [st.sb(f"cols{k}", [P, GRP], F32) for k in range(2)]
            ps_a = [st.ps(f"ps_a{k}", [LO, 512], F32) for k in range(2)]
        where_in, spread, compared = st.sem("where_in"), st.sem("spread"), st.sem("compared")
        chain_attr = st.sem("chain_attr")
        gathered, used = st.sem("gathered"), st.sem("used")
        hot, attr_mm, staged = st.sem("hot"), st.sem("attr_mm"), st.sem("staged")
        with nc.Block() as block:
            @block.sync
            def _(sp):
                sp.dma_start(where[:, :], g.pairs_dram).then_inc(where_in, 16)
                sp.dma_start(dsts[:, :], g.dst_dram).then_inc(where_in, 16)

            @block.tensor
            def _(pe):
                pe.sem_inc(gathered, 2)
                if attr is not None:
                    pe.sem_inc(attr_mm, 2)
                pe.wait_ge(where_in, 32)

                def spread_rows(b, col, k):
                    for ps, rows in ((ps_s[b], g.row_src), (ps_d[b], g.row_dst)):
                        pe.matmul(ps[:, :], g.ident_b[0:NI, col].to_broadcast([NI, P]),
                                  rows[:, k * GRP:(k + 1) * GRP, :].rearrange("i u e -> i (u e)"),
                                  start=True, stop=True).then_inc(spread, 1)

                spread_rows(0, bass.ds(0, 1), 0)
                with pe.Fori(0, NI) as i:
                    chunk = chunks_of(nc, pe, where, i, 2 * U)
                    for k in range(KG):
                        n, b = i * KG + k, k % 2
                        pe.wait_ge(compared, n * 2 + 4)
                        spread_rows(1 - b, bass.ds(i + (k + 1) // KG, 1), (k + 1) % KG)
                        pe.wait_ge(compared, n * 2 + 6)
                        pe.wait_ge(used, n + 1)
                        for t in range(GRP):
                            cs, cd = chunk[k * 2 * GRP + 2 * t], chunk[k * 2 * GRP + 2 * t + 1]
                            parts = [(hot_s[b], src_parts, cs), (hot_d[b], dst_parts, cd)]
                            if H == 1:
                                todo = [(h, tab[:, bass.ds(c, 1), q, :]) for h, tab, c in parts for q in range(3)]
                            else:
                                todo = [(h, tab[:, bass.ds(c, 1), :, :]) for h, tab, c in parts]
                            for m, (h, rhs) in enumerate(todo):
                                if H == 1:
                                    rhs = rhs.rearrange("p a f -> p (a f)")
                                else:
                                    rhs = rhs.rearrange("p a s f -> p (a s f)")
                                mm = pe.matmul(ps_x[b][:, t * WW:(t + 1) * WW], h[:, t * P:(t + 1) * P], rhs,
                                               start=(m == 0), stop=(m == len(todo) - 1))
                        mm.then_inc(gathered, 1)
                        if attr is not None:
                            pe.wait_ge(hot, n + 1)
                            for t in range(GRP):
                                mm = pe.matmul(ps_a[b][:, t * W:(t + 1) * W], oh[b][:, t, 0:LO],
                                               attr[:, bass.ds(i * U + k * GRP + t, 1), :].rearrange("p a h -> p (a h)"),
                                               start=True, stop=True)
                            mm.then_inc(attr_mm, 1)

            if attr is not None:
                @block.gpsimd
                def _(pool):
                    with pool.Fori(0, NI) as i:
                        for k in range(KG):
                            pool.wait_ge(attr_mm, i * KG + k + 1)
                            pool.tensor_copy(cols[k % 2][:, :], slots[:, 1, bass.ds(i * U + k * GRP, GRP)]
                                             ).then_inc(staged, 1)

            more = finish(st, block, ps_x, gathered, used)

            @block.vector
            def _(v):
                v.sem_inc(compared, 4)
                v.sem_inc(used, 2)
                v.wait_ge(where_in, 32)

                def compare(b):
                    for h, ps in ((hot_s[b], ps_s[b]), (hot_d[b], ps_d[b])):
                        v.tensor_scalar(h[:, :], ps[0:LO, :], g.iota_part[0:LO, 0:1], None, ALU.is_equal
                                        ).then_inc(compared, 1)

                v.wait_ge(spread, 2)
                compare(0)
                with v.Fori(0, NI) as i:
                    if attr is not None:
                        chunk = chunks_of(nc, v, dsts, i)
                    for k in range(KG):
                        n, b = i * KG + k, k % 2
                        v.wait_ge(spread, n * 2 + 4)
                        v.wait_ge(gathered, n + 2)
                        compare(1 - b)
                        if attr is not None:
                            v.wait_ge(staged, n + 1)
                            for t in range(GRP):
                                mm = v.tensor_scalar(oh[b][:, t, :], g.iota_free[:, :],
                                                     cols[b][:, t:t + 1], None,
                                                     ALU.is_equal)
                            mm.then_inc(hot, 1)
                        more(v, i, n, k, b)
                        if attr is not None:
                            v.wait_ge(attr_mm, n + 3)
                            done = Chain(v, chain_attr, n * GRP)
                            for t in range(GRP):
                                cell = attr_sum[:, bass.ds(chunk[k * GRP + t], 1), :].rearrange("p a h -> p (a h)")
                                done(v.tensor_tensor(cell, cell, ps_a[b][:, t * W:(t + 1) * W], ALU.add))


def max_pass(nc, g, name, H, rows, top):
    TB = GRP // H
    NQ = GRP // TB
    with Stage(nc, name) as st:
        where = st.sb("where", [1, NT], I32)
        hot_d = [st.sb(f"hot_d{k}", [LO, GRP * P], BF16) for k in range(2)]
        tile_top = [st.sb(f"tile_top{k}", [LO, GRP, H], F32) for k in range(2)]
        ps_d = [st.ps(f"ps_d{k}", [P, 512], F32) for k in range(2)]
        ps_m = [st.ps(f"ps_m{k}", [LO, 512], F32) for k in range(4)]
        where_in, spread, compared = st.sem("where_in"), st.sem("spread"), st.sem("compared")
        masked, reduced, chain_sem = st.sem("masked"), st.sem("reduced"), st.sem("chain")
        with nc.Block() as block:
            @block.sync
            def _(sp):
                sp.dma_start(where[:, :], g.dst_dram).then_inc(where_in, 16)

            @block.tensor
            def _(pe):
                pe.sem_inc(masked, NQ)

                def spread_rows(b, col, k):
                    pe.matmul(ps_d[b][:, :], g.ident_b[0:NI, col].to_broadcast([NI, P]),
                              g.row_dst[:, k * GRP:(k + 1) * GRP, :].rearrange("i u e -> i (u e)"),
                              start=True, stop=True).then_inc(spread, 1)

                spread_rows(0, bass.ds(0, 1), 0)
                with pe.Fori(0, NI) as i:
                    for k in range(KG):
                        n, b = i * KG + k, k % 2
                        pe.wait_ge(compared, n + 2)
                        spread_rows(1 - b, bass.ds(i + (k + 1) // KG, 1), (k + 1) % KG)
                        pe.wait_ge(compared, n + 3)
                        for q in range(NQ):
                            bank = ps_m[(k * NQ + q) % 4]
                            pe.wait_ge(reduced, n * NQ + q + 1)
                            if H == 1:
                                hot = hot_d[b][:, :]
                            else:
                                hot = hot_d[b][:, q * P:(q + 1) * P].rearrange("p (a e) -> p a e", a=1
                                                                                ).to_broadcast([LO, H, P])
                            pe.matmul(bank[:, :] if H == 1 else bank[:, :].rearrange("p (h e) -> p h e", h=H),
                                      g.off_diag[0:LO, 0:LO], hot, start=True, stop=False)
                            one = g.ident_b[0:NI, bass.ds(i, 1)].to_broadcast([NI, LO])
                            for part in range(2):
                                r = rows[:, (k * NQ + q) * TB:(k * NQ + q + 1) * TB, :, part, :]
                                mm = pe.matmul(bank[:, :].rearrange("p (u e) -> p u e", u=GRP), one,
                                               r.rearrange("i u h e -> i (u h) e"), start=False, stop=(part == 1))
                            mm.then_inc(masked, 1)

            @block.vector
            def _(v):
                v.sem_inc(compared, 2)
                v.sem_inc(reduced, 4)
                v.wait_ge(where_in, 16)

                def compare(b):
                    v.tensor_scalar(hot_d[b][:, :], ps_d[b][0:LO, :], g.iota_part[0:LO, 0:1], None, ALU.is_equal
                                    ).then_inc(compared, 1)

                v.wait_ge(spread, 1)
                compare(0)
                with v.Fori(0, NI) as i:
                    chunk = chunks_of(nc, v, where, i)
                    for k in range(KG):
                        n, b = i * KG + k, k % 2
                        v.wait_ge(spread, n + 2)
                        v.wait_ge(masked, n * NQ + NQ)
                        compare(1 - b)
                        for q in range(NQ):
                            v.wait_ge(masked, n * NQ + NQ + q + 1)
                            v.tensor_reduce(tile_top[b][:, q * TB:(q + 1) * TB, :].rearrange("p t h -> p (t h)"),
                                            ps_m[(k * NQ + q) % 4][:, :].rearrange("p (u e) -> p u e", u=GRP),
                                            AX_X, ALU.max).then_inc(reduced, 1)
                            v.wait_ge(reduced, n * NQ + q + 5)
                            done = Chain(v, chain_sem, n * GRP + q * TB)
                            for t in range(q * TB, (q + 1) * TB):
                                cell = top[:, bass.ds(chunk[k * GRP + t], 1), :].rearrange("p a h -> p (a h)")
                                done(v.tensor_tensor(cell, cell, tile_top[b][:, t, :], ALU.max))


def sum_pass(nc, g, name, H, scores, top_parts, src_parts, slots, total):
    M = H * D + H
    with Stage(nc, name) as st:
        where = st.sb("where", [1, 2 * NT], I32)
        dsts = st.sb("dsts", [1, NT], I32)
        hot_s = [st.sb(f"hot_s{k}", [LO, GRP * P], BF16) for k in range(2)]
        hot_d = [st.sb(f"hot_d{k}", [LO, GRP * P], BF16) for k in range(2)]
        oh = [st.sb(f"oh{k}", [P, GRP, P], F32) for k in range(2)]
        cols = [st.sb(f"cols{k}", [P, GRP], F32) for k in range(2)]
        staged = st.sem("staged")
        below = [st.sb(f"below{k}", [P, GRP, H], F32) for k in range(2)]
        y = [st.sb(f"y{k}", [P, GRP, M], F32) for k in range(2)]
        ps_s = st.ps("ps_s", [P, 512], F32)
        ps_d = st.ps("ps_d", [P, 512], F32)
        ps_x = [st.ps(f"ps_x{k}", [P, 512], F32) for k in range(2)]
        ps_t = [st.ps(f"ps_t{k}", [P, 512], F32) for k in range(2)]
        ps_y = [st.ps(f"ps_y{k}", [LO, 512], F32) for k in range(2)]
        where_in, spread, compared, gathered = (st.sem(n) for n in ("where_in", "spread", "compared", "gathered"))
        hot, lowered, weighed, scaled = (st.sem(n) for n in ("hot", "lowered", "weighed", "scaled"))
        summed, chain_b, chain_y = st.sem("summed"), st.sem("chain_b"), st.sem("chain_y")
        with nc.Block() as block:
            @block.sync
            def _(sp):
                sp.dma_start(where[:, :], g.pairs_dram).then_inc(where_in, 16)
                sp.dma_start(dsts[:, :], g.dst_dram).then_inc(where_in, 16)

            @block.tensor
            def _(pe):
                pe.sem_inc(gathered, 2)
                pe.sem_inc(summed, 2 * GRP)
                pe.wait_ge(where_in, 32)

                def spread_rows(col, k):
                    for ps, rows in ((ps_s, g.row_src), (ps_d, g.row_dst)):
                        pe.matmul(ps[:, :], g.ident_b[0:NI, col].to_broadcast([NI, P]),
                                  rows[:, k * GRP:(k + 1) * GRP, :].rearrange("i u e -> i (u e)"),
                                  start=True, stop=True).then_inc(spread, 1)

                def gather(chunk, k, b):
                    for t in range(GRP):
                        cs, cd = chunk[k * 2 * GRP + 2 * t], chunk[k * 2 * GRP + 2 * t + 1]
                        pe.matmul(ps_t[b][:, t * 3 * H:(t + 1) * 3 * H], hot_d[b][:, t * P:(t + 1) * P],
                                  top_parts[:, bass.ds(cd, 1), :].rearrange("p a f -> p (a f)"), start=True, stop=True)
                        for q in range(3):
                            mm = pe.matmul(ps_x[b][:, t * D:(t + 1) * D], hot_s[b][:, t * P:(t + 1) * P],
                                           src_parts[:, bass.ds(cs, 1), q, :].rearrange("p a f -> p (a f)"),
                                           start=(q == 0), stop=(q == 2))
                    mm.then_inc(gathered, 1)

                spread_rows(bass.ds(0, 1), 0)
                with pe.Fori(0, NI) as i:
                    chunk = chunks_of(nc, pe, where, i, 2 * U)
                    for k in range(KG):
                        n, b = i * KG + k, k % 2
                        pe.wait_ge(compared, n * 2 + 6)
                        spread_rows(bass.ds(i + (k + 1) // KG, 1), (k + 1) % KG)
                        pe.wait_ge(scaled, n + 1)
                        gather(chunk, k, b)
                        pe.wait_ge(hot, n + 1)
                        pe.wait_ge(scaled, n + 3)
                        for t in range(GRP):
                            pe.wait_ge(chain_y, n * GRP + t + 1)
                            pe.matmul(ps_y[t % 2][:, 0:M], oh[b][:, t, 0:LO], y[b][:, t, :], start=True, stop=True
                                      ).then_inc(summed, 1)

            @block.gpsimd
            def _(pool):
                with pool.Fori(0, NI) as i:
                    for k in range(KG):
                        pool.wait_ge(summed, (i * KG + k) * GRP + GRP)
                        pool.tensor_copy(cols[k % 2][:, :], slots[:, 1, bass.ds(i * U + k * GRP, GRP)]
                                         ).then_inc(staged, 1)

            @block.scalar
            def _(act):
                with act.Fori(0, NI) as i:
                    for k in range(KG):
                        n, b = i * KG + k, k % 2
                        act.wait_ge(lowered, n + 1)
                        act.wait_ge(summed, n * GRP + GRP)
                        act.activation(y[b][:, :, H * D:M], below[b][:, :, :], ACT.Exp).then_inc(weighed, 1)

            @block.vector
            def _(v):
                v.sem_inc(compared, 4)
                v.sem_inc(scaled, 2)
                v.sem_inc(chain_y, 2)
                v.wait_ge(where_in, 32)

                def compare(b):
                    for h, ps in ((hot_s[b], ps_s), (hot_d[b], ps_d)):
                        v.tensor_scalar(h[:, :], ps[0:LO, :], g.iota_part[0:LO, 0:1], None, ALU.is_equal
                                        ).then_inc(compared, 1)

                v.wait_ge(spread, 2)
                compare(0)
                with v.Fori(0, NI) as i:
                    chunk = chunks_of(nc, v, dsts, i)
                    for k in range(KG):
                        n, b = i * KG + k, k % 2
                        v.wait_ge(staged, n + 1)
                        for t in range(GRP):
                            mm = v.tensor_scalar(oh[b][:, t, :], g.iota_free[:, :],
                                                 cols[b][:, t:t + 1], None, ALU.is_equal)
                        mm.then_inc(hot, 1)
                        v.wait_ge(gathered, n + 3)
                        done = Chain(v, chain_b, n * 2)
                        done(v.tensor_reduce(below[b][:, :, :].rearrange("p t h -> p (t h)"),
                                             ps_t[b][:, 0:GRP * 3 * H].rearrange("p (t s h) -> p t h s", t=GRP, s=3),
                                             AX_X, ALU.add))
                        done(v.tensor_tensor(below[b][:, :, :], scores[:, bass.ds(i * U + k * GRP, GRP), :],
                                             below[b][:, :, :], ALU.subtract))
                        v.sem_inc(lowered, 1)
                        v.wait_ge(spread, n * 2 + 4)
                        compare(1 - b)
                        v.wait_ge(weighed, n + 1)
                        for t in range(GRP):
                            mm = v.tensor_tensor(
                                y[b][:, t, 0:H * D].rearrange("p (h f) -> p h f", h=H),
                                ps_x[b][:, t * D:(t + 1) * D].rearrange("p (a f) -> p a f", a=1).to_broadcast([P, H, D]),
                                y[b][:, t, H * D:M].rearrange("p (h a) -> p h a", a=1).to_broadcast([P, H, D]),
                                ALU.mult)
                        mm.then_inc(scaled, 1)
                        for t in range(GRP):
                            v.wait_ge(summed, n * GRP + 2 * GRP + t + 1)
                            cell = total[:, bass.ds(chunk[k * GRP + t], 1), :].rearrange("p a f -> p (a f)")
                            v.tensor_tensor(cell, cell, ps_y[t % 2][:, 0:M], ALU.add).then_inc(chain_y, 1)
                            v.wait_ge(chain_y, n * GRP + t + 3)


def layer_gat2(nc, g, W):
    with Stage(nc, "gat2") as st:
        slots = st.sb("slots", [P, 2, NT], BF16)
        g.row_src = st.sb("row_src", [NI, U, P], BF16)
        g.row_dst = st.sb("row_dst", [NI, U, P], BF16)
        load_slots(nc, g, "load1", slots)
        turn_slots(nc, g, "turn1", slots, g.row_src, g.row_dst)
        h = st.sb("h", [LO, CH, D], F32)
        lr = st.sb("lr", [LO, CH, 2 * D], F32)
        l_parts = st.sb("l_parts", [LO, CH, 3, D], BF16)
        r_parts = st.sb("r_parts", [LO, CH, 3, D], BF16)
        rest = st.sb("rest", [LO, CH, D], F32)
        w = st.sb("w", [D, 2 * D], F32)
        bias = st.sb("bias", [LO, 2 * D], F32)
        att = st.sb("att", [P, D], F32)
        tail = st.sb("tail", [LO, 3, D], F32)
        own = st.sb("own", [LO, CH, 1], F32)
        top = st.sb("top", [LO, CH, 1], F32)
        top_parts = st.sb("top_parts", [LO, CH, 3], BF16)
        scores = st.sb("scores", [P, NT, 1], F32)
        rows = st.sb("rows", [NI, U, 1, 2, P], BF16)
        total = st.sb("total", [LO, CH, D + 1], F32)
        w_in = st.sem("w_in")
        chain = [st.sem(f"chain{k}") for k in range(6)]

        def row(name, p, n):
            return W[name].rearrange("(a f) -> a f", a=1).to_broadcast([p, n])

        with nc.Block() as block:
            @block.sync
            def _(sp):
                sp.dma_start(w[:, 0:D], W["L1_gnn_W_l"]).then_inc(w_in, 16)
                sp.dma_start(w[:, D:2 * D], W["L1_gnn_W_r"]).then_inc(w_in, 16)
                sp.dma_start(bias[:, 0:D], row("L1_gnn_b_l", LO, D)).then_inc(w_in, 16)
                sp.dma_start(bias[:, D:2 * D], row("L1_gnn_b_r", LO, D)).then_inc(w_in, 16)
                sp.dma_start(att[:, :], row("L1_gnn_att", P, D)).then_inc(w_in, 16)
                for n, name in enumerate(("L1_gnn_bias", "L1_gnn_gamma", "L1_gnn_beta")):
                    sp.dma_start(tail[:, n, :], row(name, LO, D)).then_inc(w_in, 16)
                sp.wait_ge(w_in, 16 * 8)
        norm_relu(nc, g, "gat2_norm", g.x, h[:, :, :])
        linear(nc, g, "gat2_lin", h, D, [w[:, :]], 2 * D, bias[:, :], lr)
        with nc.Block() as block:
            @block.vector
            def _(v):
                done = Chain(v, chain[0])
                v.memset(total[:, :, :], 0.0)
                split3(v, done, lr[:, :, 0:D], l_parts, rest[:, :, :])
                split3(v, done, lr[:, :, D:2 * D], r_parts, rest[:, :, :])
                done(v.tensor_tensor(h[:, :, :], lr[:, :, 0:D], lr[:, :, D:2 * D], ALU.add))
                done(v.scalar_tensor_tensor(out=rest[:, :, :], in0=h[:, :, :], scalar=0.2, in1=h[:, :, :],
                                            op0=ALU.mult, op1=ALU.max))
                done(v.tensor_tensor(rest[:, :, :], rest[:, :, :],
                                     att[0:LO, :].rearrange("p (a f) -> p a f", a=1).to_broadcast([LO, CH, D]),
                                     ALU.mult))
                done(v.tensor_reduce(own[:, :, :].rearrange("p c a -> p (c a)"), rest[:, :, :], AX_X, ALU.add))
                done(v.tensor_copy(top[:, :, :], own[:, :, :]))

        def finish(st2, block, ps_x, gathered, used):
            bent = [st2.sb(f"bent{k}", [P, GRP * D], F32) for k in range(2)]
            copied, chain_s = st2.sem("copied"), st2.sem("chain_s")

            @block.scalar
            def _(act):
                act.sem_inc(chain_s, 6)
                with act.Fori(0, NI) as i:
                    for k in range(KG):
                        n, b = i * KG + k, k % 2
                        act.wait_ge(gathered, n + 3)
                        act.wait_ge(chain_s, n * 3 + 3)
                        act.activation(bent[b][:, :], ps_x[b][:, 0:GRP * D], ACT.Copy).then_inc(copied, 1)

            def more(v, i, n, k, b):
                v.wait_ge(copied, n + 1)
                done = Chain(v, chain_s, n * 3 + 6)
                done(v.scalar_tensor_tensor(out=bent[b][:, :], in0=ps_x[b][:, 0:GRP * D], scalar=0.2,
                                            in1=bent[b][:, :], op0=ALU.mult, op1=ALU.max))
                v.sem_inc(used, 1)
                x3 = bent[b][:, :].rearrange("p (t f) -> p t f", t=GRP)
                done(v.tensor_tensor(x3, x3, att[:, :].rearrange("p (a f) -> p a f", a=1).to_broadcast([P, GRP, D]),
                                     ALU.mult))
                done(v.tensor_reduce(scores[:, bass.ds(i * U + k * GRP, GRP), :].rearrange("p t a -> p (t a)"),
                                     x3, AX_X, ALU.add))
            return more

        score_pass(nc, g, "gat2_score", 1, l_parts, r_parts, D, finish)
        empty_scores(nc, "gat2_empty", 1, slots, scores)
        turn_scores(nc, g, "gat2_turn", 1, scores, rows)
        max_pass(nc, g, "gat2_max", 1, rows, top)
        with nc.Block() as block:
            @block.vector
            def _(v):
                done = Chain(v, chain[1])
                r = rest[:, :, 0]
                tp = top[:, :, 0]
                done(v.tensor_copy(top_parts[:, :, 0], tp))
                done(v.tensor_tensor(r, tp, top_parts[:, :, 0], ALU.subtract))
                done(v.tensor_copy(top_parts[:, :, 1], r))
                done(v.tensor_tensor(top_parts[:, :, 2], r, top_parts[:, :, 1], ALU.subtract))
        sum_pass(nc, g, "gat2_sum", 1, scores, top_parts, l_parts, slots, total)
        with Stage(nc, "gat2_end") as s2:
            ps = s2.ps("ps", [LO, 512], F32)
            stat = s2.sb("stat", [LO, 2, D], F32)
            part = s2.sb("part", [LO, D], F32)
            ones = s2.sb("ones", [LO, LO], F32)
            weighed, lowered, summed = s2.sem("weighed"), s2.sem("lowered"), s2.sem("summed")
            parted, rooted = s2.sem("parted"), s2.sem("rooted")

            def over(a, shape):
                return a.rearrange("p (a f) -> p a f", a=1).to_broadcast(shape)

            S3 = [LO, CH, D]
            with nc.Block() as block:
                @block.tensor
                def _(pe):
                    for n in range(2):
                        pe.wait_ge(parted, n + 1)
                        pe.matmul(ps[:, n * D:(n + 1) * D], ones[:, :], part[:, :], start=True, stop=True
                                  ).then_inc(summed, 1)

                @block.scalar
                def _(act):
                    act.wait_ge(lowered, 1)
                    act.activation(own[:, :, 0], own[:, :, 0], ACT.Exp).then_inc(weighed, 1)
                    act.wait_ge(lowered, 2)
                    act.activation(stat[:, 1, :], stat[:, 1, :], ACT.Sqrt).then_inc(rooted, 1)

                @block.vector
                def _(v):
                    done = Chain(v, chain[2])
                    done(v.memset(ones[:, :], 1.0))
                    done(v.tensor_tensor(own[:, :, :], own[:, :, :], top[:, :, :], ALU.subtract))
                    v.sem_inc(lowered, 1)
                    v.wait_ge(weighed, 1)
                    done(v.tensor_tensor(rest[:, :, :], lr[:, :, 0:D], own[:, :, :].to_broadcast(S3), ALU.mult))
                    done(v.tensor_tensor(rest[:, :, :], rest[:, :, :], total[:, :, 0:D], ALU.add))
                    done(v.tensor_tensor(own[:, :, :], own[:, :, :], total[:, :, D:D + 1], ALU.add))
                    done(v.reciprocal(own[:, :, :], own[:, :, :]))
                    done(v.tensor_tensor(rest[:, :, :], rest[:, :, :], own[:, :, :].to_broadcast(S3), ALU.mult))
                    done(v.tensor_tensor(rest[:, :, :], rest[:, :, :], over(tail[:, 0, :], S3), ALU.add))
                    done(v.tensor_reduce(part[:, :], rest[:, :, :].rearrange("p c f -> p f c"), AX_X, ALU.add))
                    v.sem_inc(parted, 1)
                    v.wait_ge(summed, 1)
                    done(v.tensor_scalar(stat[:, 0, :], ps[:, 0:D], 1.0 / NODES, None, ALU.mult))
                    done(v.tensor_tensor(rest[:, :, :], rest[:, :, :], over(stat[:, 0, :], S3), ALU.subtract))
                    done(v.tensor_tensor(h[:, :, :], rest[:, :, :], rest[:, :, :], ALU.mult))
                    done(v.tensor_reduce(part[:, :], h[:, :, :].rearrange("p c f -> p f c"), AX_X, ALU.add))
                    v.sem_inc(parted, 1)
                    v.wait_ge(summed, 2)
                    done(v.tensor_scalar(stat[:, 1, :], ps[:, D:2 * D], 1.0 / NODES, 1e-5, ALU.mult, ALU.add))
                    v.sem_inc(lowered, 1)
                    v.wait_ge(rooted, 1)
                    done(v.reciprocal(stat[:, 1, :], stat[:, 1, :]))
                    done(v.tensor_tensor(stat[:, 1, :], stat[:, 1, :], tail[:, 1, :], ALU.mult))
                    done(v.tensor_tensor(rest[:, :, :], rest[:, :, :], over(stat[:, 1, :], S3), ALU.mult))
                    done(v.tensor_tensor(rest[:, :, :], rest[:, :, :], over(tail[:, 2, :], S3), ALU.add))
                    done(v.tensor_tensor(g.x[:, :, :], g.x[:, :, :], rest[:, :, :], ALU.add))


def layer_gat(nc, g, W):
    H = HEADS
    with Stage(nc, "gat") as st:
        slots = st.sb("slots", [P, 2, NT], BF16)
        g.row_src = st.sb("row_src", [NI, U, P], BF16)
        g.row_dst = st.sb("row_dst", [NI, U, P], BF16)
        h = st.sb("h", [LO, CH, D], F32)
        h_parts = st.sb("h_parts", [LO, CH, 3, D], BF16)
        own = st.sb("own", [LO, CH, H], F32)
        top = st.sb("top", [LO, CH, H], F32)
        top_parts = st.sb("top_parts", [LO, CH, 3 * H], BF16)
        scores = st.sb("scores", [P, NT, H], F32)
        a_sd = st.sb("a_sd", [LO, CH, 2 * H], F32)
        rest4 = st.sb("rest4", [LO, CH, H], F32)
        a_parts = [st.sb(f"a_parts{k}", [LO, CH, 3, H], BF16) for k in range(2)]
        combined = st.sb("combined", [P, 2, D], F32)
        shift = st.sb("shift", [LO, D], F32)
        tail = st.sb("tail", [LO, 3, D], F32)
        chain = [st.sem(f"chain{k}") for k in range(6)]
        norm_relu(nc, g, "gat_norm", g.x, h[:, :, :])

        def row(ap, p, n):
            return ap.to_broadcast([p, n])

        with Stage(nc, "gat_w") as s2:
            w = s2.sb("w", [D, H * D], F32)
            att = s2.sb("att", [D, 2, H * D], F32)
            prod = s2.sb("prod", [D, 2, H * D], F32)
            vec = s2.sb("vec", [D, 2 * H], F32)
            wp = s2.sb("wp", [P, 2, D], F32)
            bias_col = s2.sb("bias_col", [P, 2], F32)
            diag = s2.sb("diag", [P, 2, P], F32)
            none = s2.sb("none", [LO, 2 * H], F32)
            ps_w = s2.ps("ps_w", [P, 512], F32)
            ps_c = s2.ps("ps_c", [P, 512], F32)
            ps_b = s2.ps("ps_b", [LO, 512], F32)
            w_in, turned, laid, mixed = s2.sem("w_in"), s2.sem("turned"), s2.sem("laid"), s2.sem("mixed")
            with nc.Block() as block:
                @block.sync
                def _(sp):
                    sp.dma_start(w[:, :], W["L3_gnn_W"]).then_inc(w_in, 16)
                    for n, name in enumerate(("L3_gnn_att_src", "L3_gnn_att_dst")):
                        sp.dma_start(att[:, n, :], row(W[name].rearrange("(a h) c -> a (h c)", a=1), D, H * D)
                                     ).then_inc(w_in, 16)
                    sp.dma_start(wp[:, :, :], W["L3_gnn_Wp"].rearrange("(b k) f -> k b f", b=2)).then_inc(w_in, 16)
                    sp.dma_start(bias_col[:, :], W["L3_gnn_bias"].rearrange("(b k) -> k b", b=2),
                                 allow_slow_non_contiguous=True).then_inc(w_in, 16)
                    for n, name in enumerate(("L3_gnn_bp", "L3_gnn_gamma", "L3_gnn_beta")):
                        sp.dma_start(tail[:, n, :], row(W[name].rearrange("(a f) -> a f", a=1), LO, D)).then_inc(w_in, 16)
                    sp.wait_ge(w_in, 16 * 8)

                @block.tensor
                def _(pe):
                    pe.wait_ge(w_in, 16 * 8)
                    for b in range(2):
                        pe.transpose(ps_w[:, b * D:(b + 1) * D], w[:, b * P:(b + 1) * P], g.ident[0:D, 0:D]
                                     ).then_inc(turned, 1)
                    pe.wait_ge(laid, 1)
                    for b in range(2):
                        pe.matmul(ps_c[:, b * D:(b + 1) * D], diag[:, b, :], wp[:, b, :], start=True, stop=True
                                  ).then_inc(mixed, 1)
                    for b in range(2):
                        pe.matmul(ps_b[:, 0:D], bias_col[:, b:b + 1].to_broadcast([P, LO]), wp[:, b, :],
                                  start=(b == 0), stop=(b == 1)).then_inc(mixed, 1)

                @block.vector
                def _(v):
                    done = Chain(v, chain[0])
                    v.memset(none[:, :], 0.0)
                    done(v.memset(diag[:, :, :], 0.0))
                    v.wait_ge(turned, 2)
                    for b in range(2):
                        for k in range(2):
                            half = slice(k * D, (k + 1) * D)
                            done(v.tensor_copy(diag[half, b, half], ps_w[half, b * D:(b + 1) * D]))
                    v.sem_inc(laid, 1)
                    v.wait_ge(w_in, 16 * 8)
                    done(v.tensor_tensor(prod[:, :, :], att[:, :, :],
                                         w[:, :].rearrange("p (a c) -> p a c", a=1).to_broadcast([D, 2, H * D]),
                                         ALU.mult))
                    done(v.tensor_reduce(vec[:, :], prod[:, :, :].rearrange("p n (h c) -> p (n h) c", h=H),
                                         AX_X, ALU.add))
                    v.wait_ge(mixed, 4)
                    done(v.tensor_copy(combined[:, :, :].rearrange("p b f -> p (b f)"), ps_c[:, 0:2 * D]))
                    done(v.tensor_tensor(shift[:, :], ps_b[:, 0:D], tail[:, 0, :], ALU.add))
            linear(nc, g, "gat_vec", h, D, [vec[:, :]], 2 * H, none[:, :], a_sd)

        with Stage(nc, "gat_attr") as s2:
            attr = s2.sb("attr", [P, NT, H], F32)
            attr_sum = s2.sb("attr_sum", [LO, CH, H], F32)
            inv = s2.sb("inv", [LO, CH], F32)
            rest = s2.sb("rest", [LO, CH, D], F32)
            load_slots(nc, g, "load3", slots, attr)
            turn_slots(nc, g, "turn3", slots, g.row_src, g.row_dst)
            with nc.Block() as block:
                @block.vector
                def _(v):
                    done = Chain(v, chain[1])
                    v.memset(attr_sum[:, :, :], 0.0)
                    split3(v, done, h[:, :, :], h_parts, rest[:, :, :])
                    for k in range(2):
                        split3(v, done, a_sd[:, :, k * H:(k + 1) * H], a_parts[k], rest4[:, :, :])

            def finish(st2, block, ps_x, gathered, used):
                raw = [st2.sb(f"raw{k}", [P, GRP, H], F32) for k in range(2)]
                chain_s = st2.sem("chain_s")

                def more(v, i, n, k, b):
                    v.wait_ge(gathered, n + 3)
                    done = Chain(v, chain_s, n * 3)
                    done(v.tensor_reduce(raw[b][:, :, :].rearrange("p t h -> p (t h)"),
                                         ps_x[b][:, 0:GRP * 3 * H].rearrange("p (t s h) -> p t h s", t=GRP, s=3),
                                         AX_X, ALU.add))
                    v.sem_inc(used, 1)
                    col = bass.ds(i * U + k * GRP, GRP)
                    done(v.tensor_tensor(raw[b][:, :, :], raw[b][:, :, :], attr[:, col, :], ALU.add))
                    done(v.scalar_tensor_tensor(out=scores[:, col, :], in0=raw[b][:, :, :], scalar=0.2,
                                                in1=raw[b][:, :, :], op0=ALU.mult, op1=ALU.max))
                return more

            score_pass(nc, g, "gat_score", H, a_parts[0], a_parts[1], H, finish, slots, attr, attr_sum)
            empty_scores(nc, "gat_empty", H, slots, scores)
            with nc.Block() as block:
                @block.vector
                def _(v):
                    done = Chain(v, chain[2])
                    done(v.tensor_scalar(inv[:, :], g.degree[:, :], 1.0, None, ALU.max))
                    done(v.reciprocal(inv[:, :], inv[:, :]))
                    done(v.tensor_tensor(attr_sum[:, :, :], attr_sum[:, :, :],
                                         inv[:, :].rearrange("p (c a) -> p c a", a=1).to_broadcast([LO, CH, H]),
                                         ALU.mult))
                    done(v.tensor_tensor(own[:, :, :], a_sd[:, :, 0:H], a_sd[:, :, H:2 * H], ALU.add))
                    done(v.tensor_tensor(own[:, :, :], own[:, :, :], attr_sum[:, :, :], ALU.add))
                    done(v.scalar_tensor_tensor(out=own[:, :, :], in0=own[:, :, :], scalar=0.2, in1=own[:, :, :],
                                                op0=ALU.mult, op1=ALU.max))
                    done(v.tensor_copy(top[:, :, :], own[:, :, :]))
        with Stage(nc, "gat_rows") as s2:
            rows = s2.sb("rows", [NI, U, H, 2, P], BF16)
            turn_scores(nc, g, "gat_turn", H, scores, rows)
            max_pass(nc, g, "gat_max", H, rows, top)
        total = st.sb("total", [LO, CH, H * D + H], F32)
        with nc.Block() as block:
            @block.vector
            def _(v):
                done = Chain(v, chain[3])
                v.memset(total[:, :, :], 0.0)
                split3(v, done, top[:, :, :], top_parts[:, :, :].rearrange("p c (s h) -> p c s h", s=3), rest4[:, :, :])
        sum_pass(nc, g, "gat_sum", H, scores, top_parts, h_parts, slots, total)
        with Stage(nc, "gat_end") as s2:
            agg = s2.sb("agg", [LO, CH, H * D], F32)
            proj = s2.sb("proj", [LO, CH, D], F32)
            neg = s2.sb("neg", [LO, CH, D], F32)
            mean = s2.sb("mean", [LO, CH], F32)
            lowered, weighed = s2.sem("lowered"), s2.sem("weighed")

            def over(a):
                return a[:, :].rearrange("p (c a) -> p c a", a=1).to_broadcast([LO, CH, D])

            def all_over(a):
                return a.rearrange("p (a f) -> p a f", a=1).to_broadcast([LO, CH, D])

            with nc.Block() as block:
                @block.scalar
                def _(act):
                    act.wait_ge(lowered, 1)
                    act.activation(own[:, :, :], own[:, :, :], ACT.Exp).then_inc(weighed, 1)

                @block.vector
                def _(v):
                    done = Chain(v, chain[4])
                    done(v.tensor_tensor(own[:, :, :], own[:, :, :], top[:, :, :], ALU.subtract))
                    v.sem_inc(lowered, 1)
                    v.wait_ge(weighed, 1)
                    done(v.tensor_tensor(rest4[:, :, :], own[:, :, :], total[:, :, H * D:], ALU.add))
                    done(v.reciprocal(rest4[:, :, :], rest4[:, :, :]))
                    for k in range(H):
                        part = agg[:, :, k * D:(k + 1) * D]
                        done(v.tensor_tensor(part, h[:, :, :], own[:, :, k:k + 1].to_broadcast([LO, CH, D]), ALU.mult))
                        done(v.tensor_tensor(part, part, total[:, :, k * D:(k + 1) * D], ALU.add))
                        done(v.tensor_tensor(part, part, rest4[:, :, k:k + 1].to_broadcast([LO, CH, D]), ALU.mult))
            linear(nc, g, "gat_proj", agg, P, [combined[:, 0, :], combined[:, 1, :]], D, shift[:, :], proj)
            minned, exped, varied, rooted = s2.sem("minned"), s2.sem("exped"), s2.sem("varied"), s2.sem("rooted")
            with nc.Block() as block:
                @block.scalar
                def _(act):
                    act.wait_ge(minned, 1)
                    act.activation(neg[:, :, :], neg[:, :, :], ACT.Exp).then_inc(exped, 1)
                    act.wait_ge(varied, 1)
                    act.activation(mean[:, :], mean[:, :], ACT.Sqrt).then_inc(rooted, 1)

                @block.vector
                def _(v):
                    done = Chain(v, chain[5])
                    done(v.tensor_scalar(neg[:, :, :], proj[:, :, :], 0.0, None, ALU.min))
                    v.sem_inc(minned, 1)
                    done(v.scalar_tensor_tensor(out=h[:, :, :], in0=proj[:, :, :], scalar=0.0, in1=h[:, :, :],
                                                op0=ALU.max, op1=ALU.add))
                    v.wait_ge(exped, 1)
                    done(v.scalar_tensor_tensor(out=h[:, :, :], in0=neg[:, :, :], scalar=-1.0, in1=h[:, :, :],
                                                op0=ALU.add, op1=ALU.add))
                    done(v.tensor_reduce(mean[:, :], h[:, :, :], AX_X, ALU.add))
                    done(v.tensor_scalar(mean[:, :], mean[:, :], 1.0 / D, None, ALU.mult))
                    done(v.tensor_tensor(h[:, :, :], h[:, :, :], over(mean), ALU.subtract))
                    done(v.tensor_tensor(proj[:, :, :], h[:, :, :], h[:, :, :], ALU.mult))
                    done(v.tensor_reduce(mean[:, :], proj[:, :, :], AX_X, ALU.add))
                    done(v.tensor_scalar(mean[:, :], mean[:, :], 1.0 / D, 1e-5, ALU.mult, ALU.add))
                    v.sem_inc(varied, 1)
                    v.wait_ge(rooted, 1)
                    done(v.reciprocal(mean[:, :], mean[:, :]))
                    done(v.tensor_tensor(h[:, :, :], h[:, :, :], over(mean), ALU.mult))
                    done(v.tensor_tensor(h[:, :, :], h[:, :, :], all_over(tail[:, 1, :]), ALU.mult))
                    done(v.tensor_tensor(h[:, :, :], h[:, :, :], all_over(tail[:, 2, :]), ALU.add))
                    done(v.tensor_tensor(g.x[:, :, :], g.x[:, :, :], h[:, :, :], ALU.add))


def empty_scores(nc, name, H, slots, scores):
    with Stage(nc, name) as st:
        low = st.sb("low", [P, NT], F32)
        chain = st.sem("chain")
        with nc.Block() as block:
            @block.vector
            def _(v):
                done = Chain(v, chain)
                done(v.tensor_scalar(low[:, :], slots[:, 0, :], 0.0, -BIG, ALU.is_lt, ALU.mult))
                for h in range(H):
                    done(v.tensor_tensor(scores[:, :, h], scores[:, :, h], low[:, :], ALU.add))


class Globals:
    pass


def program(nc, x, src, dst, ea16, w_edge, att_edge, out, **W):
    g = Globals()
    with Stage(nc, "g") as st:
        g.iota_free = st.sb("iota_free", [P, P], F32)
        g.iota_b = st.sb("iota_b", [P, P], BF16)
        g.ident = st.sb("ident", [P, P], F32)
        g.ident_h = st.sb("ident_h", [P, P], FP16)
        g.ident_b = st.sb("ident_b", [P, P], BF16)
        g.before = st.sb("before", [P, P], F32)
        g.after = st.sb("after", [P, P], F32)
        g.off_diag = st.sb("off_diag", [P, P], BF16)
        g.cleared = st.sem("cleared")
        g.scattered = [st.sem(f"scattered{k}") for k in range(3)]
        g.iota_part = st.sb("iota_part", [P, 1], F32)
        g.slots = nc.dram_tensor("slots", (P, NT, REC), F32, kind="Internal").ap()
        g.ends_dram = nc.dram_tensor("ends", (CH, CH), F32, kind="Internal").ap()
        g.pairs_dram = nc.dram_tensor("tile_pairs", (1, NT * 2), I32, kind="Internal").ap()
        g.dst_dram = nc.dram_tensor("tile_dst", (1, NT), I32, kind="Internal").ap()
        g.cell_dram = nc.dram_tensor("tile_cell", (1, NT), I32, kind="Internal").ap()
        g.counts_dram = nc.dram_tensor("countsd", (LO, CH * NODES), BF16, kind="Internal").ap()
        build_constants(nc, g)
        sort_edges(nc, g, src, dst, ea16, w_edge, att_edge)
        g.x = st.sb("x", [LO, CH, D], F32)
        g.degree = st.sb("degree", [LO, CH], F32)
        g.degree_out = st.sb("degree_out", [LO, CH], F32)
        x_in, saved, loaded = st.sem("x_in"), st.sem("saved"), st.sem("loaded")
        with Stage(nc, "first") as s2:
            counts = s2.sb("counts", [LO, CH * NODES], BF16)
            with Stage(nc, "slots0") as s3:
                slots = s3.sb("slots", [P, 2, NT], BF16)
                load_slots(nc, g, "load0", slots)
                build_counts(nc, g, counts, slots)
            with nc.Block() as block:
                @block.sync
                def _(sp):
                    sp.dma_start(g.x[:, :, :], x.rearrange("(p c) f -> p c f", p=LO)).then_inc(x_in, 16)
                    sp.wait_ge(x_in, 16)
                    sp.dma_start(g.counts_dram, counts[:, :]).then_inc(saved, 16)
            counts_rows(nc, g, counts, g.degree_out)
            layer_sage(nc, g, W, counts)
            with nc.Block() as block:
                @block.sync
                def _(sp):
                    sp.wait_ge(saved, 16)
        layer_gat2(nc, g, W)
        with Stage(nc, "second") as s2:
            counts = s2.sb("counts", [LO, CH * NODES], BF16)
            with nc.Block() as block:
                @block.sync
                def _(sp):
                    sp.dma_start(counts[:, :], g.counts_dram).then_inc(loaded, 16)
                    sp.wait_ge(loaded, 16)
            layer_appnp(nc, g, W, counts)
        layer_gat(nc, g, W)
        with nc.Block() as block:
            @block.sync
            def _(sp):
                sp.dma_start(out.rearrange("(p c) f -> p c f", p=LO), g.x[:, :, :]).then_inc(saved, 16)
                sp.wait_ge(saved, 32)


_INS = {"x": "x", "src": "src", "dst": "dst", "ea16": "edge_attr_16", "w_edge": "L3_gnn_W_edge",
        "att_edge": "L3_gnn_att_edge"}
_SAME = ["L0_gnn_Wl0", "L0_gnn_Wr0", "L0_gnn_b0", "L0_gnn_Wl1", "L0_gnn_Wr1", "L0_gnn_b1", "L0_gnn_Wl2",
         "L0_gnn_Wr2", "L0_gnn_b2", "L1_gnn_W_l", "L1_gnn_b_l", "L1_gnn_W_r", "L1_gnn_b_r", "L1_gnn_att",
         "L1_gnn_bias", "L1_gnn_gamma", "L1_gnn_beta", "L2_gnn_W", "L2_gnn_b", "L3_gnn_W", "L3_gnn_att_src",
         "L3_gnn_att_dst", "L3_gnn_bias", "L3_gnn_Wp", "L3_gnn_bp", "L3_gnn_gamma", "L3_gnn_beta"]


def kernel(**inputs):
    import numpy as _np
    import concourse.bacc as _bacc
    from concourse import mybir as _mybir
    from concourse.bass_utils import run_bass_kernel_spmd as _run

    nc = _bacc.Bacc("TRN2", target_bir_lowering=False, num_devices=1)
    arrays, args = {}, {}
    for arg, name in {**_INS, **{n: n for n in _SAME}}.items():
        a = _np.ascontiguousarray(inputs[name])
        arrays[f"in_{name}_dram"] = a
        args[arg] = nc.dram_tensor(f"in_{name}_dram", a.shape, _mybir.dt.from_np(a.dtype), kind="ExternalInput").ap()
    args["out"] = nc.dram_tensor("out_dram", (NODES, D), F32, kind="ExternalOutput").ap()
    program(nc, **args)
    r = _run(nc, [arrays], core_ids=[0])
    return r.results[0]["out_dram"]
```

```python
from contextlib import ExitStack

import concourse.bass as bass
from concourse import mybir

ALU = mybir.AluOpType
ACT = mybir.ActivationFunctionType
F32 = mybir.dt.float32
BF16 = mybir.dt.bfloat16
FP16 = mybir.dt.float16
I32 = mybir.dt.int32
U32 = mybir.dt.uint32
AX_X = mybir.AxisListType.X

NODES = 3125
CH = 25
LO = NODES // CH
D = 64
HEADS = 4
EDGES = 103125
EP = 125
ET = EDGES // EP
EPAD = 832
P = 128
U = 16
NI = 90
NT = U * NI
assert NT >= (EDGES + CH * CH * (P - 1)) // P and LO * CH == NODES and EP * ET == EDGES
REC = 6
MAGIC = 12582912.0
BIG = 1.0e30


class Chain:

    def __init__(self, eng, sem, start=0):
        self.eng, self.sem, self.n = eng, sem, start

    def __call__(self, ins):
        self.n = self.n + 1
        ins.then_inc(self.sem, 1)
        self.eng.wait_ge(self.sem, self.n)


class Stage:

    def __init__(self, nc, name):
        self.nc, self.name, self.ctx, self.sems = nc, name, ExitStack(), []

    def __enter__(self):
        return self

    def __exit__(self, *a):
        if self.sems:
            for sem in self.sems:
                self.nc.gpsimd.sem_clear(sem)
            self.nc.all_engine_barrier()
        self.ctx.close()

    def sb(self, name, shape, dt):
        return self.ctx.enter_context(self.nc.sbuf_tensor(f"{self.name}_{name}", shape, dt))

    def ps(self, name, shape, dt):
        return self.ctx.enter_context(self.nc.psum_tensor(f"{self.name}_{name}", shape, dt))

    def sem(self, name):
        self.sems.append(self.ctx.enter_context(self.nc.semaphore(f"{self.name}_{name}")))
        return self.sems[-1]


def build_constants(nc, g):
    with Stage(nc, "const") as st:
        ready = st.sem("ready")
        chain_sem = st.sem("chain")
        with nc.Block() as block:
            @block.gpsimd
            def _(pool):
                pool.iota(g.iota_free[:, :], [[1, P]], base=0, channel_multiplier=0,
                          allow_small_or_imprecise_dtypes=True).then_inc(ready, 1)
                pool.iota(g.iota_part[:, :], [[1, 1]], base=0, channel_multiplier=1,
                          allow_small_or_imprecise_dtypes=True).then_inc(ready, 1)

            @block.vector
            def _(v):
                done = Chain(v, chain_sem)
                v.wait_ge(ready, 2)
                v.tensor_scalar(g.ident[:, :], g.iota_free[:, :], g.iota_part[:, 0:1], None, ALU.is_equal)
                v.tensor_scalar(g.ident_h[:, :], g.iota_free[:, :], g.iota_part[:, 0:1], None, ALU.is_equal)
                v.tensor_scalar(g.ident_b[:, :], g.iota_free[:, :], g.iota_part[:, 0:1], None, ALU.is_equal)
                v.tensor_copy(g.iota_b[:, :], g.iota_free[:, :])
                v.tensor_scalar(g.before[:, :], g.iota_free[:, :], g.iota_part[:, 0:1], None, ALU.is_lt)
                v.tensor_scalar(g.after[:, :], g.iota_free[:, :], g.iota_part[:, 0:1], None, ALU.is_gt)
                done(v.tensor_scalar(g.off_diag[:, :], g.iota_free[:, :], g.iota_part[:, 0:1], -BIG,
                                     ALU.not_equal, ALU.mult))


def sort_edges(nc, g, src, dst, ea16, w_edge, att_edge):
    with Stage(nc, "sort") as st:
        chunk_s = st.sb("chunk_s", [EP, EPAD + 8], F32)
        chunk_d = st.sb("chunk_d", [EP, EPAD + 8], F32)
        bucket = st.sb("bucket", [EP, EPAD], F32)
        rank = st.sb("rank", [EP, EPAD], F32)
        rec = st.sb("rec", [EP, EPAD, REC], F32)

        with Stage(nc, "decode") as s2:
            src_i = s2.sb("src_i", [EP, ET], I32)
            dst_i = s2.sb("dst_i", [EP, ET], I32)
            attrs = s2.sb("attrs", [EP, ET, 16], F32)
            prod = s2.sb("prod", [EP, ET, 16], F32)
            we = s2.sb("we", [EP, 16, HEADS * D], F32)
            wp = s2.sb("wp", [EP, 16, HEADS * D], F32)
            att = s2.sb("att", [EP, HEADS * D], F32)
            wh = s2.sb("wh", [EP, 16, HEADS], F32)
            empty = s2.sb("empty", [P, U * REC], F32)
            nodes_in = s2.sem("nodes_in")
            attrs_in = s2.sem("attrs_in")
            weights_in = s2.sem("weights_in")
            empty_set = s2.sem("empty_set")
            chain_sem = s2.sem("chain")
            with nc.Block() as block:
                @block.sync
                def _(sp):
                    sp.dma_start(src_i[:, :], src.rearrange("(p t) -> p t", p=EP)).then_inc(nodes_in, 16)
                    sp.dma_start(dst_i[:, :], dst.rearrange("(p t) -> p t", p=EP)).then_inc(nodes_in, 16)
                    sp.dma_start(we[:, :, :].rearrange("p k c -> p (k c)"),
                                 w_edge.rearrange("(a k) c -> a (k c)", a=1).to_broadcast([EP, 16 * HEADS * D])
                                 ).then_inc(weights_in, 16)
                    sp.dma_start(att[:, :], att_edge.rearrange("(a h) c -> a (h c)", a=1)
                                 .to_broadcast([EP, HEADS * D])).then_inc(weights_in, 16)
                    sp.dma_start(attrs[:, :, :], ea16.rearrange("(p t) k -> p t k", p=EP)).then_inc(attrs_in, 16)

                @block.gpsimd
                def _(pool):
                    pool.memset(empty[:, :], 0.0).then_inc(empty_set, 1)
                    pool.wait_ge(empty_set, 1)
                    pool.memset(empty[:, :].rearrange("p (n r) -> p n r", r=REC)[:, :, 0:2], -1.0
                                ).then_inc(empty_set, 1)
                    pool.wait_ge(empty_set, 2)
                    slots = g.slots.rearrange("p (n u) r -> p n (u r)", u=U)
                    pool.dma_start(slots, empty[:, :].rearrange("p (a f) -> p a f", a=1)
                                   .to_broadcast([P, NI, U * REC])).then_inc(g.cleared, 16)
                    pool.wait_ge(g.cleared, 16)

                @block.vector
                def _(v):
                    done = Chain(v, chain_sem)
                    v.memset(chunk_s[:, ET:EPAD + 8], -1.0)
                    v.memset(chunk_d[:, ET:EPAD + 8], -1.0)
                    v.memset(bucket[:, ET:EPAD], -1.0)
                    v.wait_ge(nodes_in, 32)
                    for ids, chunk, field in ((src_i, chunk_s, 0), (dst_i, chunk_d, 1)):
                        done(v.tensor_copy(rank[:, 0:ET], ids[:, :]))
                        lo = rec[:, 0:ET, field]
                        done(v.tensor_scalar(lo, rank[:, 0:ET], 1.0 / CH, -0.48, ALU.mult, ALU.add))
                        done(v.tensor_scalar(lo, lo, MAGIC, MAGIC, ALU.add, ALU.subtract))
                        done(v.scalar_tensor_tensor(out=chunk[:, 0:ET], in0=lo, scalar=-float(CH),
                                                    in1=rank[:, 0:ET], op0=ALU.mult, op1=ALU.add))
                    done(v.scalar_tensor_tensor(out=bucket[:, 0:ET], in0=chunk_d[:, 0:ET], scalar=float(CH),
                                                in1=chunk_s[:, 0:ET], op0=ALU.mult, op1=ALU.add))
                    v.wait_ge(weights_in, 32)
                    done(v.tensor_tensor(wp[:, :, :], we[:, :, :],
                                         att[:, :].rearrange("p (a c) -> p a c", a=1)
                                         .to_broadcast([EP, 16, HEADS * D]), ALU.mult))
                    done(v.tensor_reduce(wh[:, :, :], wp[:, :, :].rearrange("p k (h c) -> p k h c", h=HEADS),
                                         AX_X, ALU.add))
                    v.wait_ge(attrs_in, 16)
                    for h in range(HEADS):
                        done(v.tensor_tensor(prod[:, :, :], attrs[:, :, :],
                                             wh[:, :, h].rearrange("p (a k) -> p a k", a=1)
                                             .to_broadcast([EP, ET, 16]), ALU.mult))
                        done(v.tensor_reduce(rec[:, 0:ET, 2 + h], prod[:, :, :], AX_X, ALU.add))

        pre = st.sb("pre", [CH, CH, EPAD + 1], F32)

        with Stage(nc, "count") as s2:
            GT = 16
            oh_s = [s2.sb(f"oh_s{k}", [EP, GT, CH], BF16) for k in range(2)]
            oh_d = [s2.sb(f"oh_d{k}", [EP, GT, CH], BF16) for k in range(2)]
            cnt = [s2.ps(f"cnt{k}", [CH, 512], F32) for k in range(2)]
            hot = s2.sem("hot")
            counted, copied = s2.sem("counted"), s2.sem("copied")
            n_iter = EPAD // (2 * GT)
            with nc.Block() as block:
                @block.vector
                def _(v):
                    v.memset(pre[:, :, 0:1], 0.0)
                    with v.Fori(0, n_iter) as i:
                        for k in range(2):
                            v.wait_ge(counted, i * 2 + k + 1)
                            for oh, chunk in ((oh_s[k], chunk_s), (oh_d[k], chunk_d)):
                                v.tensor_tensor(
                                    oh[:, :, :],
                                    chunk[:, bass.ds(i * 2 * GT + k * GT, GT)].rearrange("p (t a) -> p t a", a=1)
                                    .to_broadcast([EP, GT, CH]),
                                    g.iota_free[0:EP, 0:CH].rearrange("p (a c) -> p a c", a=1)
                                    .to_broadcast([EP, GT, CH]), ALU.is_equal).then_inc(hot, 1)

                @block.tensor
                def _(pe):
                    pe.sem_inc(counted, 2)
                    with pe.Fori(0, n_iter) as i:
                        for k in range(2):
                            pe.wait_ge(hot, i * 4 + 2 * k + 2)
                            pe.wait_ge(copied, i * 2 + k + 1)
                            for t in range(GT):
                                mm = pe.matmul(cnt[k][:, t * CH:(t + 1) * CH], oh_d[k][:, t, :], oh_s[k][:, t, :],
                                               start=True, stop=True)
                            mm.then_inc(counted, 1)

                @block.scalar
                def _(act):
                    act.sem_inc(copied, 2)
                    with act.Fori(0, n_iter) as i:
                        for k in range(2):
                            act.wait_ge(counted, i * 2 + k + 3)
                            act.activation(pre[:, :, bass.ds(i * 2 * GT + k * GT + 1, GT)],
                                           cnt[k][:, 0:GT * CH].rearrange("p (t c) -> p c t", c=CH),
                                           ACT.Copy).then_inc(copied, 1)

        with Stage(nc, "prefix") as s2:
            tiles = s2.sb("tiles", [CH, CH], F32)
            upto = s2.sb("upto", [CH, CH], F32)
            base = s2.sb("base", [CH, CH], F32)
            end = s2.sb("end", [CH, CH], F32)
            rows = s2.ps("rows", [CH, 1], F32)
            ends = s2.sb("ends", [NI, CH * CH], F32)
            tile_no = s2.sb("tile_no", [NI, U], F32)
            hits = s2.sb("hits", [NI, CH * CH], F32)
            tb = s2.sb("tb", [NI, U], F32)
            td = s2.sb("td", [NI, U], F32)
            ts = s2.sb("ts", [NI, U], F32)
            pairs = s2.sb("pairs", [NI, U, 2], I32)
            dsts = s2.sb("dsts", [NI, U], I32)
            cells = s2.sb("cells", [NI, U], I32)
            chain_sem = s2.sem("chain")
            summed, end_out, end_in = s2.sem("summed"), s2.sem("end_out"), s2.sem("end_in")
            row_base, numbered = s2.sem("row_base"), s2.sem("numbered")
            found, map_out = s2.sem("found"), s2.sem("map_out")
            with nc.Block() as block:
                @block.gpsimd
                def _(pool):
                    pool.iota(tile_no[:, :], [[1, U]], base=0, channel_multiplier=U,
                              allow_small_or_imprecise_dtypes=True).then_inc(numbered, 1)

                @block.tensor
                def _(pe):
                    pe.wait_ge(summed, 1)
                    pe.matmul(rows[:, :], g.after[0:CH, 0:CH], upto[:, CH - 1:CH], start=True, stop=True
                              ).then_inc(row_base, 1)

                @block.sync
                def _(sp):
                    sp.wait_ge(end_out, 1)
                    sp.dma_start(g.ends_dram, end[:, :]).then_inc(end_in, 16)
                    sp.wait_ge(end_in, 16)
                    sp.dma_start(ends[:, :], g.ends_dram.rearrange("(a d) s -> a (d s)", a=1)
                                 .to_broadcast([NI, CH * CH])).then_inc(end_in, 16)
                    sp.wait_ge(found, 1)
                    sp.dma_start(g.pairs_dram.rearrange("a (i u f) -> (a i) u f", u=U, f=2), pairs[:, :, :]).then_inc(map_out, 16)
                    sp.dma_start(g.dst_dram.rearrange("a (i u) -> (a i) u", u=U), dsts[:, :]).then_inc(map_out, 16)
                    sp.dma_start(g.cell_dram.rearrange("a (i u) -> (a i) u", u=U), cells[:, :]).then_inc(map_out, 16)
                    sp.wait_ge(map_out, 48)

                @block.vector
                def _(v):
                    done = Chain(v, chain_sem)
                    for cs in range(CH):
                        last = v.tensor_tensor_scan(pre[:, cs, :], pre[:, cs, :], pre[:, cs, :], 0.0,
                                                    ALU.add, ALU.bypass)
                        last.then_inc(chain_sem, 1)
                        done.n += 1
                    v.wait_ge(chain_sem, done.n)
                    done(v.tensor_scalar(tiles[:, :], pre[:, :, EPAD], P / 2 - 0.5, 1.0 / P, ALU.add, ALU.mult))
                    done(v.tensor_scalar(tiles[:, :], tiles[:, :], MAGIC, MAGIC, ALU.add, ALU.subtract))
                    done(v.tensor_tensor_scan(upto[:, :], tiles[:, :], tiles[:, :], 0.0, ALU.add, ALU.bypass))
                    v.sem_inc(summed, 1)
                    done(v.tensor_tensor(base[:, :], upto[:, :], tiles[:, :], ALU.subtract))
                    v.wait_ge(row_base, 1)
                    done(v.tensor_scalar(end[:, :], upto[:, :], rows[:, 0:1], None, ALU.add))
                    v.sem_inc(end_out, 1)
                    done(v.tensor_scalar(base[:, :], base[:, :], rows[:, 0:1], None, ALU.add))
                    done(v.scalar_tensor_tensor(
                        out=pre[:, :, :], in0=base[:, :].rearrange("p (c a) -> p c a", a=1)
                        .to_broadcast([CH, CH, EPAD + 1]), scalar=float(P), in1=pre[:, :, :],
                        op0=ALU.mult, op1=ALU.add))
                    v.wait_ge(end_in, 32)
                    v.wait_ge(numbered, 1)
                    for u in range(U):
                        done(v.tensor_scalar(hits[:, :], ends[:, :], tile_no[:, u:u + 1], None,
                                             ALU.is_le, ALU.add, accum_out=tb[:, u:u + 1]))
                    done(v.tensor_scalar(tb[:, :], tb[:, :], float(CH * CH - 1), None, ALU.min))
                    done(v.tensor_scalar(td[:, :], tb[:, :], 1.0 / CH, -0.48, ALU.mult, ALU.add))
                    done(v.tensor_scalar(td[:, :], td[:, :], MAGIC, MAGIC, ALU.add, ALU.subtract))
                    done(v.scalar_tensor_tensor(out=ts[:, :], in0=td[:, :], scalar=-float(CH), in1=tb[:, :],
                                                op0=ALU.mult, op1=ALU.add))
                    done(v.tensor_copy(pairs[:, :, 0], ts[:, :]))
                    done(v.tensor_copy(pairs[:, :, 1], td[:, :]))
                    done(v.tensor_copy(dsts[:, :], td[:, :]))
                    done(v.scalar_tensor_tensor(out=tb[:, :], in0=ts[:, :], scalar=float(CH), in1=td[:, :],
                                                op0=ALU.mult, op1=ALU.add))
                    done(v.tensor_copy(cells[:, :], tb[:, :]))
                    v.sem_inc(found, 1)

        KB, GT = 8, 4
        NB = EPAD // KB
        with Stage(nc, "place") as s2:
            b_t = s2.sb("b_t", [NB, KB, EP], FP16)
            oh_s = [s2.sb(f"oh_s{k}", [EP, GT, CH], F32) for k in range(2)]
            oh_d = [s2.sb(f"oh_d{k}", [EP, GT, CH], BF16) for k in range(2)]
            oh_t = [s2.sb(f"oh_t{k}", [CH, GT * EP], F32) for k in range(2)]
            same = s2.sb("same", [EP, 2 * GT, EP], F32)
            pick = [s2.sb(f"pick{k}", [EP, GT, CH], F32) for k in range(2)]
            ahead = s2.sb("ahead", [EP, EPAD], F32)
            slot_row = s2.sb("slot_row", [EP, ET], F32)
            slot_u = s2.sb("slot_u", [EP, ET], U32)
            ps_t = [s2.ps(f"ps_t{k}", [CH, 1024], BF16) for k in range(2)]
            ps_b = [s2.ps(f"ps_b{k}", [EP, 512], F32) for k in range(2)]
            ps_l = [s2.ps(f"ps_l{k}", [EP, 512], F32) for k in range(2)]
            turned, b_ready = s2.sem("turned"), s2.sem("b_ready")
            with nc.Block() as block:
                @block.tensor
                def _(pe):
                    for k in range(KB):
                        if k >= 2:
                            pe.wait_ge(b_ready, k - 1)
                        pe.transpose(ps_b[k % 2][0:NB, 0:EP], bucket[:, k::KB], g.ident[0:EP, 0:EP]
                                     ).then_inc(turned, 1)

                @block.scalar
                def _(act):
                    for k in range(KB):
                        act.wait_ge(turned, k + 1)
                        act.activation(b_t[:, k, :], ps_b[k % 2][0:NB, 0:EP], ACT.Copy).then_inc(b_ready, 1)

            hot = s2.sem("hot")
            t_ready, t_copied = s2.sem("t_ready"), s2.sem("t_copied")
            b_bcast, b_used = s2.sem("b_bcast"), s2.sem("b_used")
            looked, l_used = s2.sem("looked"), s2.sem("l_used")
            chain_sem = s2.sem("chain")
            with nc.Block() as block:
                @block.tensor
                def _(pe):
                    pe.sem_inc(looked, 2)
                    with pe.Fori(0, NB) as i:
                        for k in range(2):
                            n = i * 2 + k
                            pe.wait_ge(hot, n * 2 + 2)
                            pe.wait_ge(t_copied, n + 1)
                            for t in range(GT):
                                mm = pe.transpose(ps_t[k][:, t * P:t * P + EP], oh_d[k][:, t, :],
                                                  g.ident_b[0:EP, 0:EP])
                            mm.then_inc(t_ready, 1)
                            pe.wait_ge(b_used, n + 1)
                            pe.matmul(ps_b[k][:, 0:GT * EP], g.ident_h[0:NB, bass.ds(i, 1)].to_broadcast([NB, EP]),
                                      b_t[:, k * GT:(k + 1) * GT, :].rearrange("p t e -> p (t e)"),
                                      start=True, stop=True).then_inc(b_bcast, 1)
                            pe.wait_ge(t_copied, n + 3)
                            pe.wait_ge(l_used, n + 1)
                            for t in range(GT):
                                mm = pe.matmul(ps_l[k][:, t * CH:(t + 1) * CH], oh_t[k][:, t * EP:(t + 1) * EP],
                                               pre[:, :, bass.ds(i * KB + k * GT + t, 1)].rearrange("p c a -> p (c a)"),
                                               start=True, stop=True)
                            mm.then_inc(looked, 1)

                @block.scalar
                def _(act):
                    act.sem_inc(t_copied, 2)
                    with act.Fori(0, NB) as i:
                        for k in range(2):
                            act.wait_ge(t_ready, i * 2 + k + 1)
                            act.wait_ge(looked, i * 2 + k + 1)
                            act.activation(oh_t[k][:, :].rearrange("c (t e) -> c t e", t=GT),
                                           ps_t[k][:, 0:GT * P].rearrange("c (t e) -> c t e", t=GT)[:, :, 0:EP],
                                           ACT.Copy).then_inc(t_copied, 1)

                @block.vector
                def _(v):
                    v.sem_inc(b_used, 2)
                    v.sem_inc(l_used, 2)

                    def one_hots(k, col):
                        for oh, chunk in ((oh_s[k], chunk_s), (oh_d[k], chunk_d)):
                            v.tensor_tensor(
                                oh[:, :, :], chunk[:, col].rearrange("p (t a) -> p t a", a=1)
                                .to_broadcast([EP, GT, CH]),
                                g.iota_free[0:EP, 0:CH].rearrange("p (a c) -> p a c", a=1)
                                .to_broadcast([EP, GT, CH]), ALU.is_equal).then_inc(hot, 1)

                    one_hots(0, bass.ds(0, GT))

                    with v.Fori(0, NB) as i:
                        done = Chain(v, chain_sem, i * 4)
                        for k in range(2):
                            n = i * 2 + k
                            v.wait_ge(looked, n + 2)
                            one_hots(1 - k, bass.ds(i * KB + (k + 1) * GT, GT))
                            v.wait_ge(b_bcast, n + 1)
                            for t in range(GT):
                                col = bass.ds(i * KB + k * GT + t, 1)
                                mm = v.scalar_tensor_tensor(
                                    out=same[:, k * GT + t, :], in0=ps_b[k][:, t * EP:(t + 1) * EP], scalar=bucket[:, col],
                                    in1=g.before[0:EP, 0:EP], op0=ALU.is_equal, op1=ALU.mult,
                                    accum_out=rank[:, col])
                            mm.then_inc(b_used, 1)
                            v.wait_ge(looked, n + 3)
                            v.wait_ge(hot, n * 2 + 2)
                            done(v.tensor_tensor(pick[k][:, :, :], oh_s[k][:, :, :],
                                                 ps_l[k][:, 0:GT * CH].rearrange("p (t c) -> p t c", c=CH), ALU.mult))
                            v.sem_inc(l_used, 1)
                            done(v.tensor_reduce(ahead[:, bass.ds(i * KB + k * GT, GT)], pick[k][:, :, :],
                                                 AX_X, ALU.add))

            chain2 = s2.sem("chain2")
            with nc.Block() as block:
                @block.vector
                def _(v):
                    done = Chain(v, chain2)
                    slot, col = ahead[:, 0:ET], rank[:, 0:ET]
                    done(v.tensor_tensor(slot, slot, col, ALU.add))
                    done(v.tensor_scalar(col, slot, 1.0 / P, -0.498, ALU.mult, ALU.add))
                    done(v.tensor_scalar(col, col, MAGIC, MAGIC, ALU.add, ALU.subtract))
                    done(v.scalar_tensor_tensor(out=slot_row[:, :], in0=col, scalar=-float(P), in1=slot,
                                                op0=ALU.mult, op1=ALU.add))
                    done(v.scalar_tensor_tensor(out=slot_row[:, :], in0=slot_row[:, :], scalar=float(NT), in1=col,
                                                op0=ALU.mult, op1=ALU.add))
                    done(v.tensor_copy(slot_u[:, :], slot_row[:, :]))

            SB, NS = 25, len(g.scattered)
            stage = s2.sb("stage", [EP, NS, SB, REC], F32)
            stage_i = s2.sb("stage_i", [EP, NS, SB], U32)
            issuing = s2.sem("issuing")
            staged, scattered = s2.sem("staged"), g.scattered
            with nc.Block() as block:
                @block.vector
                def _(v):
                    def fill(k, col):
                        v.tensor_copy(stage[:, k, :, :], rec[:, col, :]).then_inc(staged, 1)
                        v.tensor_copy(stage_i[:, k, :], slot_u[:, col]).then_inc(staged, 1)

                    for k in range(NS):
                        fill(k, bass.ds(k * SB, SB))
                    with v.Fori(1, ET // (SB * NS)) as i:
                        for k in range(NS):
                            v.wait_ge(scattered[k], i * (16 * SB))
                            fill(k, bass.ds(i * SB * NS + k * SB, SB))

                @block.gpsimd
                def _(pool):
                    rows = g.slots.rearrange("p n r -> (p n) r")
                    with pool.Fori(0, ET // (SB * NS)) as i:
                        for k in range(NS):
                            pool.wait_ge(staged, i * (2 * NS) + 2 * k + 2)
                            pool.sem_inc(issuing, 1)
                            for t in range(SB):
                                pool.indirect_dma_start(
                                    out=rows, out_offset=bass.IndirectOffsetOnAxis(stage_i[:, k, t:t + 1], 0),
                                    in_=stage[:, k, t, :], in_offset=None).then_inc(scattered[k], 16)
                    for k in range(NS):
                        pool.wait_ge(scattered[k], 16 * SB * (ET // (SB * NS)))


def load_slots(nc, g, name, slots, attr=None):
    with Stage(nc, name) as st:
        recs = st.sb("recs", [P, NT, REC], F32)
        recs_in = st.sem("recs_in")
        with nc.Block() as block:
            @block.sync
            def _(sp):
                sp.dma_start(recs[:, :, :], g.slots).then_inc(recs_in, 16)

            @block.vector
            def _(v):
                v.wait_ge(recs_in, 16)
                for n in range(2):
                    v.tensor_copy(slots[:, n, :], recs[:, :, n])
                if attr is not None:
                    v.tensor_copy(attr[:, :, :], recs[:, :, 2:REC])


def turn_slots(nc, g, name, slots, row_src, row_dst):
    with Stage(nc, name) as st:
        turned = [st.ps(f"turned{k}", [P, 1024], BF16) for k in range(2)]
        transposed, copied = st.sem("transposed"), st.sem("copied")
        with nc.Block() as block:
            @block.tensor
            def _(pe):
                for n in range(2):
                    for q in range(U // 4):
                        m = n * (U // 4) + q
                        if m >= 2:
                            pe.wait_ge(copied, m - 1)
                        for k in range(4):
                            mm = pe.transpose(turned[m % 2][0:NI, k * P:(k + 1) * P], slots[:, n, q * 4 + k:NT:U],
                                              g.ident_b[:, :])
                        mm.then_inc(transposed, 1)

            @block.scalar
            def _(act):
                for n, rows in enumerate((row_src, row_dst)):
                    for q in range(U // 4):
                        m = n * (U // 4) + q
                        act.wait_ge(transposed, m + 1)
                        act.activation(rows[:, q * 4:(q + 1) * 4, :].rearrange("i u e -> i (u e)"),
                                       turned[m % 2][0:NI, 0:4 * P], ACT.Copy).then_inc(copied, 1)


def chunks_of(nc, eng, where, i, n=U, most=CH - 1):
    _, values = nc.values_load_multi_w_load_instructions(
        where[0:1, bass.ds(i * n, n)], engines=[eng.engine], min_val=0, max_val=most,
        skip_runtime_bounds_check_because="the tile map is clamped to the last bucket on chip")
    return values


def build_counts(nc, g, counts, slots):
    G = 4
    K = U // G
    with Stage(nc, "build") as st:
        where = st.sb("where", [1, NT], I32)
        cols = [st.sb(f"cols{k}", [P, 2, G], F32) for k in range(K)]
        oh_s = [st.sb(f"oh_s{k}", [P, G, P], BF16) for k in range(K)]
        oh_d = [st.sb(f"oh_d{k}", [P, G, P], BF16) for k in range(K)]
        blk = [st.ps(f"blk{k}", [LO, 512], F32) for k in range(K)]
        zeroed, where_in, hot = st.sem("zeroed"), st.sem("where_in"), st.sem("hot")
        multiplied, added, staged = st.sem("multiplied"), st.sem("added"), st.sem("staged")
        with nc.Block() as block:
            @block.sync
            def _(sp):
                sp.dma_start(where[:, :], g.cell_dram).then_inc(where_in, 16)

            @block.gpsimd
            def _(pool):
                for n in range(5):
                    pool.memset(counts[:, n * 5 * NODES:(n + 1) * 5 * NODES], 0.0).then_inc(zeroed, 1)

            @block.scalar
            def _(act):
                with act.Fori(0, NI) as i:
                    for k in range(K):
                        act.wait_ge(multiplied, i * K + k + 1)
                        act.activation(cols[k][:, :, :], slots[:, :, bass.ds(i * U + k * G, G)], ACT.Copy
                                       ).then_inc(staged, 1)

            @block.tensor
            def _(pe):
                pe.sem_inc(multiplied, K)
                with pe.Fori(0, NI) as i:
                    for k in range(K):
                        n = i * K + k
                        pe.wait_ge(hot, n * 2 * G + 2 * G)
                        pe.wait_ge(added, (n + 1) * G)
                        for t in range(G):
                            mm = pe.matmul(blk[k][:, t * LO:(t + 1) * LO], oh_s[k][:, t, 0:LO], oh_d[k][:, t, 0:LO],
                                           start=True, stop=True)
                        mm.then_inc(multiplied, 1)

            @block.vector
            def _(v):
                v.sem_inc(added, K * G)
                v.wait_ge(zeroed, 5)
                v.wait_ge(where_in, 16)

                def one_hot(k, t):
                    for n, oh in enumerate((oh_s[k], oh_d[k])):
                        v.tensor_scalar(oh[:, t, :], g.iota_b[:, :], cols[k][:, n, t:t + 1], None, ALU.is_equal
                                        ).then_inc(hot, 1)

                def step(i, cell, n, k, ahead):
                    if ahead:
                        v.wait_ge(staged, n + 2)
                    for t in range(G):
                        if ahead:
                            one_hot((k + 1) % K, t)
                        if t == 0:
                            v.wait_ge(multiplied, n + K + 1)
                        cells = counts[:, bass.ds(cell[k * G + t] * LO, LO)]
                        v.wait_ge(added, K * G + n * G + t)
                        v.tensor_tensor(cells, cells, blk[k][:, t * LO:(t + 1) * LO], ALU.add).then_inc(added, 1)

                v.wait_ge(staged, 1)
                for t in range(G):
                    one_hot(0, t)
                with v.Fori(0, NI - 1) as i:
                    cell = chunks_of(nc, v, where, i, U, CH * CH - 1)
                    for k in range(K):
                        step(i, cell, i * K + k, k, True)
                cell = chunks_of(nc, v, where, NI - 1, U, CH * CH - 1)
                for k in range(K):
                    step(NI - 1, cell, (NI - 1) * K + k, k, k < K - 1)


def split3(v, done, whole, parts, rest):
    done(v.tensor_copy(parts[:, :, 0, :], whole))
    done(v.tensor_tensor(rest, whole, parts[:, :, 0, :], ALU.subtract))
    done(v.tensor_copy(parts[:, :, 1, :], rest))
    done(v.tensor_tensor(parts[:, :, 2, :], rest, parts[:, :, 1, :], ALU.subtract))


def spmm(nc, g, name, counts, parts, out, degree=None):
    N = 3 * D + (1 if degree is not None else 0)
    B = 5
    with Stage(nc, name) as st:
        acc = [st.ps(f"acc{k}", [LO, 512], F32) for k in range(B)]
        summed, taken = st.sem("summed"), st.sem("taken")
        with nc.Block() as block:
            @block.tensor
            def _(pe):
                for cd in range(CH):
                    pe.wait_ge(taken, cd + 1)
                    for cs in range(CH):
                        mm = pe.matmul(acc[cd % B][:, 0:N], counts[:, (cs * CH + cd) * LO:(cs * CH + cd + 1) * LO],
                                       parts[:, cs, 0:N], start=(cs == 0), stop=(cs == CH - 1))
                    mm.then_inc(summed, 1)

            @block.vector
            def _(v):
                v.sem_inc(taken, B)
                with v.Fori(0, CH // B) as i:
                    for k in range(B):
                        v.wait_ge(summed, i * B + k + 1)
                        if degree is not None:
                            v.tensor_copy(degree[:, bass.ds(i * B + k, 1)], acc[k][:, 3 * D:3 * D + 1])
                        v.tensor_reduce(out[:, bass.ds(i * B + k, 1), :].rearrange("p a f -> p (a f)"),
                                        acc[k][:, 0:3 * D].rearrange("p (s f) -> p f s", s=3),
                                        AX_X, ALU.add).then_inc(taken, 1)


def linear(nc, g, name, rows, K, weights, M, bias, out):
    NW = len(weights)
    with Stage(nc, name) as st:
        turned = [st.ps(f"turned{k}", [K, 512], F32) for k in range(2)]
        prod = [st.ps(f"prod{k}", [LO, 512], F32) for k in range(2)]
        lhs = [st.sb(f"lhs{k}", [K, NW * P], F32) for k in range(2)]
        transposed, copied = st.sem("transposed"), st.sem("copied")
        multiplied, added = st.sem("multiplied"), st.sem("added")
        with nc.Block() as block:
            @block.tensor
            def _(pe):
                for c in range(CH):
                    if c >= 2:
                        pe.wait_ge(copied, c - 1)
                    for w in range(NW):
                        mm = pe.transpose(turned[c % 2][:, w * P:w * P + LO], rows[:, c, w * K:(w + 1) * K],
                                          g.ident[0:LO, 0:LO])
                    mm.then_inc(transposed, 1)
                    if c >= 2:
                        pe.wait_ge(added, c - 1)
                    pe.wait_ge(copied, c + 1)
                    for w in range(NW):
                        mm = pe.matmul(prod[c % 2][:, 0:M], lhs[c % 2][:, w * P:w * P + LO], weights[w],
                                       start=(w == 0), stop=(w == NW - 1))
                    mm.then_inc(multiplied, 1)

            @block.scalar
            def _(act):
                for c in range(CH):
                    act.wait_ge(transposed, c + 1)
                    if c >= 2:
                        act.wait_ge(multiplied, c - 1)
                    act.activation(lhs[c % 2][:, :].rearrange("k (w p) -> k w p", w=NW)[:, :, 0:LO],
                                   turned[c % 2][:, 0:NW * P].rearrange("k (w p) -> k w p", w=NW)[:, :, 0:LO],
                                   ACT.Copy).then_inc(copied, 1)

            @block.vector
            def _(v):
                for c in range(CH):
                    v.wait_ge(multiplied, c + 1)
                    v.tensor_tensor(out[:, c, :], prod[c % 2][:, 0:M], bias, ALU.add).then_inc(added, 1)


def norm_relu(nc, g, name, x, out):
    with Stage(nc, name) as st:
        mean = st.sb("mean", [LO, CH], F32)
        var = st.sb("var", [LO, CH], F32)
        dev = st.sb("dev", [LO, CH], F32)
        sq = st.sb("sq", [LO, CH, D], F32)
        chain_sem, varied, rooted = st.sem("chain"), st.sem("varied"), st.sem("rooted")

        def over_features(a):
            return a[:, :].rearrange("p (c a) -> p c a", a=1).to_broadcast([LO, CH, D])

        with nc.Block() as block:
            @block.vector
            def _(v):
                done = Chain(v, chain_sem)
                done(v.tensor_reduce(mean[:, :], x[:, :, :], AX_X, ALU.add))
                done(v.tensor_scalar(mean[:, :], mean[:, :], 1.0 / D, None, ALU.mult))
                done(v.tensor_tensor(sq[:, :, :], x[:, :, :], over_features(mean), ALU.subtract))
                done(v.tensor_tensor(out, sq[:, :, :], sq[:, :, :], ALU.mult))
                done(v.tensor_reduce(var[:, :], out, AX_X, ALU.add))
                done(v.tensor_scalar(var[:, :], var[:, :], 1.0 / D, 1e-5, ALU.mult, ALU.add))
                v.sem_inc(varied, 1)
                v.wait_ge(rooted, 1)
                done(v.reciprocal(dev[:, :], var[:, :]))
                done(v.tensor_tensor(sq[:, :, :], sq[:, :, :], over_features(dev), ALU.mult))
                done(v.tensor_scalar(out, sq[:, :, :], 0.0, None, ALU.max))

            @block.scalar
            def _(act):
                act.wait_ge(varied, 1)
                act.activation(var[:, :], var[:, :], ACT.Sqrt).then_inc(rooted, 1)


def layer_sage(nc, g, W, counts):
    with Stage(nc, "sage") as st:
        parts = st.sb("parts", [LO, CH, 3 * D + 4], BF16)
        rows = st.sb("rows", [LO, CH, 2 * D], F32)
        rest = st.sb("rest", [LO, CH, D], F32)
        inv = st.sb("inv", [LO, CH], F32)
        w = st.sb("w", [2 * D, 3, D], F32)
        bias = st.sb("bias", [LO, 3, D], F32)
        w_in = st.sem("w_in")
        norm_relu(nc, g, "sage_norm", g.x, rows[:, :, D:2 * D])
        for layer in range(3):
            chain = [st.sem(f"chain{layer}{k}") for k in range(3)]
            with nc.Block() as block:
                if layer == 0:
                    @block.sync
                    def _(sp):
                        for n in range(3):
                            sp.dma_start(w[0:D, n, :], W[f"L0_gnn_Wl{n}"]).then_inc(w_in, 16)
                            sp.dma_start(w[D:2 * D, n, :], W[f"L0_gnn_Wr{n}"]).then_inc(w_in, 16)
                            sp.dma_start(bias[:, n, :], W[f"L0_gnn_b{n}"].rearrange("(a f) -> a f", a=1)
                                         .to_broadcast([LO, D])).then_inc(w_in, 16)
                        sp.wait_ge(w_in, 16 * 9)

                @block.vector
                def _(v):
                    done = Chain(v, chain[0])
                    if layer == 0:
                        v.memset(parts[:, :, 3 * D:], 1.0)
                    split3(v, done, rows[:, :, D:2 * D], parts[:, :, 0:3 * D].rearrange("p c (s f) -> p c s f", s=3),
                           rest[:, :, :])
            spmm(nc, g, f"sage_sum{layer}", counts, parts, rows[:, :, 0:D], g.degree if layer == 0 else None)
            with nc.Block() as block:
                @block.vector
                def _(v):
                    done = Chain(v, chain[1])
                    if layer == 0:
                        done(v.tensor_scalar(inv[:, :], g.degree[:, :], 1.0, None, ALU.max))
                        done(v.reciprocal(inv[:, :], inv[:, :]))
                    done(v.tensor_tensor(rows[:, :, 0:D], rows[:, :, 0:D],
                                         inv[:, :].rearrange("p (c a) -> p c a", a=1).to_broadcast([LO, CH, D]),
                                         ALU.mult))
            linear(nc, g, f"sage_lin{layer}", rows, 2 * D, [w[:, layer, :]], D, bias[:, layer, :], rest)
            with nc.Block() as block:
                @block.vector
                def _(v):
                    done = Chain(v, chain[2])
                    if layer < 2:
                        done(v.tensor_scalar(rows[:, :, D:2 * D], rest[:, :, :], 0.0, None, ALU.max))
                    else:
                        done(v.tensor_tensor(g.x[:, :, :], g.x[:, :, :], rest[:, :, :], ALU.add))


def counts_rows(nc, g, counts, degree_out):
    with Stage(nc, "degout") as st:
        scrap = st.sb("scrap", [LO, 2, CH * LO], BF16)
        s = st.sem("s")
        with nc.Block() as block:
            @block.scalar
            def _(act):
                for cs in range(CH):
                    if cs >= 2:
                        act.wait_ge(s, cs - 1)
                    act.activation(scrap[:, cs % 2, :], counts[:, cs * CH * LO:(cs + 1) * CH * LO], ACT.Copy,
                                   accum_out=degree_out[:, cs:cs + 1]).then_inc(s, 1)


def layer_appnp(nc, g, W, counts):
    with Stage(nc, "prop") as st:
        parts = st.sb("parts", [LO, CH, 3 * D], BF16)
        h = st.sb("h", [LO, CH, D], F32)
        h0 = st.sb("h0", [LO, CH, D], F32)
        rest = st.sb("rest", [LO, CH, D], F32)
        n_src = st.sb("n_src", [LO, CH], F32)
        n_dst = st.sb("n_dst", [LO, CH], F32)
        pos = st.sb("pos", [LO, CH], F32)
        w = st.sb("w", [D, D], F32)
        bias = st.sb("bias", [LO, D], F32)
        w_in, chain_sem, chain2, rooted, lifted = (st.sem(n) for n in ("w_in", "chain", "chain2", "rooted", "lifted"))
        norm_relu(nc, g, "prop_norm", g.x, h[:, :, :])
        with nc.Block() as block:
            @block.sync
            def _(sp):
                sp.dma_start(w[:, :], W["L2_gnn_W"]).then_inc(w_in, 16)
                sp.dma_start(bias[:, :], W["L2_gnn_b"].rearrange("(a f) -> a f", a=1).to_broadcast([LO, D])
                             ).then_inc(w_in, 16)
                sp.wait_ge(w_in, 32)

            @block.vector
            def _(v):
                done = Chain(v, chain_sem)
                for n, (deg, norm) in enumerate(((g.degree_out, n_src), (g.degree, n_dst))):
                    done(v.tensor_scalar(norm[:, :], deg[:, :], 1.0, None, ALU.max))
                v.sem_inc(lifted, 1)
                v.wait_ge(rooted, 2)
                for n, (deg, norm) in enumerate(((g.degree_out, n_src), (g.degree, n_dst))):
                    done(v.reciprocal(norm[:, :], norm[:, :]))
                    done(v.tensor_scalar(pos[:, :], deg[:, :], 0.0, 1.0 if n == 0 else 0.9, ALU.is_gt, ALU.mult))
                    done(v.tensor_tensor(norm[:, :], norm[:, :], pos[:, :], ALU.mult))

            @block.scalar
            def _(act):
                act.wait_ge(lifted, 1)
                act.activation(n_src[:, :], n_src[:, :], ACT.Sqrt).then_inc(rooted, 1)
                act.activation(n_dst[:, :], n_dst[:, :], ACT.Sqrt).then_inc(rooted, 1)
        linear(nc, g, "prop_lin", h, D, [w[:, :]], D, bias[:, :], h0)

        B = 5
        STEPS = 10
        acc = [st.ps(f"acc{k}", [LO, 512], F32) for k in range(B)]
        split, summed, chain3, chain4 = st.sem("split"), st.sem("summed"), st.sem("chain3"), st.sem("chain4")
        taken, started = st.sem("taken"), st.sem("started")

        def over(a):
            return a[:, :].rearrange("p (c a) -> p c a", a=1).to_broadcast([LO, CH, D])

        with nc.Block() as block:
            @block.tensor
            def _(pe):
                with pe.Fori(0, STEPS) as step:
                    pe.wait_ge(split, step + 1)
                    pe.sem_inc(started, 1)
                    for cd in range(CH):
                        pe.wait_ge(taken, step * CH + cd + 1)
                        for cs in range(CH):
                            mm = pe.matmul(acc[cd % B][:, 0:3 * D],
                                           counts[:, (cs * CH + cd) * LO:(cs * CH + cd + 1) * LO],
                                           parts[:, cs, :], start=(cs == 0), stop=(cs == CH - 1))
                        mm.then_inc(summed, 1)

            @block.vector
            def _(v):
                v.sem_inc(taken, B)
                done = Chain(v, chain2)
                done(v.tensor_copy(h[:, :, :], h0[:, :, :]))
                done(v.tensor_scalar(h0[:, :, :], h0[:, :, :], 0.1, None, ALU.mult))
                with v.Fori(0, STEPS) as step:
                    done = Chain(v, chain3, step * 7)
                    done(v.tensor_tensor(h[:, :, :], h[:, :, :], over(n_src), ALU.mult))
                    split3(v, done, h[:, :, :], parts[:, :, :].rearrange("p c (s f) -> p c s f", s=3), rest[:, :, :])
                    v.sem_inc(split, 1)
                    with v.Fori(0, CH // B) as i:
                        for k in range(B):
                            v.wait_ge(summed, step * CH + i * B + k + 1)
                            v.tensor_reduce(rest[:, bass.ds(i * B + k, 1), :].rearrange("p a f -> p (a f)"),
                                            acc[k][:, 0:3 * D].rearrange("p (s f) -> p f s", s=3),
                                            AX_X, ALU.add).then_inc(taken, 1)
                    v.wait_ge(taken, step * CH + CH + B)
                    done(v.tensor_tensor(rest[:, :, :], rest[:, :, :], over(n_dst), ALU.mult))
                    done(v.tensor_tensor(h[:, :, :], rest[:, :, :], h0[:, :, :], ALU.add))
                done = Chain(v, chain4)
                done(v.tensor_tensor(g.x[:, :, :], g.x[:, :, :], h[:, :, :], ALU.add))


GRP = 4
KG = U // GRP
NG = NT // GRP


def turn_scores(nc, g, name, H, scores, rows):
    with Stage(nc, name) as st:
        part = [st.sb(f"part{k}", [P, NT * H], BF16) for k in range(2)]
        turned = [st.ps(f"turned{k}", [P, 1024], BF16) for k in range(2)]
        chain_sem = st.sem("chain")
        transposed, copied, split = st.sem("transposed"), st.sem("copied"), st.sem("split")
        n_mm = 2 * H * U // 4
        with nc.Block() as block:
            @block.vector
            def _(v):
                done = Chain(v, chain_sem)
                flat = scores[:, :, :].rearrange("p n h -> p (n h)")
                done(v.tensor_copy(part[0][:, :], flat))
                done(v.tensor_tensor(part[1][:, :], flat, part[0][:, :], ALU.subtract))
                v.sem_inc(split, 1)

            @block.tensor
            def _(pe):
                pe.wait_ge(split, 1)
                m = 0
                for h in range(H):
                    for q in range(2):
                        src = part[q][:, :].rearrange("p (n h) -> p n h", h=H)
                        for u in range(0, U, 4):
                            if m >= 2:
                                pe.wait_ge(copied, m - 1)
                            for k in range(4):
                                mm = pe.transpose(turned[m % 2][0:NI, k * P:(k + 1) * P], src[:, u + k:NT:U, h],
                                                  g.ident_b[:, :])
                            mm.then_inc(transposed, 1)
                            m += 1

            @block.scalar
            def _(act):
                m = 0
                for h in range(H):
                    for q in range(2):
                        for u in range(0, U, 4):
                            act.wait_ge(transposed, m + 1)
                            act.activation(rows[:, u:u + 4, h, q, :],
                                           turned[m % 2][0:NI, 0:4 * P].rearrange("i (k e) -> i k e", k=4),
                                           ACT.Copy).then_inc(copied, 1)
                            m += 1


AHEAD = 2
HOT = 4
assert HOT == KG


class Rows:

    def __init__(self, nc, st, sides):
        self.nc, self.sides = nc, sides
        self.ps = [st.ps(f"ps_row{s}", [P, 512], F32) for s in range(len(sides))]
        self.wide = [[st.sb(f"wide{s}_{k}", [LO, GRP * P], BF16) for k in range(2)] for s in range(len(sides))]
        self.hot = [[st.sb(f"hot{s}_{k}", [LO, GRP * P], BF16) for k in range(HOT)] for s in range(len(sides))]
        self.spread, self.copied, self.compared = st.sem("spread"), st.sem("copied"), st.sem("compared")

    def spread_group(self, pe, g, m, i, k):
        n = len(self.sides)
        if not isinstance(m, int) or m > 0:
            pe.wait_ge(self.copied, m * n)
        for ps, rows in zip(self.ps, self.sides):
            pe.matmul(ps[:, :], g.ident_b[0:NI, bass.ds(i, 1)].to_broadcast([NI, P]),
                      rows[:, k * GRP:(k + 1) * GRP, :].rearrange("i u e -> i (u e)"),
                      start=True, stop=True).then_inc(self.spread, 1)

    def copy_group(self, act, m, b):
        n = len(self.sides)
        for s in range(n):
            act.wait_ge(self.spread, m * n + s + 1)
            if not isinstance(m, int) or m >= 2:
                act.wait_ge(self.compared, m * n - 2 * n + s + 1)
            act.activation(self.wide[s][b][:, :], self.ps[s][0:LO, :], ACT.Copy).then_inc(self.copied, 1)

    def compare_side(self, v, g, m, s, b, k):
        v.wait_ge(self.copied, m * len(self.sides) + s + 1)
        v.tensor_scalar(self.hot[s][k][:, :], self.wide[s][b][:, :], g.iota_part[0:LO, 0:1], None, ALU.is_equal
                        ).then_inc(self.compared, 1)


def score_pass(nc, g, name, src_parts, dst_parts, W, finish, slots=None, attr=None, attr_sum=None):
    with Stage(nc, name) as st:
        where = st.sb("where", [1, 2 * NT], I32)
        dsts = st.sb("dsts", [1, NT + GRP], I32)
        rows = Rows(nc, st, (g.row_src, g.row_dst))
        ROOM = 256 if W > P else W
        ps_x = [st.ps(f"ps_x{k}", [P, max(512, GRP * ROOM)], F32) for k in range(2)]
        if attr is not None:
            oh = [st.sb(f"oh{k}", [P, GRP, P], F32) for k in range(2)]
            cols = [st.sb(f"cols{k}", [P, GRP], F32) for k in range(2)]
            A = attr.shape[2]
            ps_a = [st.ps(f"ps_a{k}", [LO, 512], F32) for k in range(2)]
        where_in, cleared, attr_added = st.sem("where_in"), st.sem("cleared"), st.sem("attr_added")
        gathered, used = st.sem("gathered"), st.sem("used")
        hot, attr_mm, staged = st.sem("hot"), st.sem("attr_mm"), st.sem("staged")
        steps = finish(st, ps_x, gathered, used)
        with nc.Block() as block:
            @block.sync
            def _(sp):
                sp.dma_start(where[:, :], g.pairs_dram).then_inc(where_in, 16)
                sp.dma_start(dsts[:, GRP:], g.dst_dram).then_inc(where_in, 16)

            @block.tensor
            def _(pe):
                pe.sem_inc(gathered, 2)
                pe.wait_ge(where_in, 32)
                if attr is not None:
                    pe.sem_inc(attr_mm, GRP)
                def sum_attr(n, b, col):
                    pe.wait_ge(hot, n + 1)
                    pe.wait_ge(attr_added, n * GRP + GRP)
                    for t in range(GRP):
                        pe.matmul(ps_a[b][:, t * A:(t + 1) * A], oh[b][:, t, 0:LO],
                                  attr[:, bass.ds(col + t, 1), :].rearrange("p a h -> p (a h)"),
                                  start=True, stop=True).then_inc(attr_mm, 1)

                for m in range(AHEAD + 1):
                    rows.spread_group(pe, g, m, 0, m)
                with pe.Fori(0, NI) as i:
                    chunk = chunks_of(nc, pe, where, i, 2 * U)
                    for k in range(KG):
                        n, b = i * KG + k, k % 2
                        pe.wait_ge(rows.compared, n * 2 + 2)
                        pe.wait_ge(used, n + 1)
                        for t in range(GRP):
                            cs, cd = chunk[k * 2 * GRP + 2 * t], chunk[k * 2 * GRP + 2 * t + 1]
                            parts = [(rows.hot[0][k], src_parts, cs), (rows.hot[1][k], dst_parts, cd)]
                            for m, (h, table, c) in enumerate(parts):
                                mm = pe.matmul(ps_x[b][:, t * ROOM:t * ROOM + W], h[:, t * P:(t + 1) * P],
                                               table[:, bass.ds(c, 1), 0:W].rearrange("p a f -> p (a f)"),
                                               start=(m == 0), stop=(m == 1))
                        mm.then_inc(gathered, 1)
                        rows.spread_group(pe, g, n + AHEAD + 1, i + (k + AHEAD + 1) // KG, (k + AHEAD + 1) % KG)
                        if attr is not None:
                            sum_attr(n, 1 - b, i * U + k * GRP)
                if attr is not None:
                    sum_attr(NG, (NG - 1) % 2, NT)

            if attr is not None:
                @block.gpsimd
                def _(pool):
                    with pool.Fori(0, NI) as i:
                        for k in range(KG):
                            pool.wait_ge(attr_mm, (i * KG + k) * GRP + GRP)
                            pool.tensor_copy(cols[k % 2][:, :], slots[:, 1, bass.ds(i * U + k * GRP, GRP)]
                                             ).then_inc(staged, 1)

            @block.scalar
            def _(act):
                for m in range(AHEAD + 1):
                    rows.copy_group(act, m, m % 2)
                with act.Fori(0, NI) as i:
                    for k in range(KG):
                        n, b = i * KG + k, k % 2
                        rows.copy_group(act, n + AHEAD + 1, 1 - b)

            @block.vector
            def _(v):
                v.sem_inc(used, 2)
                if attr is not None:
                    v.sem_inc(attr_added, 2 * GRP)
                    v.memset(oh[1][:, :, :], 0.0).then_inc(cleared, 1)
                    v.memset(dsts[:, 0:GRP], 0).then_inc(cleared, 1)
                    v.wait_ge(cleared, 2)
                    v.sem_inc(hot, 1)
                v.wait_ge(where_in, 32)

                def attr_add(n, b, cell, t):
                    v.tensor_tensor(cell, cell, ps_a[b][:, t * A:(t + 1) * A], ALU.add).then_inc(attr_added, 1)

                for m in range(AHEAD):
                    for s in range(2):
                        rows.compare_side(v, g, m, s, m % 2, m)
                with v.Fori(0, NI) as i:
                    if attr is not None:
                        chunk = chunks_of(nc, v, dsts, i)
                    for k in range(KG):
                        n, b = i * KG + k, k % 2
                        steps[0](v, i, n, k, b)
                        v.wait_ge(gathered, n + 1)
                        rows.compare_side(v, g, n + AHEAD, 0, b, (k + AHEAD) % HOT)
                        if attr is not None:
                            v.wait_ge(staged, n + 1)
                            for t in range(GRP):
                                mm = v.tensor_scalar(oh[b][:, t, :], g.iota_free[:, :],
                                                     cols[b][:, t:t + 1], None, ALU.is_equal)
                            mm.then_inc(hot, 1)
                        steps[1](v, i, n, k, b)
                        rows.compare_side(v, g, n + AHEAD, 1, b, (k + AHEAD) % HOT)
                        if attr is not None:
                            v.wait_ge(attr_mm, n * GRP + 2 * GRP)
                            v.wait_ge(attr_added, n * GRP + 2 * GRP)
                            for t in range(GRP):
                                cell = attr_sum[:, t, bass.ds(chunk[k * GRP + t], 1), :].rearrange("p a h -> p (a h)")
                                attr_add(n, 1 - b, cell, t)
                        steps[2](v, i, n, k, b)
                if attr is not None:
                    chunk = chunks_of(nc, v, dsts, NG, GRP)
                    v.wait_ge(attr_mm, NG * GRP + 2 * GRP)
                    v.wait_ge(attr_added, NG * GRP + 2 * GRP)
                    for t in range(GRP):
                        cell = attr_sum[:, t, bass.ds(chunk[t], 1), :].rearrange("p a h -> p (a h)")
                        attr_add(NG, (NG - 1) % 2, cell, t)
                    v.wait_ge(attr_added, NG * GRP + 3 * GRP)
                    for t in range(1, GRP):
                        v.tensor_tensor(attr_sum[:, 0, :, :], attr_sum[:, 0, :, :], attr_sum[:, t, :, :], ALU.add
                                        ).then_inc(cleared, 1)
                        v.wait_ge(cleared, 2 + t)


def max_pass(nc, g, name, H, rows, top):
    TB = GRP // H
    NQ = GRP // TB
    with Stage(nc, name) as st:
        where = st.sb("where", [1, NT + GRP], I32)
        dst_rows = Rows(nc, st, (g.row_dst,))
        tile_top = [st.sb(f"tile_top{k}", [LO, GRP, H], F32) for k in range(2)]
        tops = st.sb("tops", [LO, GRP, CH, H], F32)
        ps_m = [st.ps(f"ps_m{k}", [LO, 512], F32) for k in range(4)]
        where_in, cleared = st.sem("where_in"), st.sem("cleared")
        masked, reduced, raised = st.sem("masked"), st.sem("reduced"), st.sem("raised")
        with nc.Block() as block:
            @block.sync
            def _(sp):
                sp.dma_start(where[:, GRP:], g.dst_dram).then_inc(where_in, 16)

            @block.tensor
            def _(pe):
                pe.sem_inc(masked, 2 * NQ)
                for m in range(AHEAD + 1):
                    dst_rows.spread_group(pe, g, m, 0, m)
                with pe.Fori(0, NI) as i:
                    for k in range(KG):
                        n = i * KG + k
                        pe.wait_ge(dst_rows.compared, n + 1)
                        for q in range(NQ):
                            bank = ps_m[(k * NQ + q) % 4]
                            pe.wait_ge(reduced, n * NQ + q + 1)
                            if H == 1:
                                hot = dst_rows.hot[0][k][:, :]
                            else:
                                hot = dst_rows.hot[0][k][:, q * P:(q + 1) * P].rearrange("p (a e) -> p a e", a=1
                                                                                         ).to_broadcast([LO, H, P])
                            pe.matmul(bank[:, :] if H == 1 else bank[:, :].rearrange("p (h e) -> p h e", h=H),
                                      g.off_diag[0:LO, 0:LO], hot, start=True, stop=False)
                            one = g.ident_b[0:NI, bass.ds(i, 1)].to_broadcast([NI, LO])
                            for part in range(2):
                                r = rows[:, (k * NQ + q) * TB:(k * NQ + q + 1) * TB, :, part, :]
                                mm = pe.matmul(bank[:, :].rearrange("p (u e) -> p u e", u=GRP), one,
                                               r.rearrange("i u h e -> i (u h) e"), start=False, stop=(part == 1))
                            mm.then_inc(masked, 1)
                        dst_rows.spread_group(pe, g, n + AHEAD + 1, i + (k + AHEAD + 1) // KG, (k + AHEAD + 1) % KG)

            @block.scalar
            def _(act):
                for m in range(AHEAD + 1):
                    dst_rows.copy_group(act, m, m % 2)
                with act.Fori(0, NI) as i:
                    for k in range(KG):
                        dst_rows.copy_group(act, i * KG + k + AHEAD + 1, (k + 1) % 2)

            @block.vector
            def _(v):
                v.sem_inc(reduced, 4)
                v.sem_inc(raised, GRP)
                v.memset(tile_top[1][:, :, :], -3.0e38).then_inc(cleared, 1)
                v.memset(where[:, 0:GRP], 0).then_inc(cleared, 1)
                for t in range(GRP):
                    v.tensor_copy(tops[:, t, :, :], top[:, :, :]).then_inc(cleared, 1)
                v.wait_ge(cleared, 2 + GRP)
                v.wait_ge(where_in, 16)

                def raise_top(chunk, b, t):
                    cell = tops[:, t, bass.ds(chunk, 1), :].rearrange("p a h -> p (a h)")
                    v.tensor_tensor(cell, cell, tile_top[b][:, t, :], ALU.max).then_inc(raised, 1)

                for m in range(AHEAD):
                    dst_rows.compare_side(v, g, m, 0, m % 2, m)
                with v.Fori(0, NI) as i:
                    chunk = chunks_of(nc, v, where, i)
                    for k in range(KG):
                        n, b = i * KG + k, k % 2
                        v.wait_ge(masked, n * NQ + NQ)
                        dst_rows.compare_side(v, g, n + AHEAD, 0, b, (k + AHEAD) % HOT)
                        v.wait_ge(raised, n * GRP + GRP)
                        for q in range(NQ):
                            v.wait_ge(masked, (n + 2) * NQ + q + 1)
                            v.tensor_reduce(tile_top[b][:, q * TB:(q + 1) * TB, :].rearrange("p t h -> p (t h)"),
                                            ps_m[(k * NQ + q) % 4][:, :].rearrange("p (u e) -> p u e", u=GRP),
                                            AX_X, ALU.max).then_inc(reduced, 1)
                            if q == 0:
                                v.wait_ge(reduced, n * NQ + 4)
                            for t in range(q * TB, (q + 1) * TB):
                                raise_top(chunk[k * GRP + t], 1 - b, t)
                chunk = chunks_of(nc, v, where, NG, GRP)
                v.wait_ge(reduced, NG * NQ + 4)
                v.wait_ge(raised, NG * GRP + GRP)
                for t in range(GRP):
                    raise_top(chunk[t], (NG - 1) % 2, t)
                v.wait_ge(raised, NG * GRP + 2 * GRP)
                for t in range(GRP):
                    v.tensor_tensor(top[:, :, :], top[:, :, :], tops[:, t, :, :], ALU.max).then_inc(cleared, 1)
                    v.wait_ge(cleared, 3 + GRP + t)


def sum_pass(nc, g, name, H, scores, top_parts, src_parts, slots, total):
    M = H * D + H
    with Stage(nc, name) as st:
        where = st.sb("where", [1, 2 * NT], I32)
        dsts = st.sb("dsts", [1, NT + GRP], I32)
        rows = Rows(nc, st, (g.row_src, g.row_dst))
        oh = [st.sb(f"oh{k}", [P, GRP, P], F32) for k in range(2)]
        cols = [st.sb(f"cols{k}", [P, GRP], F32) for k in range(2)]
        below = [st.sb(f"below{k}", [P, GRP, H], F32) for k in range(2)]
        y = [st.sb(f"y{k}", [P, GRP, M], F32) for k in range(2)]
        ps_x = [st.ps(f"ps_x{k}", [P, 512], F32) for k in range(2)]
        ps_y = [st.ps(f"ps_y{k}", [LO, 512], F32) for k in range(GRP)]
        where_in, cleared, gathered = (st.sem(n) for n in ("where_in", "cleared", "gathered"))
        staged, collected, lowered, weighed = (st.sem(n) for n in ("staged", "collected", "lowered", "weighed"))
        scaled, summed, added = (st.sem(n) for n in ("scaled", "summed", "added"))
        TOP = GRP * D
        with nc.Block() as block:
            @block.sync
            def _(sp):
                sp.dma_start(where[:, :], g.pairs_dram).then_inc(where_in, 16)
                sp.dma_start(dsts[:, GRP:], g.dst_dram).then_inc(where_in, 16)

            @block.tensor
            def _(pe):
                pe.sem_inc(gathered, 2)
                pe.sem_inc(summed, GRP)
                pe.wait_ge(where_in, 32)

                def gather(chunk, k, b):
                    for t in range(GRP):
                        cs, cd = chunk[k * 2 * GRP + 2 * t], chunk[k * 2 * GRP + 2 * t + 1]
                        pe.matmul(ps_x[b][:, TOP + t * 3 * H:TOP + (t + 1) * 3 * H],
                                  rows.hot[1][k][:, t * P:(t + 1) * P],
                                  top_parts[:, bass.ds(cd, 1), :].rearrange("p a f -> p (a f)"), start=True, stop=True)
                        for q in range(3):
                            mm = pe.matmul(ps_x[b][:, t * D:(t + 1) * D], rows.hot[0][k][:, t * P:(t + 1) * P],
                                           src_parts[:, bass.ds(cs, 1), q * D:(q + 1) * D
                                                     ].rearrange("p a f -> p (a f)"),
                                           start=(q == 0), stop=(q == 2))
                    mm.then_inc(gathered, 1)

                def sum_group(n, b):
                    pe.wait_ge(scaled, n + 2)
                    for t in range(GRP):
                        pe.wait_ge(added, n * GRP + t + 1)
                        pe.matmul(ps_y[t][:, 0:M], oh[b][:, t, 0:LO], y[b][:, t, :], start=True, stop=True
                                  ).then_inc(summed, 1)

                for m in range(AHEAD + 1):
                    rows.spread_group(pe, g, m, 0, m)
                with pe.Fori(0, NI) as i:
                    chunk = chunks_of(nc, pe, where, i, 2 * U)
                    for k in range(KG):
                        n, b = i * KG + k, k % 2
                        pe.wait_ge(rows.compared, n * 2 + 2)
                        pe.wait_ge(scaled, n + 1)
                        gather(chunk, k, b)
                        sum_group(n, 1 - b)
                        rows.spread_group(pe, g, n + AHEAD + 1, i + (k + AHEAD + 1) // KG, (k + AHEAD + 1) % KG)
                sum_group(NG, (NG - 1) % 2)

            @block.gpsimd
            def _(pool):
                with pool.Fori(0, NI) as i:
                    for k in range(KG):
                        pool.wait_ge(summed, (i * KG + k) * GRP + GRP)
                        pool.tensor_copy(cols[k % 2][:, :], slots[:, 1, bass.ds(i * U + k * GRP, GRP)]
                                         ).then_inc(staged, 1)

            @block.scalar
            def _(act):
                for m in range(AHEAD + 1):
                    rows.copy_group(act, m, m % 2)
                with act.Fori(0, NI) as i:
                    for k in range(KG):
                        n, b = i * KG + k, k % 2
                        act.wait_ge(lowered, n + 1)
                        act.wait_ge(summed, n * GRP + GRP)
                        act.activation(y[b][:, :, H * D:M], below[b][:, :, :], ACT.Exp).then_inc(weighed, 1)
                        rows.copy_group(act, n + AHEAD + 1, 1 - b)

            @block.vector
            def _(v):
                v.memset(dsts[:, 0:GRP], 0).then_inc(cleared, 1)
                v.memset(oh[1][:, :, :], 0.0).then_inc(cleared, 1)
                v.memset(y[1][:, :, :], 0.0).then_inc(cleared, 1)
                v.wait_ge(cleared, 3)
                v.sem_inc(scaled, 2)
                v.sem_inc(added, GRP)
                v.wait_ge(where_in, 32)

                def one_hot(b, t):
                    v.tensor_scalar(oh[b][:, t, :], g.iota_free[:, :], cols[b][:, t:t + 1], None, ALU.is_equal)

                def scale(b, t, w):
                    return v.tensor_tensor(
                        y[b][:, t:t + w, 0:H * D].rearrange("p t (h f) -> p t h f", h=H),
                        ps_x[b][:, t * D:(t + w) * D].rearrange("p (t a f) -> p t a f", t=w, a=1
                                                                ).to_broadcast([P, w, H, D]),
                        y[b][:, t:t + w, H * D:M].rearrange("p t (h a) -> p t h a", a=1).to_broadcast([P, w, H, D]),
                        ALU.mult)

                def add(chunk, n, t):
                    v.wait_ge(summed, (n + 1) * GRP + t + 1)
                    v.wait_ge(added, (n + 1) * GRP + t)
                    cell = total[:, bass.ds(chunk, 1), :].rearrange("p a f -> p (a f)")
                    v.tensor_tensor(cell, cell, ps_y[t][:, 0:M], ALU.add).then_inc(added, 1)

                for m in range(AHEAD):
                    for s in range(2):
                        rows.compare_side(v, g, m, s, m % 2, m)
                with v.Fori(0, NI) as i:
                    chunk = chunks_of(nc, v, dsts, i)
                    for k in range(KG):
                        n, b = i * KG + k, k % 2
                        before = chunk[k * GRP:(k + 1) * GRP]
                        v.wait_ge(gathered, n + 3)
                        v.tensor_reduce(below[b][:, :, :].rearrange("p t h -> p (t h)"),
                                        ps_x[b][:, TOP:TOP + GRP * 3 * H].rearrange("p (t s h) -> p t h s", t=GRP, s=3),
                                        AX_X, ALU.add).then_inc(collected, 1)
                        rows.compare_side(v, g, n + AHEAD, 0, b, (k + AHEAD) % HOT)
                        v.wait_ge(collected, n + 1)
                        v.tensor_tensor(below[b][:, :, :], scores[:, bass.ds(i * U + k * GRP, GRP), :],
                                        below[b][:, :, :], ALU.subtract).then_inc(lowered, 1)
                        rows.compare_side(v, g, n + AHEAD, 1, b, (k + AHEAD) % HOT)
                        add(before[0], n, 0)
                        v.wait_ge(staged, n + 1)
                        one_hot(b, 0)
                        one_hot(b, 1)
                        add(before[1], n, 1)
                        one_hot(b, 2)
                        one_hot(b, 3)
                        add(before[2], n, 2)
                        v.wait_ge(weighed, n + 1)
                        scale(b, 0, 2)
                        add(before[3], n, 3)
                        scale(b, 2, 2).then_inc(scaled, 1)
                last = chunks_of(nc, v, dsts, NG, GRP)
                for t in range(GRP):
                    add(last[t], NG, t)


def layer_gat2(nc, g, W):
    with Stage(nc, "gat2") as st:
        slots = st.sb("slots", [P, 2, NT], BF16)
        g.row_src = st.sb("row_src", [NI, U, P], BF16)
        g.row_dst = st.sb("row_dst", [NI, U, P], BF16)
        load_slots(nc, g, "load1", slots)
        turn_slots(nc, g, "turn1", slots, g.row_src, g.row_dst)
        h = st.sb("h", [LO, CH, D], F32)
        lr = st.sb("lr", [LO, CH, 2 * D], F32)
        l_parts = st.sb("l_parts", [LO, CH, 3 * D], BF16)
        r_parts = st.sb("r_parts", [LO, CH, 3 * D], BF16)
        rest = st.sb("rest", [LO, CH, D], F32)
        w = st.sb("w", [D, 2 * D], F32)
        bias = st.sb("bias", [LO, 2 * D], F32)
        att = st.sb("att", [P, D], F32)
        tail = st.sb("tail", [LO, 3, D], F32)
        own = st.sb("own", [LO, CH, 1], F32)
        top = st.sb("top", [LO, CH, 1], F32)
        top_parts = st.sb("top_parts", [LO, CH, 3], BF16)
        scores = st.sb("scores", [P, NT, 1], F32)
        rows = st.sb("rows", [NI, U, 1, 2, P], BF16)
        total = st.sb("total", [LO, CH, D + 1], F32)
        w_in = st.sem("w_in")
        chain = [st.sem(f"chain{k}") for k in range(6)]

        def row(name, p, n):
            return W[name].rearrange("(a f) -> a f", a=1).to_broadcast([p, n])

        with nc.Block() as block:
            @block.sync
            def _(sp):
                sp.dma_start(w[:, 0:D], W["L1_gnn_W_l"]).then_inc(w_in, 16)
                sp.dma_start(w[:, D:2 * D], W["L1_gnn_W_r"]).then_inc(w_in, 16)
                sp.dma_start(bias[:, 0:D], row("L1_gnn_b_l", LO, D)).then_inc(w_in, 16)
                sp.dma_start(bias[:, D:2 * D], row("L1_gnn_b_r", LO, D)).then_inc(w_in, 16)
                sp.dma_start(att[:, :], row("L1_gnn_att", P, D)).then_inc(w_in, 16)
                for n, name in enumerate(("L1_gnn_bias", "L1_gnn_gamma", "L1_gnn_beta")):
                    sp.dma_start(tail[:, n, :], row(name, LO, D)).then_inc(w_in, 16)
                sp.wait_ge(w_in, 16 * 8)
        norm_relu(nc, g, "gat2_norm", g.x, h[:, :, :])
        linear(nc, g, "gat2_lin", h, D, [w[:, :]], 2 * D, bias[:, :], lr)
        with nc.Block() as block:
            @block.vector
            def _(v):
                done = Chain(v, chain[0])
                v.memset(total[:, :, :], 0.0)
                for k, parts in enumerate((l_parts, r_parts)):
                    split3(v, done, lr[:, :, k * D:(k + 1) * D],
                           parts[:, :, :].rearrange("p c (s f) -> p c s f", s=3), rest[:, :, :])
                done(v.tensor_tensor(h[:, :, :], lr[:, :, 0:D], lr[:, :, D:2 * D], ALU.add))
                done(v.scalar_tensor_tensor(out=rest[:, :, :], in0=h[:, :, :], scalar=0.2, in1=h[:, :, :],
                                            op0=ALU.mult, op1=ALU.max))
                done(v.tensor_tensor(rest[:, :, :], rest[:, :, :],
                                     att[0:LO, :].rearrange("p (a f) -> p a f", a=1).to_broadcast([LO, CH, D]),
                                     ALU.mult))
                done(v.tensor_reduce(own[:, :, :].rearrange("p c a -> p (c a)"), rest[:, :, :], AX_X, ALU.add))
                done(v.tensor_copy(top[:, :, :], own[:, :, :]))

        def finish(st2, ps_x, gathered, used):
            z = [st2.sb(f"z{k}", [P, GRP, D], F32) for k in range(2)]
            bent = [st2.sb(f"bent{k}", [P, GRP, D], F32) for k in range(2)]
            bent_ready, weighed, scored = (st2.sem(n) for n in ("bent_ready", "weighed", "scored"))

            def collect(v, i, n, k, b):
                v.wait_ge(gathered, n + 3)
                v.tensor_reduce(z[b][:, :, :],
                                ps_x[b][:, :].rearrange("p (t x) -> p t x", t=GRP)[:, :, 0:3 * D]
                                .rearrange("p t (s f) -> p t f s", s=3), AX_X, ALU.add).then_inc(used, 1)

            def bend(v, i, n, k, b):
                v.wait_ge(used, n + 3)
                v.scalar_tensor_tensor(out=bent[b][:, :, :], in0=z[b][:, :, :], scalar=0.2, in1=z[b][:, :, :],
                                       op0=ALU.mult, op1=ALU.max).then_inc(bent_ready, 1)

            def score(v, i, n, k, b):
                v.wait_ge(bent_ready, n + 1)
                v.tensor_tensor(bent[b][:, :, :], bent[b][:, :, :],
                                att[:, :].rearrange("p (a f) -> p a f", a=1).to_broadcast([P, GRP, D]),
                                ALU.mult).then_inc(weighed, 1)
                v.wait_ge(weighed, n + 1)
                v.tensor_reduce(scores[:, bass.ds(i * U + k * GRP, GRP), :].rearrange("p t a -> p (t a)"),
                                bent[b][:, :, :], AX_X, ALU.add).then_inc(scored, 1)
            return collect, bend, score

        score_pass(nc, g, "gat2_score", l_parts, r_parts, 3 * D, finish)
        empty_scores(nc, "gat2_empty", 1, slots, scores)
        turn_scores(nc, g, "gat2_turn", 1, scores, rows)
        max_pass(nc, g, "gat2_max", 1, rows, top)
        with nc.Block() as block:
            @block.vector
            def _(v):
                done = Chain(v, chain[1])
                r = rest[:, :, 0]
                tp = top[:, :, 0]
                done(v.tensor_copy(top_parts[:, :, 0], tp))
                done(v.tensor_tensor(r, tp, top_parts[:, :, 0], ALU.subtract))
                done(v.tensor_copy(top_parts[:, :, 1], r))
                done(v.tensor_tensor(top_parts[:, :, 2], r, top_parts[:, :, 1], ALU.subtract))
        sum_pass(nc, g, "gat2_sum", 1, scores, top_parts, l_parts, slots, total)
        with Stage(nc, "gat2_end") as s2:
            ps = s2.ps("ps", [LO, 512], F32)
            stat = s2.sb("stat", [LO, 2, D], F32)
            part = s2.sb("part", [LO, D], F32)
            ones = s2.sb("ones", [LO, LO], F32)
            weighed, lowered, summed = s2.sem("weighed"), s2.sem("lowered"), s2.sem("summed")
            parted, rooted = s2.sem("parted"), s2.sem("rooted")

            def over(a, shape):
                return a.rearrange("p (a f) -> p a f", a=1).to_broadcast(shape)

            S3 = [LO, CH, D]
            with nc.Block() as block:
                @block.tensor
                def _(pe):
                    for n in range(2):
                        pe.wait_ge(parted, n + 1)
                        pe.matmul(ps[:, n * D:(n + 1) * D], ones[:, :], part[:, :], start=True, stop=True
                                  ).then_inc(summed, 1)

                @block.scalar
                def _(act):
                    act.wait_ge(lowered, 1)
                    act.activation(own[:, :, 0], own[:, :, 0], ACT.Exp).then_inc(weighed, 1)
                    act.wait_ge(lowered, 2)
                    act.activation(stat[:, 1, :], stat[:, 1, :], ACT.Sqrt).then_inc(rooted, 1)

                @block.vector
                def _(v):
                    done = Chain(v, chain[2])
                    done(v.memset(ones[:, :], 1.0))
                    done(v.tensor_tensor(own[:, :, :], own[:, :, :], top[:, :, :], ALU.subtract))
                    v.sem_inc(lowered, 1)
                    v.wait_ge(weighed, 1)
                    done(v.tensor_tensor(rest[:, :, :], lr[:, :, 0:D], own[:, :, :].to_broadcast(S3), ALU.mult))
                    done(v.tensor_tensor(rest[:, :, :], rest[:, :, :], total[:, :, 0:D], ALU.add))
                    done(v.tensor_tensor(own[:, :, :], own[:, :, :], total[:, :, D:D + 1], ALU.add))
                    done(v.reciprocal(own[:, :, :], own[:, :, :]))
                    done(v.tensor_tensor(rest[:, :, :], rest[:, :, :], own[:, :, :].to_broadcast(S3), ALU.mult))
                    done(v.tensor_tensor(rest[:, :, :], rest[:, :, :], over(tail[:, 0, :], S3), ALU.add))
                    done(v.tensor_reduce(part[:, :], rest[:, :, :].rearrange("p c f -> p f c"), AX_X, ALU.add))
                    v.sem_inc(parted, 1)
                    v.wait_ge(summed, 1)
                    done(v.tensor_scalar(stat[:, 0, :], ps[:, 0:D], 1.0 / NODES, None, ALU.mult))
                    done(v.tensor_tensor(rest[:, :, :], rest[:, :, :], over(stat[:, 0, :], S3), ALU.subtract))
                    done(v.tensor_tensor(h[:, :, :], rest[:, :, :], rest[:, :, :], ALU.mult))
                    done(v.tensor_reduce(part[:, :], h[:, :, :].rearrange("p c f -> p f c"), AX_X, ALU.add))
                    v.sem_inc(parted, 1)
                    v.wait_ge(summed, 2)
                    done(v.tensor_scalar(stat[:, 1, :], ps[:, D:2 * D], 1.0 / NODES, 1e-5, ALU.mult, ALU.add))
                    v.sem_inc(lowered, 1)
                    v.wait_ge(rooted, 1)
                    done(v.reciprocal(stat[:, 1, :], stat[:, 1, :]))
                    done(v.tensor_tensor(stat[:, 1, :], stat[:, 1, :], tail[:, 1, :], ALU.mult))
                    done(v.tensor_tensor(rest[:, :, :], rest[:, :, :], over(stat[:, 1, :], S3), ALU.mult))
                    done(v.tensor_tensor(rest[:, :, :], rest[:, :, :], over(tail[:, 2, :], S3), ALU.add))
                    done(v.tensor_tensor(g.x[:, :, :], g.x[:, :, :], rest[:, :, :], ALU.add))


def layer_gat(nc, g, W):
    H = HEADS
    with Stage(nc, "gat") as st:
        slots = st.sb("slots", [P, 2, NT], BF16)
        g.row_src = st.sb("row_src", [NI, U, P], BF16)
        g.row_dst = st.sb("row_dst", [NI, U, P], BF16)
        h = st.sb("h", [LO, CH, D], F32)
        h_parts = st.sb("h_parts", [LO, CH, 3 * D], BF16)
        own = st.sb("own", [LO, CH, H], F32)
        top = st.sb("top", [LO, CH, H], F32)
        top_parts = st.sb("top_parts", [LO, CH, 3 * H], BF16)
        scores = st.sb("scores", [P, NT, H], F32)
        a_sd = st.sb("a_sd", [LO, CH, 2 * H], F32)
        rest4 = st.sb("rest4", [LO, CH, H], F32)
        a_parts = [st.sb(f"a_parts{k}", [LO, CH, 3, H], BF16) for k in range(2)]
        combined = st.sb("combined", [P, 2, D], F32)
        shift = st.sb("shift", [LO, D], F32)
        tail = st.sb("tail", [LO, 3, D], F32)
        chain = [st.sem(f"chain{k}") for k in range(6)]
        norm_relu(nc, g, "gat_norm", g.x, h[:, :, :])

        def row(ap, p, n):
            return ap.to_broadcast([p, n])

        with Stage(nc, "gat_w") as s2:
            w = s2.sb("w", [D, H * D], F32)
            att = s2.sb("att", [D, 2, H * D], F32)
            prod = s2.sb("prod", [D, 2, H * D], F32)
            vec = s2.sb("vec", [D, 2 * H], F32)
            wp = s2.sb("wp", [P, 2, D], F32)
            bias_col = s2.sb("bias_col", [P, 2], F32)
            diag = s2.sb("diag", [P, 2, P], F32)
            none = s2.sb("none", [LO, 2 * H], F32)
            ps_w = s2.ps("ps_w", [P, 512], F32)
            ps_c = s2.ps("ps_c", [P, 512], F32)
            ps_b = s2.ps("ps_b", [LO, 512], F32)
            w_in, turned, laid, mixed = s2.sem("w_in"), s2.sem("turned"), s2.sem("laid"), s2.sem("mixed")
            with nc.Block() as block:
                @block.sync
                def _(sp):
                    sp.dma_start(w[:, :], W["L3_gnn_W"]).then_inc(w_in, 16)
                    for n, name in enumerate(("L3_gnn_att_src", "L3_gnn_att_dst")):
                        sp.dma_start(att[:, n, :], row(W[name].rearrange("(a h) c -> a (h c)", a=1), D, H * D)
                                     ).then_inc(w_in, 16)
                    sp.dma_start(wp[:, :, :], W["L3_gnn_Wp"].rearrange("(b k) f -> k b f", b=2)).then_inc(w_in, 16)
                    sp.dma_start(bias_col[:, :], W["L3_gnn_bias"].rearrange("(b k) -> k b", b=2),
                                 allow_slow_non_contiguous=True).then_inc(w_in, 16)
                    for n, name in enumerate(("L3_gnn_bp", "L3_gnn_gamma", "L3_gnn_beta")):
                        sp.dma_start(tail[:, n, :], row(W[name].rearrange("(a f) -> a f", a=1), LO, D)).then_inc(w_in, 16)
                    sp.wait_ge(w_in, 16 * 8)

                @block.tensor
                def _(pe):
                    pe.wait_ge(w_in, 16 * 8)
                    for b in range(2):
                        pe.transpose(ps_w[:, b * D:(b + 1) * D], w[:, b * P:(b + 1) * P], g.ident[0:D, 0:D]
                                     ).then_inc(turned, 1)
                    pe.wait_ge(laid, 1)
                    for b in range(2):
                        pe.matmul(ps_c[:, b * D:(b + 1) * D], diag[:, b, :], wp[:, b, :], start=True, stop=True
                                  ).then_inc(mixed, 1)
                    for b in range(2):
                        pe.matmul(ps_b[:, 0:D], bias_col[:, b:b + 1].to_broadcast([P, LO]), wp[:, b, :],
                                  start=(b == 0), stop=(b == 1)).then_inc(mixed, 1)

                @block.vector
                def _(v):
                    done = Chain(v, chain[0])
                    v.memset(none[:, :], 0.0)
                    done(v.memset(diag[:, :, :], 0.0))
                    v.wait_ge(turned, 2)
                    for b in range(2):
                        for k in range(2):
                            half = slice(k * D, (k + 1) * D)
                            done(v.tensor_copy(diag[half, b, half], ps_w[half, b * D:(b + 1) * D]))
                    v.sem_inc(laid, 1)
                    v.wait_ge(w_in, 16 * 8)
                    done(v.tensor_tensor(prod[:, :, :], att[:, :, :],
                                         w[:, :].rearrange("p (a c) -> p a c", a=1).to_broadcast([D, 2, H * D]),
                                         ALU.mult))
                    done(v.tensor_reduce(vec[:, :], prod[:, :, :].rearrange("p n (h c) -> p (n h) c", h=H),
                                         AX_X, ALU.add))
                    v.wait_ge(mixed, 4)
                    done(v.tensor_copy(combined[:, :, :].rearrange("p b f -> p (b f)"), ps_c[:, 0:2 * D]))
                    done(v.tensor_tensor(shift[:, :], ps_b[:, 0:D], tail[:, 0, :], ALU.add))
            linear(nc, g, "gat_vec", h, D, [vec[:, :]], 2 * H, none[:, :], a_sd)

        with Stage(nc, "gat_attr") as s2:
            attr = s2.sb("attr", [P, GRP + NT, H], F32)
            attr_sum = s2.sb("attr_sum", [LO, GRP, CH, H], F32)
            inv = s2.sb("inv", [LO, CH], F32)
            rest = s2.sb("rest", [LO, CH, D], F32)
            load_slots(nc, g, "load3", slots, attr[:, GRP:, :])
            turn_slots(nc, g, "turn3", slots, g.row_src, g.row_dst)
            with nc.Block() as block:
                @block.vector
                def _(v):
                    done = Chain(v, chain[1])
                    v.memset(attr[:, 0:GRP, :], 0.0)
                    v.memset(attr_sum[:, :, :, :], 0.0)
                    split3(v, done, h[:, :, :], h_parts[:, :, :].rearrange("p c (s f) -> p c s f", s=3),
                           rest[:, :, :])
                    for k in range(2):
                        split3(v, done, a_sd[:, :, k * H:(k + 1) * H], a_parts[k], rest4[:, :, :])

            def finish(st2, ps_x, gathered, used):
                raw = [st2.sb(f"raw{k}", [P, GRP, H], F32) for k in range(2)]
                with_attr, scored = st2.sem("with_attr"), st2.sem("scored")

                def collect(v, i, n, k, b):
                    v.wait_ge(gathered, n + 3)
                    v.tensor_reduce(raw[b][:, :, :].rearrange("p t h -> p (t h)"),
                                    ps_x[b][:, 0:GRP * 3 * H].rearrange("p (t s h) -> p t h s", t=GRP, s=3),
                                    AX_X, ALU.add).then_inc(used, 1)

                def add_attr(v, i, n, k, b):
                    v.wait_ge(used, n + 3)
                    v.tensor_tensor(raw[b][:, :, :], raw[b][:, :, :], attr[:, bass.ds(i * U + k * GRP + GRP, GRP), :],
                                    ALU.add).then_inc(with_attr, 1)

                def bend(v, i, n, k, b):
                    v.wait_ge(with_attr, n + 1)
                    v.scalar_tensor_tensor(out=scores[:, bass.ds(i * U + k * GRP, GRP), :], in0=raw[b][:, :, :],
                                           scalar=0.2, in1=raw[b][:, :, :], op0=ALU.mult, op1=ALU.max
                                           ).then_inc(scored, 1)
                return collect, add_attr, bend

            score_pass(nc, g, "gat_score", a_parts[0][:, :, :, :].rearrange("p c s h -> p c (s h)"),
                       a_parts[1][:, :, :, :].rearrange("p c s h -> p c (s h)"), 3 * H, finish, slots, attr, attr_sum)
            empty_scores(nc, "gat_empty", H, slots, scores)
            with nc.Block() as block:
                @block.vector
                def _(v):
                    done = Chain(v, chain[2])
                    done(v.tensor_scalar(inv[:, :], g.degree[:, :], 1.0, None, ALU.max))
                    done(v.reciprocal(inv[:, :], inv[:, :]))
                    done(v.tensor_tensor(attr_sum[:, 0, :, :], attr_sum[:, 0, :, :],
                                         inv[:, :].rearrange("p (c a) -> p c a", a=1).to_broadcast([LO, CH, H]),
                                         ALU.mult))
                    done(v.tensor_tensor(own[:, :, :], a_sd[:, :, 0:H], a_sd[:, :, H:2 * H], ALU.add))
                    done(v.tensor_tensor(own[:, :, :], own[:, :, :], attr_sum[:, 0, :, :], ALU.add))
                    done(v.scalar_tensor_tensor(out=own[:, :, :], in0=own[:, :, :], scalar=0.2, in1=own[:, :, :],
                                                op0=ALU.mult, op1=ALU.max))
                    done(v.tensor_copy(top[:, :, :], own[:, :, :]))
        with Stage(nc, "gat_rows") as s2:
            rows = s2.sb("rows", [NI, U, H, 2, P], BF16)
            turn_scores(nc, g, "gat_turn", H, scores, rows)
            max_pass(nc, g, "gat_max", H, rows, top)
        total = st.sb("total", [LO, CH, H * D + H], F32)
        with nc.Block() as block:
            @block.vector
            def _(v):
                done = Chain(v, chain[3])
                v.memset(total[:, :, :], 0.0)
                split3(v, done, top[:, :, :], top_parts[:, :, :].rearrange("p c (s h) -> p c s h", s=3), rest4[:, :, :])
        sum_pass(nc, g, "gat_sum", H, scores, top_parts, h_parts, slots, total)
        with Stage(nc, "gat_end") as s2:
            agg = s2.sb("agg", [LO, CH, H * D], F32)
            proj = s2.sb("proj", [LO, CH, D], F32)
            neg = s2.sb("neg", [LO, CH, D], F32)
            mean = s2.sb("mean", [LO, CH], F32)
            lowered, weighed = s2.sem("lowered"), s2.sem("weighed")

            def over(a):
                return a[:, :].rearrange("p (c a) -> p c a", a=1).to_broadcast([LO, CH, D])

            def all_over(a):
                return a.rearrange("p (a f) -> p a f", a=1).to_broadcast([LO, CH, D])

            with nc.Block() as block:
                @block.scalar
                def _(act):
                    act.wait_ge(lowered, 1)
                    act.activation(own[:, :, :], own[:, :, :], ACT.Exp).then_inc(weighed, 1)

                @block.vector
                def _(v):
                    done = Chain(v, chain[4])
                    done(v.tensor_tensor(own[:, :, :], own[:, :, :], top[:, :, :], ALU.subtract))
                    v.sem_inc(lowered, 1)
                    v.wait_ge(weighed, 1)
                    done(v.tensor_tensor(rest4[:, :, :], own[:, :, :], total[:, :, H * D:], ALU.add))
                    done(v.reciprocal(rest4[:, :, :], rest4[:, :, :]))
                    for k in range(H):
                        part = agg[:, :, k * D:(k + 1) * D]
                        done(v.tensor_tensor(part, h[:, :, :], own[:, :, k:k + 1].to_broadcast([LO, CH, D]), ALU.mult))
                        done(v.tensor_tensor(part, part, total[:, :, k * D:(k + 1) * D], ALU.add))
                        done(v.tensor_tensor(part, part, rest4[:, :, k:k + 1].to_broadcast([LO, CH, D]), ALU.mult))
            linear(nc, g, "gat_proj", agg, P, [combined[:, 0, :], combined[:, 1, :]], D, shift[:, :], proj)
            minned, exped, varied, rooted = s2.sem("minned"), s2.sem("exped"), s2.sem("varied"), s2.sem("rooted")
            with nc.Block() as block:
                @block.scalar
                def _(act):
                    act.wait_ge(minned, 1)
                    act.activation(neg[:, :, :], neg[:, :, :], ACT.Exp).then_inc(exped, 1)
                    act.wait_ge(varied, 1)
                    act.activation(mean[:, :], mean[:, :], ACT.Sqrt).then_inc(rooted, 1)

                @block.vector
                def _(v):
                    done = Chain(v, chain[5])
                    done(v.tensor_scalar(neg[:, :, :], proj[:, :, :], 0.0, None, ALU.min))
                    v.sem_inc(minned, 1)
                    done(v.scalar_tensor_tensor(out=h[:, :, :], in0=proj[:, :, :], scalar=0.0, in1=h[:, :, :],
                                                op0=ALU.max, op1=ALU.add))
                    v.wait_ge(exped, 1)
                    done(v.scalar_tensor_tensor(out=h[:, :, :], in0=neg[:, :, :], scalar=-1.0, in1=h[:, :, :],
                                                op0=ALU.add, op1=ALU.add))
                    done(v.tensor_reduce(mean[:, :], h[:, :, :], AX_X, ALU.add))
                    done(v.tensor_scalar(mean[:, :], mean[:, :], 1.0 / D, None, ALU.mult))
                    done(v.tensor_tensor(h[:, :, :], h[:, :, :], over(mean), ALU.subtract))
                    done(v.tensor_tensor(proj[:, :, :], h[:, :, :], h[:, :, :], ALU.mult))
                    done(v.tensor_reduce(mean[:, :], proj[:, :, :], AX_X, ALU.add))
                    done(v.tensor_scalar(mean[:, :], mean[:, :], 1.0 / D, 1e-5, ALU.mult, ALU.add))
                    v.sem_inc(varied, 1)
                    v.wait_ge(rooted, 1)
                    done(v.reciprocal(mean[:, :], mean[:, :]))
                    done(v.tensor_tensor(h[:, :, :], h[:, :, :], over(mean), ALU.mult))
                    done(v.tensor_tensor(h[:, :, :], h[:, :, :], all_over(tail[:, 1, :]), ALU.mult))
                    done(v.tensor_tensor(h[:, :, :], h[:, :, :], all_over(tail[:, 2, :]), ALU.add))
                    done(v.tensor_tensor(g.x[:, :, :], g.x[:, :, :], h[:, :, :], ALU.add))


def empty_scores(nc, name, H, slots, scores):
    with Stage(nc, name) as st:
        low = st.sb("low", [P, NT], F32)
        chain = st.sem("chain")
        with nc.Block() as block:
            @block.vector
            def _(v):
                done = Chain(v, chain)
                done(v.tensor_scalar(low[:, :], slots[:, 0, :], 0.0, -BIG, ALU.is_lt, ALU.mult))
                for h in range(H):
                    done(v.tensor_tensor(scores[:, :, h], scores[:, :, h], low[:, :], ALU.add))


class Globals:
    pass


def program(nc, x, src, dst, ea16, w_edge, att_edge, out, **W):
    g = Globals()
    with Stage(nc, "g") as st:
        g.iota_free = st.sb("iota_free", [P, P], F32)
        g.iota_b = st.sb("iota_b", [P, P], BF16)
        g.ident = st.sb("ident", [P, P], F32)
        g.ident_h = st.sb("ident_h", [P, P], FP16)
        g.ident_b = st.sb("ident_b", [P, P], BF16)
        g.before = st.sb("before", [P, P], F32)
        g.after = st.sb("after", [P, P], F32)
        g.off_diag = st.sb("off_diag", [P, P], BF16)
        g.cleared = st.sem("cleared")
        g.scattered = [st.sem(f"scattered{k}") for k in range(3)]
        g.iota_part = st.sb("iota_part", [P, 1], F32)
        g.slots = nc.dram_tensor("slots", (P, NT, REC), F32, kind="Internal").ap()
        g.ends_dram = nc.dram_tensor("ends", (CH, CH), F32, kind="Internal").ap()
        g.pairs_dram = nc.dram_tensor("tile_pairs", (1, NT * 2), I32, kind="Internal").ap()
        g.dst_dram = nc.dram_tensor("tile_dst", (1, NT), I32, kind="Internal").ap()
        g.cell_dram = nc.dram_tensor("tile_cell", (1, NT), I32, kind="Internal").ap()
        g.counts_dram = nc.dram_tensor("countsd", (LO, CH * NODES), BF16, kind="Internal").ap()
        build_constants(nc, g)
        sort_edges(nc, g, src, dst, ea16, w_edge, att_edge)
        g.x = st.sb("x", [LO, CH, D], F32)
        g.degree = st.sb("degree", [LO, CH], F32)
        g.degree_out = st.sb("degree_out", [LO, CH], F32)
        x_in, saved, loaded = st.sem("x_in"), st.sem("saved"), st.sem("loaded")
        with Stage(nc, "first") as s2:
            counts = s2.sb("counts", [LO, CH * NODES], BF16)
            with Stage(nc, "slots0") as s3:
                slots = s3.sb("slots", [P, 2, NT], BF16)
                load_slots(nc, g, "load0", slots)
                build_counts(nc, g, counts, slots)
            with nc.Block() as block:
                @block.sync
                def _(sp):
                    sp.dma_start(g.x[:, :, :], x.rearrange("(p c) f -> p c f", p=LO)).then_inc(x_in, 16)
                    sp.wait_ge(x_in, 16)
                    sp.dma_start(g.counts_dram, counts[:, :]).then_inc(saved, 16)
            counts_rows(nc, g, counts, g.degree_out)
            layer_sage(nc, g, W, counts)
            with nc.Block() as block:
                @block.sync
                def _(sp):
                    sp.wait_ge(saved, 16)
        layer_gat2(nc, g, W)
        with Stage(nc, "second") as s2:
            counts = s2.sb("counts", [LO, CH * NODES], BF16)
            with nc.Block() as block:
                @block.sync
                def _(sp):
                    sp.dma_start(counts[:, :], g.counts_dram).then_inc(loaded, 16)
                    sp.wait_ge(loaded, 16)
            layer_appnp(nc, g, W, counts)
        layer_gat(nc, g, W)
        with nc.Block() as block:
            @block.sync
            def _(sp):
                sp.dma_start(out.rearrange("(p c) f -> p c f", p=LO), g.x[:, :, :]).then_inc(saved, 16)
                sp.wait_ge(saved, 32)


_INS = {"x": "x", "src": "src", "dst": "dst", "ea16": "edge_attr_16", "w_edge": "L3_gnn_W_edge",
        "att_edge": "L3_gnn_att_edge"}
_SAME = ["L0_gnn_Wl0", "L0_gnn_Wr0", "L0_gnn_b0", "L0_gnn_Wl1", "L0_gnn_Wr1", "L0_gnn_b1", "L0_gnn_Wl2",
         "L0_gnn_Wr2", "L0_gnn_b2", "L1_gnn_W_l", "L1_gnn_b_l", "L1_gnn_W_r", "L1_gnn_b_r", "L1_gnn_att",
         "L1_gnn_bias", "L1_gnn_gamma", "L1_gnn_beta", "L2_gnn_W", "L2_gnn_b", "L3_gnn_W", "L3_gnn_att_src",
         "L3_gnn_att_dst", "L3_gnn_bias", "L3_gnn_Wp", "L3_gnn_bp", "L3_gnn_gamma", "L3_gnn_beta"]


def kernel(**inputs):
    import numpy as _np
    import concourse.bacc as _bacc
    from concourse import mybir as _mybir
    from concourse.bass_utils import run_bass_kernel_spmd as _run

    nc = _bacc.Bacc("TRN2", target_bir_lowering=False, num_devices=1)
    arrays, args = {}, {}
    for arg, name in {**_INS, **{n: n for n in _SAME}}.items():
        a = _np.ascontiguousarray(inputs[name])
        arrays[f"in_{name}_dram"] = a
        args[arg] = nc.dram_tensor(f"in_{name}_dram", a.shape, _mybir.dt.from_np(a.dtype), kind="ExternalInput").ap()
    args["out"] = nc.dram_tensor("out_dram", (NODES, D), F32, kind="ExternalOutput").ap()
    program(nc, **args)
    r = _run(nc, [arrays], core_ids=[0])
    return r.results[0]["out_dram"]
```

```python
from contextlib import ExitStack

import concourse.bass as bass
from concourse import mybir

ALU = mybir.AluOpType
ACT = mybir.ActivationFunctionType
F32 = mybir.dt.float32
BF16 = mybir.dt.bfloat16
FP16 = mybir.dt.float16
I32 = mybir.dt.int32
U32 = mybir.dt.uint32
AX_X = mybir.AxisListType.X

NODES = 3125
CH = 25
LO = NODES // CH
D = 64
HEADS = 4
EDGES = 103125
EP = 125
ET = EDGES // EP
EPAD = 832
P = 128
U = 16
NI = 90
NT = U * NI
assert NT >= (EDGES + CH * CH * (P - 1)) // P and LO * CH == NODES and EP * ET == EDGES
REC = 6
MAGIC = 12582912.0
BIG = 1.0e30


class Chain:

    def __init__(self, eng, sem, start=0):
        self.eng, self.sem, self.n = eng, sem, start

    def __call__(self, ins):
        self.n = self.n + 1
        ins.then_inc(self.sem, 1)
        self.eng.wait_ge(self.sem, self.n)


class Stage:

    def __init__(self, nc, name):
        self.nc, self.name, self.ctx, self.sems = nc, name, ExitStack(), []

    def __enter__(self):
        return self

    def __exit__(self, *a):
        if self.sems:
            for sem in self.sems:
                self.nc.gpsimd.sem_clear(sem)
            self.nc.all_engine_barrier()
        self.ctx.close()

    def sb(self, name, shape, dt):
        return self.ctx.enter_context(self.nc.sbuf_tensor(f"{self.name}_{name}", shape, dt))

    def ps(self, name, shape, dt):
        return self.ctx.enter_context(self.nc.psum_tensor(f"{self.name}_{name}", shape, dt))

    def sem(self, name):
        self.sems.append(self.ctx.enter_context(self.nc.semaphore(f"{self.name}_{name}")))
        return self.sems[-1]


def build_constants(nc, g):
    with Stage(nc, "const") as st:
        ready = st.sem("ready")
        chain_sem = st.sem("chain")
        with nc.Block() as block:
            @block.gpsimd
            def _(pool):
                pool.iota(g.iota_free[:, :], [[1, P]], base=0, channel_multiplier=0,
                          allow_small_or_imprecise_dtypes=True).then_inc(ready, 1)
                pool.iota(g.iota_part[:, :], [[1, 1]], base=0, channel_multiplier=1,
                          allow_small_or_imprecise_dtypes=True).then_inc(ready, 1)

            @block.vector
            def _(v):
                done = Chain(v, chain_sem)
                v.wait_ge(ready, 2)
                v.tensor_scalar(g.ident[:, :], g.iota_free[:, :], g.iota_part[:, 0:1], None, ALU.is_equal)
                v.tensor_scalar(g.ident_h[:, :], g.iota_free[:, :], g.iota_part[:, 0:1], None, ALU.is_equal)
                v.tensor_scalar(g.ident_b[:, :], g.iota_free[:, :], g.iota_part[:, 0:1], None, ALU.is_equal)
                v.tensor_copy(g.iota_b[:, :], g.iota_free[:, :])
                v.tensor_scalar(g.before[:, :], g.iota_free[:, :], g.iota_part[:, 0:1], None, ALU.is_lt)
                v.tensor_scalar(g.after[:, :], g.iota_free[:, :], g.iota_part[:, 0:1], None, ALU.is_gt)
                done(v.tensor_scalar(g.off_diag[:, :], g.iota_free[:, :], g.iota_part[:, 0:1], -BIG,
                                     ALU.not_equal, ALU.mult))


def sort_edges(nc, g, src, dst, ea16, w_edge, att_edge):
    with Stage(nc, "sort") as st:
        chunk_s = st.sb("chunk_s", [EP, EPAD + 8], F32)
        chunk_d = st.sb("chunk_d", [EP, EPAD + 8], F32)
        bucket = st.sb("bucket", [EP, EPAD], F32)
        nodes = st.sb("nodes", [EP, EPAD, 2], F32)
        attrs = st.sb("attrs", [EP, EPAD, 16], F32)
        wh = st.sb("wh", [EP, HEADS, 16], F32)
        attrs_in = st.sem("attrs_in")

        with Stage(nc, "decode") as s2:
            src_i = s2.sb("src_i", [EP, ET], I32)
            dst_i = s2.sb("dst_i", [EP, ET], I32)
            number = s2.sb("number", [EP, ET], F32)
            we = s2.sb("we", [EP, 16, HEADS * D], F32)
            wp = s2.sb("wp", [EP, 16, HEADS * D], F32)
            att = s2.sb("att", [EP, HEADS * D], F32)
            empty = s2.sb("empty", [P, U * REC], F32)
            nodes_in = s2.sem("nodes_in")
            weights_in = s2.sem("weights_in")
            empty_set = s2.sem("empty_set")
            chain_sem = s2.sem("chain")
            with nc.Block() as block:
                @block.sync
                def _(sp):
                    sp.dma_start(src_i[:, :], src.rearrange("(p t) -> p t", p=EP)).then_inc(nodes_in, 16)
                    sp.dma_start(dst_i[:, :], dst.rearrange("(p t) -> p t", p=EP)).then_inc(nodes_in, 16)
                    sp.dma_start(we[:, :, :].rearrange("p k c -> p (k c)"),
                                 w_edge.rearrange("(a k) c -> a (k c)", a=1).to_broadcast([EP, 16 * HEADS * D])
                                 ).then_inc(weights_in, 16)
                    sp.dma_start(att[:, :], att_edge.rearrange("(a h) c -> a (h c)", a=1)
                                 .to_broadcast([EP, HEADS * D])).then_inc(weights_in, 16)
                    sp.dma_start(attrs[:, 0:ET, :], ea16.rearrange("(p t) k -> p t k", p=EP)).then_inc(attrs_in, 16)

                @block.gpsimd
                def _(pool):
                    pool.memset(empty[:, :], 0.0).then_inc(empty_set, 1)
                    pool.wait_ge(empty_set, 1)
                    pool.memset(empty[:, :].rearrange("p (n r) -> p n r", r=REC)[:, :, 0:2], -1.0
                                ).then_inc(empty_set, 1)
                    pool.wait_ge(empty_set, 2)
                    slots = g.slots.rearrange("p (n u) r -> p n (u r)", u=U)
                    pool.dma_start(slots, empty[:, :].rearrange("p (a f) -> p a f", a=1)
                                   .to_broadcast([P, NI, U * REC])).then_inc(g.cleared, 16)
                    pool.wait_ge(g.cleared, 16)

                @block.vector
                def _(v):
                    done = Chain(v, chain_sem)
                    v.memset(chunk_s[:, ET:EPAD + 8], -1.0)
                    v.memset(chunk_d[:, ET:EPAD + 8], -1.0)
                    v.memset(bucket[:, ET:EPAD], -1.0)
                    v.memset(nodes[:, ET:EPAD, :], 0.0)
                    v.memset(attrs[:, ET:EPAD, :], 0.0)
                    v.wait_ge(nodes_in, 32)
                    for ids, chunk, field in ((src_i, chunk_s, 0), (dst_i, chunk_d, 1)):
                        done(v.tensor_copy(number[:, :], ids[:, :]))
                        lo = nodes[:, 0:ET, field]
                        done(v.tensor_scalar(lo, number[:, :], 1.0 / CH, -0.48, ALU.mult, ALU.add))
                        done(v.tensor_scalar(lo, lo, MAGIC, MAGIC, ALU.add, ALU.subtract))
                        done(v.scalar_tensor_tensor(out=chunk[:, 0:ET], in0=lo, scalar=-float(CH),
                                                    in1=number[:, :], op0=ALU.mult, op1=ALU.add))
                    done(v.scalar_tensor_tensor(out=bucket[:, 0:ET], in0=chunk_d[:, 0:ET], scalar=float(CH),
                                                in1=chunk_s[:, 0:ET], op0=ALU.mult, op1=ALU.add))
                    v.wait_ge(weights_in, 32)
                    done(v.tensor_tensor(wp[:, :, :], we[:, :, :],
                                         att[:, :].rearrange("p (a c) -> p a c", a=1)
                                         .to_broadcast([EP, 16, HEADS * D]), ALU.mult))
                    done(v.tensor_reduce(wh[:, :, :].rearrange("p h k -> p k h"),
                                         wp[:, :, :].rearrange("p k (h c) -> p k h c", h=HEADS), AX_X, ALU.add))

        pre = st.sb("pre", [CH, CH, EPAD + 1], F32)

        with Stage(nc, "count") as s2:
            GT = 16
            oh_s = [s2.sb(f"oh_s{k}", [EP, GT, CH], BF16) for k in range(2)]
            oh_d = [s2.sb(f"oh_d{k}", [EP, GT, CH], BF16) for k in range(2)]
            cnt = [s2.ps(f"cnt{k}", [CH, 512], F32) for k in range(2)]
            hot = s2.sem("hot")
            counted, copied = s2.sem("counted"), s2.sem("copied")
            n_iter = EPAD // (2 * GT)
            with nc.Block() as block:
                @block.vector
                def _(v):
                    v.memset(pre[:, :, 0:1], 0.0)
                    with v.Fori(0, n_iter) as i:
                        for k in range(2):
                            v.wait_ge(counted, i * 2 + k + 1)
                            for oh, chunk in ((oh_s[k], chunk_s), (oh_d[k], chunk_d)):
                                v.tensor_tensor(
                                    oh[:, :, :],
                                    chunk[:, bass.ds(i * 2 * GT + k * GT, GT)].rearrange("p (t a) -> p t a", a=1)
                                    .to_broadcast([EP, GT, CH]),
                                    g.iota_free[0:EP, 0:CH].rearrange("p (a c) -> p a c", a=1)
                                    .to_broadcast([EP, GT, CH]), ALU.is_equal).then_inc(hot, 1)

                @block.tensor
                def _(pe):
                    pe.sem_inc(counted, 2)
                    with pe.Fori(0, n_iter) as i:
                        for k in range(2):
                            pe.wait_ge(hot, i * 4 + 2 * k + 2)
                            pe.wait_ge(copied, i * 2 + k + 1)
                            for t in range(GT):
                                mm = pe.matmul(cnt[k][:, t * CH:(t + 1) * CH], oh_d[k][:, t, :], oh_s[k][:, t, :],
                                               start=True, stop=True)
                            mm.then_inc(counted, 1)

                @block.scalar
                def _(act):
                    act.sem_inc(copied, 2)
                    with act.Fori(0, n_iter) as i:
                        for k in range(2):
                            act.wait_ge(counted, i * 2 + k + 3)
                            act.activation(pre[:, :, bass.ds(i * 2 * GT + k * GT + 1, GT)],
                                           cnt[k][:, 0:GT * CH].rearrange("p (t c) -> p c t", c=CH),
                                           ACT.Copy).then_inc(copied, 1)

        with Stage(nc, "prefix") as s2:
            tiles = s2.sb("tiles", [CH, CH], F32)
            upto = s2.sb("upto", [CH, CH], F32)
            base = s2.sb("base", [CH, CH], F32)
            end = s2.sb("end", [CH, CH], F32)
            rows = s2.ps("rows", [CH, 1], F32)
            ends = s2.sb("ends", [NI, CH * CH], F32)
            tile_no = s2.sb("tile_no", [NI, U], F32)
            hits = s2.sb("hits", [NI, CH * CH], F32)
            tb = s2.sb("tb", [NI, U], F32)
            td = s2.sb("td", [NI, U], F32)
            ts = s2.sb("ts", [NI, U], F32)
            pairs = s2.sb("pairs", [NI, U, 2], I32)
            dsts = s2.sb("dsts", [NI, U], I32)
            cells = s2.sb("cells", [NI, U], I32)
            chain_sem = s2.sem("chain")
            summed, end_out, end_in = s2.sem("summed"), s2.sem("end_out"), s2.sem("end_in")
            row_base, numbered = s2.sem("row_base"), s2.sem("numbered")
            found, map_out = s2.sem("found"), s2.sem("map_out")
            with nc.Block() as block:
                @block.gpsimd
                def _(pool):
                    pool.iota(tile_no[:, :], [[1, U]], base=0, channel_multiplier=U,
                              allow_small_or_imprecise_dtypes=True).then_inc(numbered, 1)

                @block.tensor
                def _(pe):
                    pe.wait_ge(summed, 1)
                    pe.matmul(rows[:, :], g.after[0:CH, 0:CH], upto[:, CH - 1:CH], start=True, stop=True
                              ).then_inc(row_base, 1)

                @block.sync
                def _(sp):
                    sp.wait_ge(end_out, 1)
                    sp.dma_start(g.ends_dram, end[:, :]).then_inc(end_in, 16)
                    sp.wait_ge(end_in, 16)
                    sp.dma_start(ends[:, :], g.ends_dram.rearrange("(a d) s -> a (d s)", a=1)
                                 .to_broadcast([NI, CH * CH])).then_inc(end_in, 16)
                    sp.wait_ge(found, 1)
                    sp.dma_start(g.pairs_dram.rearrange("a (i u f) -> (a i) u f", u=U, f=2), pairs[:, :, :]).then_inc(map_out, 16)
                    sp.dma_start(g.dst_dram.rearrange("a (i u) -> (a i) u", u=U), dsts[:, :]).then_inc(map_out, 16)
                    sp.dma_start(g.cell_dram.rearrange("a (i u) -> (a i) u", u=U), cells[:, :]).then_inc(map_out, 16)
                    sp.wait_ge(map_out, 48)

                @block.vector
                def _(v):
                    done = Chain(v, chain_sem)
                    for cs in range(CH):
                        last = v.tensor_tensor_scan(pre[:, cs, :], pre[:, cs, :], pre[:, cs, :], 0.0,
                                                    ALU.add, ALU.bypass)
                        last.then_inc(chain_sem, 1)
                        done.n += 1
                    v.wait_ge(chain_sem, done.n)
                    done(v.tensor_scalar(tiles[:, :], pre[:, :, EPAD], P / 2 - 0.5, 1.0 / P, ALU.add, ALU.mult))
                    done(v.tensor_scalar(tiles[:, :], tiles[:, :], MAGIC, MAGIC, ALU.add, ALU.subtract))
                    done(v.tensor_tensor_scan(upto[:, :], tiles[:, :], tiles[:, :], 0.0, ALU.add, ALU.bypass))
                    v.sem_inc(summed, 1)
                    done(v.tensor_tensor(base[:, :], upto[:, :], tiles[:, :], ALU.subtract))
                    v.wait_ge(row_base, 1)
                    done(v.tensor_scalar(end[:, :], upto[:, :], rows[:, 0:1], None, ALU.add))
                    v.sem_inc(end_out, 1)
                    done(v.tensor_scalar(base[:, :], base[:, :], rows[:, 0:1], None, ALU.add))
                    done(v.scalar_tensor_tensor(
                        out=pre[:, :, :], in0=base[:, :].rearrange("p (c a) -> p c a", a=1)
                        .to_broadcast([CH, CH, EPAD + 1]), scalar=float(P), in1=pre[:, :, :],
                        op0=ALU.mult, op1=ALU.add))
                    v.wait_ge(end_in, 32)
                    v.wait_ge(numbered, 1)
                    for u in range(U):
                        done(v.tensor_scalar(hits[:, :], ends[:, :], tile_no[:, u:u + 1], None,
                                             ALU.is_le, ALU.add, accum_out=tb[:, u:u + 1]))
                    done(v.tensor_scalar(tb[:, :], tb[:, :], float(CH * CH - 1), None, ALU.min))
                    done(v.tensor_scalar(td[:, :], tb[:, :], 1.0 / CH, -0.48, ALU.mult, ALU.add))
                    done(v.tensor_scalar(td[:, :], td[:, :], MAGIC, MAGIC, ALU.add, ALU.subtract))
                    done(v.scalar_tensor_tensor(out=ts[:, :], in0=td[:, :], scalar=-float(CH), in1=tb[:, :],
                                                op0=ALU.mult, op1=ALU.add))
                    done(v.tensor_copy(pairs[:, :, 0], ts[:, :]))
                    done(v.tensor_copy(pairs[:, :, 1], td[:, :]))
                    done(v.tensor_copy(dsts[:, :], td[:, :]))
                    done(v.scalar_tensor_tensor(out=tb[:, :], in0=ts[:, :], scalar=float(CH), in1=td[:, :],
                                                op0=ALU.mult, op1=ALU.add))
                    done(v.tensor_copy(cells[:, :], tb[:, :]))
                    v.sem_inc(found, 1)

        KB, GT, SB = 16, 4, 8
        NB = EPAD // KB
        LAST = ET - (NB - 1) * KB
        with Stage(nc, "place") as s2:
            b_t = s2.sb("b_t", [NB, KB, EP], FP16)
            oh_s = [s2.sb(f"oh_s{k}", [EP, GT, CH], F32) for k in range(2)]
            oh_d = [s2.sb(f"oh_d{k}", [EP, GT, CH], BF16) for k in range(2)]
            oh_t = [s2.sb(f"oh_t{k}", [CH, GT * EP], F32) for k in range(2)]
            same = s2.sb("same", [EP, 2 * GT, EP], F32)
            pick = [s2.sb(f"pick{k}", [EP, GT, CH], F32) for k in range(2)]
            inner = s2.sb("inner", [EP, KB], F32)
            ahead = s2.sb("ahead", [EP, KB], F32)
            tile = s2.sb("tile", [EP, KB], F32)
            slot_row = s2.sb("slot_row", [EP, KB], F32)
            prod = s2.sb("prod", [EP, HEADS, SB, 16], F32)
            stage = s2.sb("stage", [EP, 2, SB, REC], F32)
            stage_i = s2.sb("stage_i", [EP, 2, SB], U32)
            ps_t = [s2.ps(f"ps_t{k}", [CH, 1024], BF16) for k in range(2)]
            ps_b = [s2.ps(f"ps_b{k}", [EP, 512], F32) for k in range(2)]
            ps_l = [s2.ps(f"ps_l{k}", [EP, 512], F32) for k in range(2)]
            turned, b_ready = s2.sem("turned"), s2.sem("b_ready")
            with nc.Block() as block:
                @block.tensor
                def _(pe):
                    for k in range(KB):
                        if k >= 2:
                            pe.wait_ge(b_ready, k - 1)
                        pe.transpose(ps_b[k % 2][0:NB, 0:EP], bucket[:, k::KB], g.ident[0:EP, 0:EP]
                                     ).then_inc(turned, 1)

                @block.scalar
                def _(act):
                    for k in range(KB):
                        act.wait_ge(turned, k + 1)
                        act.activation(b_t[:, k, :], ps_b[k % 2][0:NB, 0:EP], ACT.Copy).then_inc(b_ready, 1)

            hot = s2.sem("hot")
            t_ready, t_copied = s2.sem("t_ready"), s2.sem("t_copied")
            b_bcast, b_used = s2.sem("b_bcast"), s2.sem("b_used")
            looked, l_used = s2.sem("looked"), s2.sem("l_used")
            chain_sem, staged = s2.sem("chain"), s2.sem("staged")
            issuing, spreading = s2.sem("issuing"), s2.sem("spreading")
            scattered = g.scattered
            NG4 = KB // GT
            with nc.Block() as block:
                @block.tensor
                def _(pe):
                    pe.sem_inc(looked, 2)
                    with pe.Fori(0, NB) as i:
                        for k in range(NG4):
                            n, b = i * NG4 + k, k % 2
                            pe.wait_ge(hot, n * 2 + 2)
                            pe.wait_ge(t_copied, n + 1)
                            for t in range(GT):
                                mm = pe.transpose(ps_t[b][:, t * P:t * P + EP], oh_d[b][:, t, :],
                                                  g.ident_b[0:EP, 0:EP])
                            mm.then_inc(t_ready, 1)
                            pe.wait_ge(b_used, n + 1)
                            pe.sem_inc(spreading, 1)
                            pe.matmul(ps_b[b][:, 0:GT * EP], g.ident_h[0:NB, bass.ds(i, 1)].to_broadcast([NB, EP]),
                                      b_t[:, k * GT:(k + 1) * GT, :].rearrange("p t e -> p (t e)"),
                                      start=True, stop=True).then_inc(b_bcast, 1)
                            pe.wait_ge(t_copied, n + 3)
                            pe.wait_ge(l_used, n + 1)
                            for t in range(GT):
                                mm = pe.matmul(ps_l[b][:, t * CH:(t + 1) * CH], oh_t[b][:, t * EP:(t + 1) * EP],
                                               pre[:, :, bass.ds(i * KB + k * GT + t, 1)].rearrange("p c a -> p (c a)"),
                                               start=True, stop=True)
                            mm.then_inc(looked, 1)

                @block.scalar
                def _(act):
                    act.sem_inc(t_copied, 2)
                    with act.Fori(0, NB) as i:
                        for k in range(NG4):
                            act.wait_ge(t_ready, i * NG4 + k + 1)
                            act.wait_ge(looked, i * NG4 + k + 1)
                            act.activation(oh_t[k % 2][:, :].rearrange("c (t e) -> c t e", t=GT),
                                           ps_t[k % 2][:, 0:GT * P].rearrange("c (t e) -> c t e", t=GT)[:, :, 0:EP],
                                           ACT.Copy).then_inc(t_copied, 1)

                @block.vector
                def _(v):
                    v.sem_inc(b_used, 2)
                    v.sem_inc(l_used, 2)

                    def one_hots(b, col):
                        for oh, chunk in ((oh_s[b], chunk_s), (oh_d[b], chunk_d)):
                            v.tensor_tensor(
                                oh[:, :, :], chunk[:, col].rearrange("p (t a) -> p t a", a=1)
                                .to_broadcast([EP, GT, CH]),
                                g.iota_free[0:EP, 0:CH].rearrange("p (a c) -> p a c", a=1)
                                .to_broadcast([EP, GT, CH]), ALU.is_equal).then_inc(hot, 1)

                    def place(i, n, k, done):
                        b = k % 2
                        v.wait_ge(looked, n + 2)
                        one_hots(1 - b, bass.ds(i * KB + (k + 1) * GT, GT))
                        v.wait_ge(b_bcast, n + 1)
                        for t in range(GT):
                            c = k * GT + t
                            mm = v.scalar_tensor_tensor(
                                out=same[:, b * GT + t, :], in0=ps_b[b][:, t * EP:(t + 1) * EP],
                                scalar=bucket[:, bass.ds(i * KB + c, 1)],
                                in1=g.before[0:EP, 0:EP], op0=ALU.is_equal, op1=ALU.mult,
                                accum_out=inner[:, c:c + 1])
                        mm.then_inc(b_used, 1)
                        v.wait_ge(looked, n + 3)
                        v.wait_ge(hot, n * 2 + 2)
                        done(v.tensor_tensor(pick[b][:, :, :], oh_s[b][:, :, :],
                                             ps_l[b][:, 0:GT * CH].rearrange("p (t c) -> p t c", c=CH), ALU.mult))
                        v.sem_inc(l_used, 1)
                        done(v.tensor_reduce(ahead[:, k * GT:(k + 1) * GT], pick[b][:, :, :], AX_X, ALU.add))

                    def fill(i, half, first, done):
                        c = slice(half * SB, (half + 1) * SB)
                        slot, col, row = ahead[:, c], tile[:, c], slot_row[:, c]
                        done(v.tensor_tensor(slot, slot, inner[:, c], ALU.add))
                        cols = bass.ds(i * KB + half * SB, SB)
                        done(v.tensor_tensor(
                            prod[:, :, :, :],
                            attrs[:, cols, :].rearrange("p (a t) k -> p a t k", a=1).to_broadcast([EP, HEADS, SB, 16]),
                            wh[:, :, :].rearrange("p h (a k) -> p h a k", a=1).to_broadcast([EP, HEADS, SB, 16]),
                            ALU.mult))
                        done(v.tensor_scalar(col, slot, 1.0 / P, -0.498, ALU.mult, ALU.add))
                        done(v.tensor_scalar(col, col, MAGIC, MAGIC, ALU.add, ALU.subtract))
                        done(v.scalar_tensor_tensor(out=row, in0=col, scalar=-float(P), in1=slot,
                                                    op0=ALU.mult, op1=ALU.add))
                        if not first:
                            v.wait_ge(scattered[half], i * (16 * SB))
                        v.scalar_tensor_tensor(out=stage_i[:, half, :], in0=row, scalar=float(NT), in1=col,
                                               op0=ALU.mult, op1=ALU.add).then_inc(staged, 1)
                        v.tensor_reduce(stage[:, half, :, 2:REC].rearrange("p t h -> p h t"), prod[:, :, :, :],
                                        AX_X, ALU.add).then_inc(staged, 1)
                        v.tensor_copy(stage[:, half, :, 0:2], nodes[:, cols, :]).then_inc(staged, 1)

                    def step(i, first):
                        done = Chain(v, chain_sem, i * 18)
                        for k in range(NG4):
                            place(i, i * NG4 + k, k, done)
                            if k % 2 == 1:
                                fill(i, k // 2, first, done)

                    one_hots(0, bass.ds(0, GT))
                    v.wait_ge(attrs_in, 16)
                    step(0, True)
                    with v.Fori(1, NB) as i:
                        step(i, False)

                @block.gpsimd
                def _(pool):
                    rows = g.slots.rearrange("p n r -> (p n) r")

                    def scatter(n, half, count):
                        pool.wait_ge(staged, n * 3 + 3)
                        pool.sem_inc(issuing, 1)
                        for t in range(count):
                            pool.indirect_dma_start(
                                out=rows, out_offset=bass.IndirectOffsetOnAxis(stage_i[:, half, t:t + 1], 0),
                                in_=stage[:, half, t, :], in_offset=None).then_inc(scattered[half], 16)

                    with pool.Fori(0, NB - 1) as i:
                        for half in range(2):
                            scatter(i * 2 + half, half, SB)
                    for half in range(2):
                        scatter((NB - 1) * 2 + half, half, min(SB, LAST - half * SB))
                        pool.wait_ge(scattered[half], 16 * ((NB - 1) * SB + min(SB, LAST - half * SB)))


def load_slots(nc, g, name, slots, attr=None):
    with Stage(nc, name) as st:
        recs = st.sb("recs", [P, NT, REC], F32)
        recs_in = st.sem("recs_in")
        with nc.Block() as block:
            @block.sync
            def _(sp):
                sp.dma_start(recs[:, :, :], g.slots).then_inc(recs_in, 16)

            @block.vector
            def _(v):
                v.wait_ge(recs_in, 16)
                for n in range(2):
                    v.tensor_copy(slots[:, n, :], recs[:, :, n])
                if attr is not None:
                    v.tensor_copy(attr[:, :, :], recs[:, :, 2:REC])


def turn_slots(nc, g, name, slots, row_src, row_dst):
    with Stage(nc, name) as st:
        turned = [st.ps(f"turned{k}", [P, 1024], BF16) for k in range(2)]
        transposed, copied = st.sem("transposed"), st.sem("copied")
        with nc.Block() as block:
            @block.tensor
            def _(pe):
                for n in range(2):
                    for q in range(U // 4):
                        m = n * (U // 4) + q
                        if m >= 2:
                            pe.wait_ge(copied, m - 1)
                        for k in range(4):
                            mm = pe.transpose(turned[m % 2][0:NI, k * P:(k + 1) * P], slots[:, n, q * 4 + k:NT:U],
                                              g.ident_b[:, :])
                        mm.then_inc(transposed, 1)

            @block.scalar
            def _(act):
                for n, rows in enumerate((row_src, row_dst)):
                    for q in range(U // 4):
                        m = n * (U // 4) + q
                        act.wait_ge(transposed, m + 1)
                        act.activation(rows[:, q * 4:(q + 1) * 4, :].rearrange("i u e -> i (u e)"),
                                       turned[m % 2][0:NI, 0:4 * P], ACT.Copy).then_inc(copied, 1)


def chunks_of(nc, eng, where, i, n=U, most=CH - 1):
    _, values = nc.values_load_multi_w_load_instructions(
        where[0:1, bass.ds(i * n, n)], engines=[eng.engine], min_val=0, max_val=most,
        skip_runtime_bounds_check_because="the tile map is clamped to the last bucket on chip")
    return values


class ColumnHots:

    def __init__(self, g, st, n):
        self.g, self.n = g, n
        self.sq = st.sb("sq", [P, n, P], F32)
        self.squared, self.hot = st.sem("col_squared"), st.sem("col_hot")

    def squares(self, act, cols):
        for t in range(self.n):
            mm = act.activation(self.sq[:, t, :], self.g.iota_free[:, :], ACT.Square, bias=cols[:, t:t + 1], scale=-1.0)
        mm.then_inc(self.squared, 1)

    def hots(self, act, m, out):
        act.wait_ge(self.squared, m + 1)
        act.activation(out, self.sq[:, :, :], ACT.Relu, bias=1.0, scale=-1.0).then_inc(self.hot, 1)


def build_counts(nc, g, counts, slots):
    G = 4
    K = U // G
    with Stage(nc, "build") as st:
        where = st.sb("where", [1, NT], I32)
        dst_hots = ColumnHots(g, st, G)
        cols = [st.sb(f"cols{k}", [P, 2, G], F32) for k in range(K)]
        oh_s = [st.sb(f"oh_s{k}", [P, G, P], BF16) for k in range(K)]
        oh_d = [st.sb(f"oh_d{k}", [P, G, P], BF16) for k in range(K)]
        blk = [st.ps(f"blk{k}", [LO, 512], F32) for k in range(K)]
        zeroed, where_in, hot = st.sem("zeroed"), st.sem("where_in"), st.sem("hot")
        multiplied, added, staged = st.sem("multiplied"), st.sem("added"), st.sem("staged")
        with nc.Block() as block:
            @block.sync
            def _(sp):
                sp.dma_start(where[:, :], g.cell_dram).then_inc(where_in, 16)

            @block.gpsimd
            def _(pool):
                for n in range(3):
                    pool.memset(counts[:, n * 5 * NODES:(n + 1) * 5 * NODES], 0.0).then_inc(zeroed, 1)
                with pool.Fori(0, NI) as i:
                    for k in range(K):
                        pool.wait_ge(multiplied, i * K + k + 1)
                        pool.tensor_copy(cols[k][:, :, :], slots[:, :, bass.ds(i * U + k * G, G)]
                                         ).then_inc(staged, 1)

            @block.scalar
            def _(act):
                act.sem_inc(dst_hots.hot, 1)
                with act.Fori(0, NI) as i:
                    for k in range(K):
                        n = i * K + k
                        act.wait_ge(staged, n + 1)
                        act.wait_ge(dst_hots.hot, n + 1)
                        dst_hots.squares(act, cols[k][:, 1, :])
                        dst_hots.hots(act, n, oh_d[k][:, :, :])

            @block.tensor
            def _(pe):
                pe.sem_inc(multiplied, K)
                with pe.Fori(0, NI) as i:
                    for k in range(K):
                        n = i * K + k
                        pe.wait_ge(hot, n * G + G)
                        pe.wait_ge(dst_hots.hot, n + 2)
                        pe.wait_ge(added, (n + 1) * G)
                        for t in range(G):
                            mm = pe.matmul(blk[k][:, t * LO:(t + 1) * LO], oh_s[k][:, t, 0:LO], oh_d[k][:, t, 0:LO],
                                           start=True, stop=True)
                        mm.then_inc(multiplied, 1)

            @block.vector
            def _(v):
                v.sem_inc(added, K * G)
                for n in range(3, 5):
                    v.memset(counts[:, n * 5 * NODES:(n + 1) * 5 * NODES], 0.0).then_inc(zeroed, 1)
                v.wait_ge(zeroed, 5)
                v.wait_ge(where_in, 16)

                def one_hot(k, t):
                    v.tensor_scalar(oh_s[k][:, t, :], g.iota_b[:, :], cols[k][:, 0, t:t + 1], None, ALU.is_equal
                                    ).then_inc(hot, 1)

                def step(i, cell, n, k, ahead):
                    if ahead:
                        v.wait_ge(staged, n + 2)
                    for t in range(G):
                        if ahead:
                            one_hot((k + 1) % K, t)
                        if t == 0:
                            v.wait_ge(multiplied, n + K + 1)
                        cells = counts[:, bass.ds(cell[k * G + t] * LO, LO)]
                        v.wait_ge(added, K * G + n * G + t)
                        v.tensor_tensor(cells, cells, blk[k][:, t * LO:(t + 1) * LO], ALU.add).then_inc(added, 1)

                v.wait_ge(staged, 1)
                for t in range(G):
                    one_hot(0, t)
                with v.Fori(0, NI - 1) as i:
                    cell = chunks_of(nc, v, where, i, U, CH * CH - 1)
                    for k in range(K):
                        step(i, cell, i * K + k, k, True)
                cell = chunks_of(nc, v, where, NI - 1, U, CH * CH - 1)
                for k in range(K):
                    step(NI - 1, cell, (NI - 1) * K + k, k, k < K - 1)


def split3(v, done, whole, parts, rest):
    done(v.tensor_copy(parts[:, :, 0, :], whole))
    done(v.tensor_tensor(rest, whole, parts[:, :, 0, :], ALU.subtract))
    done(v.tensor_copy(parts[:, :, 1, :], rest))
    done(v.tensor_tensor(parts[:, :, 2, :], rest, parts[:, :, 1, :], ALU.subtract))


def spmm(nc, g, name, counts, parts, out, degree=None, degree_out=None):
    N = 3 * D + (1 if degree is not None else 0)
    B = 5
    with Stage(nc, name) as st:
        acc = [st.ps(f"acc{k}", [LO, 512], F32) for k in range(B)]
        summed, taken = st.sem("summed"), st.sem("taken")
        if degree_out is not None:
            scrap = st.sb("scrap", [LO, 2, CH * LO], BF16)
            counted = st.sem("counted")
        with nc.Block() as block:
            if degree_out is not None:
                @block.scalar
                def _(act):
                    for cs in range(CH):
                        if cs >= 2:
                            act.wait_ge(counted, cs - 1)
                        act.activation(scrap[:, cs % 2, :], counts[:, cs * CH * LO:(cs + 1) * CH * LO], ACT.Copy,
                                       accum_out=degree_out[:, cs:cs + 1]).then_inc(counted, 1)

            @block.tensor
            def _(pe):
                for cd in range(CH):
                    pe.wait_ge(taken, cd + 1)
                    for cs in range(CH):
                        mm = pe.matmul(acc[cd % B][:, 0:N], counts[:, (cs * CH + cd) * LO:(cs * CH + cd + 1) * LO],
                                       parts[:, cs, 0:N], start=(cs == 0), stop=(cs == CH - 1))
                    mm.then_inc(summed, 1)

            @block.vector
            def _(v):
                v.sem_inc(taken, B)
                with v.Fori(0, CH // B) as i:
                    for k in range(B):
                        v.wait_ge(summed, i * B + k + 1)
                        if degree is not None:
                            v.tensor_copy(degree[:, bass.ds(i * B + k, 1)], acc[k][:, 3 * D:3 * D + 1])
                        v.tensor_reduce(out[:, bass.ds(i * B + k, 1), :].rearrange("p a f -> p (a f)"),
                                        acc[k][:, 0:3 * D].rearrange("p (s f) -> p f s", s=3),
                                        AX_X, ALU.add).then_inc(taken, 1)


def linear(nc, g, name, rows, K, weights, M, bias, out):
    NW = len(weights)
    with Stage(nc, name) as st:
        turned = [st.ps(f"turned{k}", [K, 512], F32) for k in range(2)]
        prod = [st.ps(f"prod{k}", [LO, 512], F32) for k in range(2)]
        lhs = [st.sb(f"lhs{k}", [K, NW * P], F32) for k in range(2)]
        transposed, copied = st.sem("transposed"), st.sem("copied")
        multiplied, added = st.sem("multiplied"), st.sem("added")
        with nc.Block() as block:
            @block.tensor
            def _(pe):
                for c in range(CH):
                    if c >= 2:
                        pe.wait_ge(copied, c - 1)
                    for w in range(NW):
                        mm = pe.transpose(turned[c % 2][:, w * P:w * P + LO], rows[:, c, w * K:(w + 1) * K],
                                          g.ident[0:LO, 0:LO])
                    mm.then_inc(transposed, 1)
                    if c >= 2:
                        pe.wait_ge(added, c - 1)
                    pe.wait_ge(copied, c + 1)
                    for w in range(NW):
                        mm = pe.matmul(prod[c % 2][:, 0:M], lhs[c % 2][:, w * P:w * P + LO], weights[w],
                                       start=(w == 0), stop=(w == NW - 1))
                    mm.then_inc(multiplied, 1)

            @block.scalar
            def _(act):
                for c in range(CH):
                    act.wait_ge(transposed, c + 1)
                    if c >= 2:
                        act.wait_ge(multiplied, c - 1)
                    act.activation(lhs[c % 2][:, :].rearrange("k (w p) -> k w p", w=NW)[:, :, 0:LO],
                                   turned[c % 2][:, 0:NW * P].rearrange("k (w p) -> k w p", w=NW)[:, :, 0:LO],
                                   ACT.Copy).then_inc(copied, 1)

            @block.vector
            def _(v):
                for c in range(CH):
                    v.wait_ge(multiplied, c + 1)
                    v.tensor_tensor(out[:, c, :], prod[c % 2][:, 0:M], bias, ALU.add).then_inc(added, 1)


def norm_relu(nc, g, name, x, out):
    with Stage(nc, name) as st:
        mean = st.sb("mean", [LO, CH], F32)
        var = st.sb("var", [LO, CH], F32)
        dev = st.sb("dev", [LO, CH], F32)
        sq = st.sb("sq", [LO, CH, D], F32)
        chain_sem, varied, rooted = st.sem("chain"), st.sem("varied"), st.sem("rooted")

        def over_features(a):
            return a[:, :].rearrange("p (c a) -> p c a", a=1).to_broadcast([LO, CH, D])

        with nc.Block() as block:
            @block.vector
            def _(v):
                done = Chain(v, chain_sem)
                done(v.tensor_reduce(mean[:, :], x[:, :, :], AX_X, ALU.add))
                done(v.tensor_scalar(mean[:, :], mean[:, :], 1.0 / D, None, ALU.mult))
                done(v.tensor_tensor(sq[:, :, :], x[:, :, :], over_features(mean), ALU.subtract))
                done(v.tensor_tensor(out, sq[:, :, :], sq[:, :, :], ALU.mult))
                done(v.tensor_reduce(var[:, :], out, AX_X, ALU.add))
                done(v.tensor_scalar(var[:, :], var[:, :], 1.0 / D, 1e-5, ALU.mult, ALU.add))
                v.sem_inc(varied, 1)
                v.wait_ge(rooted, 1)
                done(v.reciprocal(dev[:, :], var[:, :]))
                done(v.tensor_tensor(sq[:, :, :], sq[:, :, :], over_features(dev), ALU.mult))
                done(v.tensor_scalar(out, sq[:, :, :], 0.0, None, ALU.max))

            @block.scalar
            def _(act):
                act.wait_ge(varied, 1)
                act.activation(var[:, :], var[:, :], ACT.Sqrt).then_inc(rooted, 1)


def layer_sage(nc, g, W, counts):
    with Stage(nc, "sage") as st:
        parts = st.sb("parts", [LO, CH, 3 * D + 4], BF16)
        rows = st.sb("rows", [LO, CH, 2 * D], F32)
        rest = st.sb("rest", [LO, CH, D], F32)
        inv = st.sb("inv", [LO, CH], F32)
        w = st.sb("w", [2 * D, 3, D], F32)
        bias = st.sb("bias", [LO, 3, D], F32)
        w_in = st.sem("w_in")
        norm_relu(nc, g, "sage_norm", g.x, rows[:, :, D:2 * D])
        for layer in range(3):
            chain = [st.sem(f"chain{layer}{k}") for k in range(3)]
            with nc.Block() as block:
                if layer == 0:
                    @block.sync
                    def _(sp):
                        for n in range(3):
                            sp.dma_start(w[0:D, n, :], W[f"L0_gnn_Wl{n}"]).then_inc(w_in, 16)
                            sp.dma_start(w[D:2 * D, n, :], W[f"L0_gnn_Wr{n}"]).then_inc(w_in, 16)
                            sp.dma_start(bias[:, n, :], W[f"L0_gnn_b{n}"].rearrange("(a f) -> a f", a=1)
                                         .to_broadcast([LO, D])).then_inc(w_in, 16)
                        sp.wait_ge(w_in, 16 * 9)

                @block.vector
                def _(v):
                    done = Chain(v, chain[0])
                    if layer == 0:
                        v.memset(parts[:, :, 3 * D:], 1.0)
                    split3(v, done, rows[:, :, D:2 * D], parts[:, :, 0:3 * D].rearrange("p c (s f) -> p c s f", s=3),
                           rest[:, :, :])
            spmm(nc, g, f"sage_sum{layer}", counts, parts, rows[:, :, 0:D], g.degree if layer == 0 else None,
                 g.degree_out if layer == 0 else None)
            with nc.Block() as block:
                @block.vector
                def _(v):
                    done = Chain(v, chain[1])
                    if layer == 0:
                        done(v.tensor_scalar(inv[:, :], g.degree[:, :], 1.0, None, ALU.max))
                        done(v.reciprocal(inv[:, :], inv[:, :]))
                    done(v.tensor_tensor(rows[:, :, 0:D], rows[:, :, 0:D],
                                         inv[:, :].rearrange("p (c a) -> p c a", a=1).to_broadcast([LO, CH, D]),
                                         ALU.mult))
            linear(nc, g, f"sage_lin{layer}", rows, 2 * D, [w[:, layer, :]], D, bias[:, layer, :], rest)
            with nc.Block() as block:
                @block.vector
                def _(v):
                    done = Chain(v, chain[2])
                    if layer < 2:
                        done(v.tensor_scalar(rows[:, :, D:2 * D], rest[:, :, :], 0.0, None, ALU.max))
                    else:
                        done(v.tensor_tensor(g.x[:, :, :], g.x[:, :, :], rest[:, :, :], ALU.add))


def layer_appnp(nc, g, W, counts, loaded):
    B = 5
    NB = CH // B
    STEPS = 10
    OPS = 7
    with Stage(nc, "prop") as st:
        h0 = st.sb("h0", [LO, CH, D], F32)
        n_src = st.sb("n_src", [LO, CH], F32)
        n_dst = st.sb("n_dst", [LO, CH], F32)
        with Stage(nc, "prop_in") as s2:
            h = s2.sb("h", [LO, CH, D], F32)
            pos = s2.sb("pos", [LO, CH], F32)
            w = s2.sb("w", [D, D], F32)
            bias = s2.sb("bias", [LO, D], F32)
            w_in, chain_sem, rooted, lifted = (s2.sem(n) for n in ("w_in", "chain", "rooted", "lifted"))
            norm_relu(nc, g, "prop_norm", g.x, h[:, :, :])
            with nc.Block() as block:
                @block.sync
                def _(sp):
                    sp.dma_start(w[:, :], W["L2_gnn_W"]).then_inc(w_in, 16)
                    sp.dma_start(bias[:, :], W["L2_gnn_b"].rearrange("(a f) -> a f", a=1).to_broadcast([LO, D])
                                 ).then_inc(w_in, 16)
                    sp.wait_ge(w_in, 32)

                @block.vector
                def _(v):
                    done = Chain(v, chain_sem)
                    for deg, norm in ((g.degree_out, n_src), (g.degree, n_dst)):
                        done(v.tensor_scalar(norm[:, :], deg[:, :], 1.0, None, ALU.max))
                    v.sem_inc(lifted, 1)
                    v.wait_ge(rooted, 2)
                    for n, (deg, norm) in enumerate(((g.degree_out, n_src), (g.degree, n_dst))):
                        done(v.reciprocal(norm[:, :], norm[:, :]))
                        done(v.tensor_scalar(pos[:, :], deg[:, :], 0.0, 1.0 if n == 0 else 0.9, ALU.is_gt, ALU.mult))
                        done(v.tensor_tensor(norm[:, :], norm[:, :], pos[:, :], ALU.mult))

                @block.scalar
                def _(act):
                    act.wait_ge(lifted, 1)
                    act.activation(n_src[:, :], n_src[:, :], ACT.Sqrt).then_inc(rooted, 1)
                    act.activation(n_dst[:, :], n_dst[:, :], ACT.Sqrt).then_inc(rooted, 1)
            linear(nc, g, "prop_lin", h, D, [w[:, :]], D, bias[:, :], h0)

        parts = [st.sb(f"parts{k}", [LO, CH, 3 * D], BF16) for k in range(2)]
        rest = st.sb("rest", [LO, B, D], F32)
        last = st.sb("last", [LO, CH, D], F32)
        acc = [st.ps(f"acc{k}", [LO, 512], F32) for k in range(B)]
        chained, summed, taken, added = (st.sem(n) for n in ("chained", "summed", "taken", "added"))

        def over(a):
            return a.rearrange("p (c a) -> p c a", a=1).to_broadcast([LO, B, D])

        with nc.Block() as block:
            @block.tensor
            def _(pe):
                pe.wait_ge(loaded, 16)
                with pe.Fori(0, STEPS // 2) as pair:
                    for k in range(2):
                        step = pair * 2 + k
                        for cd in range(CH):
                            pe.wait_ge(taken, step * CH + cd + 1)
                            for cs in range(CH):
                                if cd == 0 and cs % B == 0:
                                    pe.wait_ge(chained, (step * NB + cs // B + 1) * OPS)
                                mm = pe.matmul(acc[cd % B][:, 0:3 * D],
                                               counts[:, (cs * CH + cd) * LO:(cs * CH + cd + 1) * LO],
                                               parts[k][:, cs, :], start=(cs == 0), stop=(cs == CH - 1))
                            mm.then_inc(summed, 1)

            @block.vector
            def _(v):
                v.sem_inc(taken, B)

                def messages(n, j, out):
                    done = Chain(v, chained, n * OPS + OPS - 5)
                    c = slice(j * B, (j + 1) * B)
                    done(v.tensor_tensor(rest[:, :, :], rest[:, :, :], over(n_src[:, c]), ALU.mult))
                    split3(v, done, rest[:, :, :], out[:, c, :].rearrange("p c (s f) -> p c s f", s=3), rest[:, :, :])

                for j in range(NB):
                    done = Chain(v, chained, j * OPS)
                    c = slice(j * B, (j + 1) * B)
                    done(v.tensor_copy(rest[:, :, :], h0[:, c, :]))
                    done(v.tensor_scalar(h0[:, c, :], h0[:, c, :], 0.1, None, ALU.mult))
                    messages(j, j, parts[0])
                with v.Fori(0, STEPS // 2) as pair:
                    for k in range(2):
                        for j in range(NB):
                            n = (pair * 2 + k) * NB + j
                            for c in range(B):
                                v.wait_ge(summed, n * B + c + 1)
                                v.tensor_reduce(rest[:, c, :], acc[c][:, 0:3 * D].rearrange("p (s f) -> p f s", s=3),
                                                AX_X, ALU.add).then_inc(taken, 1)
                            v.wait_ge(taken, n * B + 2 * B)
                            done = Chain(v, chained, (n + NB) * OPS)
                            c = slice(j * B, (j + 1) * B)
                            done(v.tensor_tensor(rest[:, :, :], rest[:, :, :], over(n_dst[:, c]), ALU.mult))
                            done(v.tensor_tensor(rest[:, :, :], rest[:, :, :], h0[:, c, :], ALU.add))
                            if k == 1:
                                v.tensor_copy(last[:, c, :], rest[:, :, :])
                            messages(n + NB, j, parts[1 - k])
                v.tensor_tensor(g.x[:, :, :], g.x[:, :, :], last[:, :, :], ALU.add).then_inc(added, 1)
                v.wait_ge(added, 1)


GRP = 4
KG = U // GRP
NG = NT // GRP


def turn_scores(nc, g, name, H, scores, rows):
    with Stage(nc, name) as st:
        part = [st.sb(f"part{k}", [P, NT * H], BF16) for k in range(2)]
        turned = [st.ps(f"turned{k}", [P, 1024], BF16) for k in range(2)]
        chain_sem = st.sem("chain")
        transposed, copied, split = st.sem("transposed"), st.sem("copied"), st.sem("split")
        n_mm = 2 * H * U // 4
        with nc.Block() as block:
            @block.vector
            def _(v):
                done = Chain(v, chain_sem)
                flat = scores[:, :, :].rearrange("p n h -> p (n h)")
                done(v.tensor_copy(part[0][:, :], flat))
                done(v.tensor_tensor(part[1][:, :], flat, part[0][:, :], ALU.subtract))
                v.sem_inc(split, 1)

            @block.tensor
            def _(pe):
                pe.wait_ge(split, 1)
                m = 0
                for h in range(H):
                    for q in range(2):
                        src = part[q][:, :].rearrange("p (n h) -> p n h", h=H)
                        for u in range(0, U, 4):
                            if m >= 2:
                                pe.wait_ge(copied, m - 1)
                            for k in range(4):
                                mm = pe.transpose(turned[m % 2][0:NI, k * P:(k + 1) * P], src[:, u + k:NT:U, h],
                                                  g.ident_b[:, :])
                            mm.then_inc(transposed, 1)
                            m += 1

            @block.scalar
            def _(act):
                m = 0
                for h in range(H):
                    for q in range(2):
                        for u in range(0, U, 4):
                            act.wait_ge(transposed, m + 1)
                            act.activation(rows[:, u:u + 4, h, q, :],
                                           turned[m % 2][0:NI, 0:4 * P].rearrange("i (k e) -> i k e", k=4),
                                           ACT.Copy).then_inc(copied, 1)
                            m += 1


AHEAD = 2
HOT = 4
assert HOT == KG


class Rows:

    def __init__(self, nc, st, sides):
        self.nc, self.sides = nc, sides
        self.ps = [st.ps(f"ps_row{s}", [P, 512], F32) for s in range(len(sides))]
        self.wide = [[st.sb(f"wide{s}_{k}", [LO, GRP * P], BF16) for k in range(2)] for s in range(len(sides))]
        self.hot = [[st.sb(f"hot{s}_{k}", [LO, GRP * P], BF16) for k in range(HOT)] for s in range(len(sides))]
        self.spread, self.copied, self.compared = st.sem("spread"), st.sem("copied"), st.sem("compared")

    def spread_group(self, pe, g, m, i, k):
        n = len(self.sides)
        if not isinstance(m, int) or m > 0:
            pe.wait_ge(self.copied, m * n)
        for ps, rows in zip(self.ps, self.sides):
            pe.matmul(ps[:, :], g.ident_b[0:NI, bass.ds(i, 1)].to_broadcast([NI, P]),
                      rows[:, k * GRP:(k + 1) * GRP, :].rearrange("i u e -> i (u e)"),
                      start=True, stop=True).then_inc(self.spread, 1)

    def copy_group(self, act, m, b):
        n = len(self.sides)
        for s in range(n):
            act.wait_ge(self.spread, m * n + s + 1)
            if not isinstance(m, int) or m >= 2:
                act.wait_ge(self.compared, m * n - 2 * n + s + 1)
            act.activation(self.wide[s][b][:, :], self.ps[s][0:LO, :], ACT.Copy).then_inc(self.copied, 1)

    def compare_side(self, v, g, m, s, b, k):
        v.wait_ge(self.copied, m * len(self.sides) + s + 1)
        v.tensor_scalar(self.hot[s][k][:, :], self.wide[s][b][:, :], g.iota_part[0:LO, 0:1], None, ALU.is_equal
                        ).then_inc(self.compared, 1)


def score_pass(nc, g, name, src_parts, dst_parts, W, finish, slots=None, attr=None, attr_sum=None):
    with Stage(nc, name) as st:
        where = st.sb("where", [1, 2 * NT], I32)
        dsts = st.sb("dsts", [1, NT + GRP], I32)
        rows = Rows(nc, st, (g.row_src, g.row_dst))
        ROOM = 256 if W > P else W
        ps_x = [st.ps(f"ps_x{k}", [P, max(512, GRP * ROOM)], F32) for k in range(2)]
        if attr is not None:
            oh = [st.sb(f"oh{k}", [P, GRP, P], F32) for k in range(2)]
            cols = [st.sb(f"cols{k}", [P, GRP], F32) for k in range(2)]
            A = attr.shape[2]
            ps_a = [st.ps(f"ps_a{k}", [LO, 512], F32) for k in range(2)]
        where_in, cleared, attr_added = st.sem("where_in"), st.sem("cleared"), st.sem("attr_added")
        gathered, used = st.sem("gathered"), st.sem("used")
        hot, attr_mm, staged = st.sem("hot"), st.sem("attr_mm"), st.sem("staged")
        steps = finish(st, ps_x, gathered, used)
        with nc.Block() as block:
            @block.sync
            def _(sp):
                sp.dma_start(where[:, :], g.pairs_dram).then_inc(where_in, 16)
                sp.dma_start(dsts[:, GRP:], g.dst_dram).then_inc(where_in, 16)

            @block.tensor
            def _(pe):
                pe.sem_inc(gathered, 2)
                pe.wait_ge(where_in, 32)
                if attr is not None:
                    pe.sem_inc(attr_mm, GRP)
                def sum_attr(n, b, col):
                    pe.wait_ge(hot, n + 1)
                    pe.wait_ge(attr_added, n * GRP + GRP)
                    for t in range(GRP):
                        pe.matmul(ps_a[b][:, t * A:(t + 1) * A], oh[b][:, t, 0:LO],
                                  attr[:, bass.ds(col + t, 1), :].rearrange("p a h -> p (a h)"),
                                  start=True, stop=True).then_inc(attr_mm, 1)

                for m in range(AHEAD + 1):
                    rows.spread_group(pe, g, m, 0, m)
                with pe.Fori(0, NI) as i:
                    chunk = chunks_of(nc, pe, where, i, 2 * U)
                    for k in range(KG):
                        n, b = i * KG + k, k % 2
                        pe.wait_ge(rows.compared, n * 2 + 2)
                        pe.wait_ge(used, n + 1)
                        for t in range(GRP):
                            cs, cd = chunk[k * 2 * GRP + 2 * t], chunk[k * 2 * GRP + 2 * t + 1]
                            parts = [(rows.hot[0][k], src_parts, cs), (rows.hot[1][k], dst_parts, cd)]
                            for m, (h, table, c) in enumerate(parts):
                                mm = pe.matmul(ps_x[b][:, t * ROOM:t * ROOM + W], h[:, t * P:(t + 1) * P],
                                               table[:, bass.ds(c, 1), 0:W].rearrange("p a f -> p (a f)"),
                                               start=(m == 0), stop=(m == 1))
                        mm.then_inc(gathered, 1)
                        rows.spread_group(pe, g, n + AHEAD + 1, i + (k + AHEAD + 1) // KG, (k + AHEAD + 1) % KG)
                        if attr is not None:
                            sum_attr(n, 1 - b, i * U + k * GRP)
                if attr is not None:
                    sum_attr(NG, (NG - 1) % 2, NT)

            if attr is not None:
                @block.gpsimd
                def _(pool):
                    with pool.Fori(0, NI) as i:
                        for k in range(KG):
                            pool.wait_ge(attr_mm, (i * KG + k) * GRP + GRP)
                            pool.tensor_copy(cols[k % 2][:, :], slots[:, 1, bass.ds(i * U + k * GRP, GRP)]
                                             ).then_inc(staged, 1)

            @block.scalar
            def _(act):
                for m in range(AHEAD + 1):
                    rows.copy_group(act, m, m % 2)
                with act.Fori(0, NI) as i:
                    for k in range(KG):
                        n, b = i * KG + k, k % 2
                        rows.copy_group(act, n + AHEAD + 1, 1 - b)

            @block.vector
            def _(v):
                v.sem_inc(used, 2)
                if attr is not None:
                    v.sem_inc(attr_added, 2 * GRP)
                    v.memset(oh[1][:, :, :], 0.0).then_inc(cleared, 1)
                    v.memset(dsts[:, 0:GRP], 0).then_inc(cleared, 1)
                    v.wait_ge(cleared, 2)
                    v.sem_inc(hot, 1)
                v.wait_ge(where_in, 32)

                def attr_add(n, b, cell, t):
                    v.tensor_tensor(cell, cell, ps_a[b][:, t * A:(t + 1) * A], ALU.add).then_inc(attr_added, 1)

                for m in range(AHEAD):
                    for s in range(2):
                        rows.compare_side(v, g, m, s, m % 2, m)
                with v.Fori(0, NI) as i:
                    if attr is not None:
                        chunk = chunks_of(nc, v, dsts, i)
                    for k in range(KG):
                        n, b = i * KG + k, k % 2
                        steps[0](v, i, n, k, b)
                        v.wait_ge(gathered, n + 1)
                        rows.compare_side(v, g, n + AHEAD, 0, b, (k + AHEAD) % HOT)
                        if attr is not None:
                            v.wait_ge(staged, n + 1)
                            for t in range(GRP):
                                mm = v.tensor_scalar(oh[b][:, t, :], g.iota_free[:, :],
                                                     cols[b][:, t:t + 1], None, ALU.is_equal)
                            mm.then_inc(hot, 1)
                        steps[1](v, i, n, k, b)
                        rows.compare_side(v, g, n + AHEAD, 1, b, (k + AHEAD) % HOT)
                        if attr is not None:
                            v.wait_ge(attr_mm, n * GRP + 2 * GRP)
                            v.wait_ge(attr_added, n * GRP + 2 * GRP)
                            for t in range(GRP):
                                cell = attr_sum[:, t, bass.ds(chunk[k * GRP + t], 1), :].rearrange("p a h -> p (a h)")
                                attr_add(n, 1 - b, cell, t)
                        steps[2](v, i, n, k, b)
                if attr is not None:
                    chunk = chunks_of(nc, v, dsts, NG, GRP)
                    v.wait_ge(attr_mm, NG * GRP + 2 * GRP)
                    v.wait_ge(attr_added, NG * GRP + 2 * GRP)
                    for t in range(GRP):
                        cell = attr_sum[:, t, bass.ds(chunk[t], 1), :].rearrange("p a h -> p (a h)")
                        attr_add(NG, (NG - 1) % 2, cell, t)
                    v.wait_ge(attr_added, NG * GRP + 3 * GRP)
                    for t in range(1, GRP):
                        v.tensor_tensor(attr_sum[:, 0, :, :], attr_sum[:, 0, :, :], attr_sum[:, t, :, :], ALU.add
                                        ).then_inc(cleared, 1)
                        v.wait_ge(cleared, 2 + t)


def max_pass(nc, g, name, H, rows, top):
    TB = GRP // H
    NQ = GRP // TB
    with Stage(nc, name) as st:
        where = st.sb("where", [1, NT + GRP], I32)
        dst_rows = Rows(nc, st, (g.row_dst,))
        tile_top = [st.sb(f"tile_top{k}", [LO, GRP, H], F32) for k in range(2)]
        tops = st.sb("tops", [LO, GRP, CH, H], F32)
        ps_m = [st.ps(f"ps_m{k}", [LO, 512], F32) for k in range(4)]
        where_in, cleared = st.sem("where_in"), st.sem("cleared")
        masked, reduced, raised = st.sem("masked"), st.sem("reduced"), st.sem("raised")
        with nc.Block() as block:
            @block.sync
            def _(sp):
                sp.dma_start(where[:, GRP:], g.dst_dram).then_inc(where_in, 16)

            @block.tensor
            def _(pe):
                pe.sem_inc(masked, 2 * NQ)
                for m in range(AHEAD + 1):
                    dst_rows.spread_group(pe, g, m, 0, m)
                with pe.Fori(0, NI) as i:
                    for k in range(KG):
                        n = i * KG + k
                        pe.wait_ge(dst_rows.compared, n + 1)
                        for q in range(NQ):
                            bank = ps_m[(k * NQ + q) % 4]
                            pe.wait_ge(reduced, n * NQ + q + 1)
                            if H == 1:
                                hot = dst_rows.hot[0][k][:, :]
                            else:
                                hot = dst_rows.hot[0][k][:, q * P:(q + 1) * P].rearrange("p (a e) -> p a e", a=1
                                                                                         ).to_broadcast([LO, H, P])
                            pe.matmul(bank[:, :] if H == 1 else bank[:, :].rearrange("p (h e) -> p h e", h=H),
                                      g.off_diag[0:LO, 0:LO], hot, start=True, stop=False)
                            one = g.ident_b[0:NI, bass.ds(i, 1)].to_broadcast([NI, LO])
                            for part in range(2):
                                r = rows[:, (k * NQ + q) * TB:(k * NQ + q + 1) * TB, :, part, :]
                                mm = pe.matmul(bank[:, :].rearrange("p (u e) -> p u e", u=GRP), one,
                                               r.rearrange("i u h e -> i (u h) e"), start=False, stop=(part == 1))
                            mm.then_inc(masked, 1)
                        dst_rows.spread_group(pe, g, n + AHEAD + 1, i + (k + AHEAD + 1) // KG, (k + AHEAD + 1) % KG)

            @block.scalar
            def _(act):
                for m in range(AHEAD + 1):
                    dst_rows.copy_group(act, m, m % 2)
                with act.Fori(0, NI) as i:
                    for k in range(KG):
                        dst_rows.copy_group(act, i * KG + k + AHEAD + 1, (k + 1) % 2)

            @block.vector
            def _(v):
                v.sem_inc(reduced, 4)
                v.sem_inc(raised, GRP)
                v.memset(tile_top[1][:, :, :], -3.0e38).then_inc(cleared, 1)
                v.memset(where[:, 0:GRP], 0).then_inc(cleared, 1)
                for t in range(GRP):
                    v.tensor_copy(tops[:, t, :, :], top[:, :, :]).then_inc(cleared, 1)
                v.wait_ge(cleared, 2 + GRP)
                v.wait_ge(where_in, 16)

                def raise_top(chunk, b, t):
                    cell = tops[:, t, bass.ds(chunk, 1), :].rearrange("p a h -> p (a h)")
                    v.tensor_tensor(cell, cell, tile_top[b][:, t, :], ALU.max).then_inc(raised, 1)

                for m in range(AHEAD):
                    dst_rows.compare_side(v, g, m, 0, m % 2, m)
                with v.Fori(0, NI) as i:
                    chunk = chunks_of(nc, v, where, i)
                    for k in range(KG):
                        n, b = i * KG + k, k % 2
                        v.wait_ge(masked, n * NQ + NQ)
                        dst_rows.compare_side(v, g, n + AHEAD, 0, b, (k + AHEAD) % HOT)
                        v.wait_ge(raised, n * GRP + GRP)
                        for q in range(NQ):
                            v.wait_ge(masked, (n + 2) * NQ + q + 1)
                            v.tensor_reduce(tile_top[b][:, q * TB:(q + 1) * TB, :].rearrange("p t h -> p (t h)"),
                                            ps_m[(k * NQ + q) % 4][:, :].rearrange("p (u e) -> p u e", u=GRP),
                                            AX_X, ALU.max).then_inc(reduced, 1)
                            if q == 0:
                                v.wait_ge(reduced, n * NQ + 4)
                            for t in range(q * TB, (q + 1) * TB):
                                raise_top(chunk[k * GRP + t], 1 - b, t)
                chunk = chunks_of(nc, v, where, NG, GRP)
                v.wait_ge(reduced, NG * NQ + 4)
                v.wait_ge(raised, NG * GRP + GRP)
                for t in range(GRP):
                    raise_top(chunk[t], (NG - 1) % 2, t)
                v.wait_ge(raised, NG * GRP + 2 * GRP)
                for t in range(GRP):
                    v.tensor_tensor(top[:, :, :], top[:, :, :], tops[:, t, :, :], ALU.max).then_inc(cleared, 1)
                    v.wait_ge(cleared, 3 + GRP + t)


def sum_pass(nc, g, name, H, scores, top_parts, src_parts, slots, total):
    M = H * D + H
    with Stage(nc, name) as st:
        where = st.sb("where", [1, 2 * NT], I32)
        dsts = st.sb("dsts", [1, NT + GRP], I32)
        rows = Rows(nc, st, (g.row_src, g.row_dst))
        oh = [st.sb(f"oh{k}", [P, GRP, P], F32) for k in range(2)]
        cols = [st.sb(f"cols{k}", [P, GRP], F32) for k in range(2)]
        col_hots = ColumnHots(g, st, GRP) if H > 1 else None
        below = [st.sb(f"below{k}", [P, GRP, H], F32) for k in range(2)]
        y = [st.sb(f"y{k}", [P, GRP, M], F32) for k in range(2)]
        ps_x = [st.ps(f"ps_x{k}", [P, 512], F32) for k in range(2)]
        ps_y = [st.ps(f"ps_y{k}", [LO, 512], F32) for k in range(GRP)]
        where_in, cleared, gathered = (st.sem(n) for n in ("where_in", "cleared", "gathered"))
        staged, collected, lowered, weighed = (st.sem(n) for n in ("staged", "collected", "lowered", "weighed"))
        scaled, summed, added = (st.sem(n) for n in ("scaled", "summed", "added"))
        TOP = GRP * D
        with nc.Block() as block:
            @block.sync
            def _(sp):
                sp.dma_start(where[:, :], g.pairs_dram).then_inc(where_in, 16)
                sp.dma_start(dsts[:, GRP:], g.dst_dram).then_inc(where_in, 16)

            @block.tensor
            def _(pe):
                pe.sem_inc(gathered, 2)
                pe.sem_inc(summed, GRP)
                pe.wait_ge(where_in, 32)

                def gather(chunk, k, b):
                    for t in range(GRP):
                        cs, cd = chunk[k * 2 * GRP + 2 * t], chunk[k * 2 * GRP + 2 * t + 1]
                        pe.matmul(ps_x[b][:, TOP + t * 3 * H:TOP + (t + 1) * 3 * H],
                                  rows.hot[1][k][:, t * P:(t + 1) * P],
                                  top_parts[:, bass.ds(cd, 1), :].rearrange("p a f -> p (a f)"), start=True, stop=True)
                        for q in range(3):
                            mm = pe.matmul(ps_x[b][:, t * D:(t + 1) * D], rows.hot[0][k][:, t * P:(t + 1) * P],
                                           src_parts[:, bass.ds(cs, 1), q * D:(q + 1) * D
                                                     ].rearrange("p a f -> p (a f)"),
                                           start=(q == 0), stop=(q == 2))
                    mm.then_inc(gathered, 1)

                def sum_group(n, b):
                    pe.wait_ge(scaled, n + 2)
                    if col_hots is not None:
                        pe.wait_ge(col_hots.hot, n + 1)
                    for t in range(GRP):
                        pe.wait_ge(added, n * GRP + t + 1)
                        pe.matmul(ps_y[t][:, 0:M], oh[b][:, t, 0:LO], y[b][:, t, :], start=True, stop=True
                                  ).then_inc(summed, 1)

                for m in range(AHEAD + 1):
                    rows.spread_group(pe, g, m, 0, m)
                with pe.Fori(0, NI) as i:
                    chunk = chunks_of(nc, pe, where, i, 2 * U)
                    for k in range(KG):
                        n, b = i * KG + k, k % 2
                        pe.wait_ge(rows.compared, n * 2 + 2)
                        pe.wait_ge(scaled, n + 1)
                        gather(chunk, k, b)
                        sum_group(n, 1 - b)
                        rows.spread_group(pe, g, n + AHEAD + 1, i + (k + AHEAD + 1) // KG, (k + AHEAD + 1) % KG)
                sum_group(NG, (NG - 1) % 2)

            @block.gpsimd
            def _(pool):
                with pool.Fori(0, NI) as i:
                    for k in range(KG):
                        pool.wait_ge(summed, (i * KG + k) * GRP + GRP)
                        pool.tensor_copy(cols[k % 2][:, :], slots[:, 1, bass.ds(i * U + k * GRP, GRP)]
                                         ).then_inc(staged, 1)

            @block.scalar
            def _(act):
                for m in range(AHEAD + 1):
                    rows.copy_group(act, m, m % 2)
                with act.Fori(0, NI) as i:
                    for k in range(KG):
                        n, b = i * KG + k, k % 2
                        if col_hots is not None:
                            act.wait_ge(staged, n + 1)
                            act.wait_ge(col_hots.hot, n + 1)
                            col_hots.squares(act, cols[b])
                        act.wait_ge(lowered, n + 1)
                        act.wait_ge(summed, n * GRP + GRP)
                        act.activation(y[b][:, :, H * D:M], below[b][:, :, :], ACT.Exp).then_inc(weighed, 1)
                        if col_hots is not None:
                            col_hots.hots(act, n, oh[b][:, :, :])
                        rows.copy_group(act, n + AHEAD + 1, 1 - b)

            @block.vector
            def _(v):
                v.memset(dsts[:, 0:GRP], 0).then_inc(cleared, 1)
                v.memset(oh[1][:, :, :], 0.0).then_inc(cleared, 1)
                v.memset(y[1][:, :, :], 0.0).then_inc(cleared, 1)
                v.wait_ge(cleared, 3)
                v.sem_inc(scaled, 2)
                if col_hots is not None:
                    v.sem_inc(col_hots.hot, 1)
                v.sem_inc(added, GRP)
                v.wait_ge(where_in, 32)

                def one_hot(b, t):
                    v.tensor_scalar(oh[b][:, t, :], g.iota_free[:, :], cols[b][:, t:t + 1], None, ALU.is_equal)

                def scale(b, t, w):
                    return v.tensor_tensor(
                        y[b][:, t:t + w, 0:H * D].rearrange("p t (h f) -> p t h f", h=H),
                        ps_x[b][:, t * D:(t + w) * D].rearrange("p (t a f) -> p t a f", t=w, a=1
                                                                ).to_broadcast([P, w, H, D]),
                        y[b][:, t:t + w, H * D:M].rearrange("p t (h a) -> p t h a", a=1).to_broadcast([P, w, H, D]),
                        ALU.mult)

                def add(chunk, n, t):
                    v.wait_ge(summed, (n + 1) * GRP + t + 1)
                    v.wait_ge(added, (n + 1) * GRP + t)
                    cell = total[:, bass.ds(chunk, 1), :].rearrange("p a f -> p (a f)")
                    v.tensor_tensor(cell, cell, ps_y[t][:, 0:M], ALU.add).then_inc(added, 1)

                for m in range(AHEAD):
                    for s in range(2):
                        rows.compare_side(v, g, m, s, m % 2, m)
                with v.Fori(0, NI) as i:
                    chunk = chunks_of(nc, v, dsts, i)
                    for k in range(KG):
                        n, b = i * KG + k, k % 2
                        before = chunk[k * GRP:(k + 1) * GRP]
                        v.wait_ge(gathered, n + 3)
                        v.tensor_reduce(below[b][:, :, :].rearrange("p t h -> p (t h)"),
                                        ps_x[b][:, TOP:TOP + GRP * 3 * H].rearrange("p (t s h) -> p t h s", t=GRP, s=3),
                                        AX_X, ALU.add).then_inc(collected, 1)
                        rows.compare_side(v, g, n + AHEAD, 0, b, (k + AHEAD) % HOT)
                        v.wait_ge(collected, n + 1)
                        v.tensor_tensor(below[b][:, :, :], scores[:, bass.ds(i * U + k * GRP, GRP), :],
                                        below[b][:, :, :], ALU.subtract).then_inc(lowered, 1)
                        rows.compare_side(v, g, n + AHEAD, 1, b, (k + AHEAD) % HOT)
                        if col_hots is None:
                            v.wait_ge(staged, n + 1)
                        for t in range(GRP):
                            add(before[t], n, t)
                            if t == (0 if H > 1 else 2):
                                v.wait_ge(weighed, n + 1)
                            if H > 1:
                                mm = scale(b, t, 1)
                            elif t < 2:
                                one_hot(b, 2 * t)
                                one_hot(b, 2 * t + 1)
                            else:
                                mm = scale(b, 2 * t - 4, 2)
                        mm.then_inc(scaled, 1)
                last = chunks_of(nc, v, dsts, NG, GRP)
                for t in range(GRP):
                    add(last[t], NG, t)


def layer_gat2(nc, g, W):
    with Stage(nc, "gat2") as st:
        slots = st.sb("slots", [P, 2, NT], BF16)
        g.row_src = st.sb("row_src", [NI, U, P], BF16)
        g.row_dst = st.sb("row_dst", [NI, U, P], BF16)
        load_slots(nc, g, "load1", slots)
        turn_slots(nc, g, "turn1", slots, g.row_src, g.row_dst)
        h = st.sb("h", [LO, CH, D], F32)
        lr = st.sb("lr", [LO, CH, 2 * D], F32)
        l_parts = st.sb("l_parts", [LO, CH, 3 * D], BF16)
        r_parts = st.sb("r_parts", [LO, CH, 3 * D], BF16)
        rest = st.sb("rest", [LO, CH, D], F32)
        w = st.sb("w", [D, 2 * D], F32)
        bias = st.sb("bias", [LO, 2 * D], F32)
        att = st.sb("att", [P, D], F32)
        tail = st.sb("tail", [LO, 3, D], F32)
        own = st.sb("own", [LO, CH, 1], F32)
        top = st.sb("top", [LO, CH, 1], F32)
        top_parts = st.sb("top_parts", [LO, CH, 3], BF16)
        scores = st.sb("scores", [P, NT, 1], F32)
        rows = st.sb("rows", [NI, U, 1, 2, P], BF16)
        total = st.sb("total", [LO, CH, D + 1], F32)
        w_in = st.sem("w_in")
        chain = [st.sem(f"chain{k}") for k in range(6)]

        def row(name, p, n):
            return W[name].rearrange("(a f) -> a f", a=1).to_broadcast([p, n])

        with nc.Block() as block:
            @block.sync
            def _(sp):
                sp.dma_start(w[:, 0:D], W["L1_gnn_W_l"]).then_inc(w_in, 16)
                sp.dma_start(w[:, D:2 * D], W["L1_gnn_W_r"]).then_inc(w_in, 16)
                sp.dma_start(bias[:, 0:D], row("L1_gnn_b_l", LO, D)).then_inc(w_in, 16)
                sp.dma_start(bias[:, D:2 * D], row("L1_gnn_b_r", LO, D)).then_inc(w_in, 16)
                sp.dma_start(att[:, :], row("L1_gnn_att", P, D)).then_inc(w_in, 16)
                for n, name in enumerate(("L1_gnn_bias", "L1_gnn_gamma", "L1_gnn_beta")):
                    sp.dma_start(tail[:, n, :], row(name, LO, D)).then_inc(w_in, 16)
                sp.wait_ge(w_in, 16 * 8)
        norm_relu(nc, g, "gat2_norm", g.x, h[:, :, :])
        linear(nc, g, "gat2_lin", h, D, [w[:, :]], 2 * D, bias[:, :], lr)
        with nc.Block() as block:
            @block.vector
            def _(v):
                done = Chain(v, chain[0])
                v.memset(total[:, :, :], 0.0)
                for k, parts in enumerate((l_parts, r_parts)):
                    split3(v, done, lr[:, :, k * D:(k + 1) * D],
                           parts[:, :, :].rearrange("p c (s f) -> p c s f", s=3), rest[:, :, :])
                done(v.tensor_tensor(h[:, :, :], lr[:, :, 0:D], lr[:, :, D:2 * D], ALU.add))
                done(v.scalar_tensor_tensor(out=rest[:, :, :], in0=h[:, :, :], scalar=0.2, in1=h[:, :, :],
                                            op0=ALU.mult, op1=ALU.max))
                done(v.tensor_tensor(rest[:, :, :], rest[:, :, :],
                                     att[0:LO, :].rearrange("p (a f) -> p a f", a=1).to_broadcast([LO, CH, D]),
                                     ALU.mult))
                done(v.tensor_reduce(own[:, :, :].rearrange("p c a -> p (c a)"), rest[:, :, :], AX_X, ALU.add))
                done(v.tensor_copy(top[:, :, :], own[:, :, :]))

        def finish(st2, ps_x, gathered, used):
            z = [st2.sb(f"z{k}", [P, GRP, D], F32) for k in range(2)]
            bent = [st2.sb(f"bent{k}", [P, GRP, D], F32) for k in range(2)]
            bent_ready, weighed, scored = (st2.sem(n) for n in ("bent_ready", "weighed", "scored"))

            def collect(v, i, n, k, b):
                v.wait_ge(gathered, n + 3)
                v.tensor_reduce(z[b][:, :, :],
                                ps_x[b][:, :].rearrange("p (t x) -> p t x", t=GRP)[:, :, 0:3 * D]
                                .rearrange("p t (s f) -> p t f s", s=3), AX_X, ALU.add).then_inc(used, 1)

            def bend(v, i, n, k, b):
                v.wait_ge(used, n + 3)
                v.scalar_tensor_tensor(out=bent[b][:, :, :], in0=z[b][:, :, :], scalar=0.2, in1=z[b][:, :, :],
                                       op0=ALU.mult, op1=ALU.max).then_inc(bent_ready, 1)

            def score(v, i, n, k, b):
                v.wait_ge(bent_ready, n + 1)
                v.tensor_tensor(bent[b][:, :, :], bent[b][:, :, :],
                                att[:, :].rearrange("p (a f) -> p a f", a=1).to_broadcast([P, GRP, D]),
                                ALU.mult).then_inc(weighed, 1)
                v.wait_ge(weighed, n + 1)
                v.tensor_reduce(scores[:, bass.ds(i * U + k * GRP, GRP), :].rearrange("p t a -> p (t a)"),
                                bent[b][:, :, :], AX_X, ALU.add).then_inc(scored, 1)
            return collect, bend, score

        score_pass(nc, g, "gat2_score", l_parts, r_parts, 3 * D, finish)
        empty_scores(nc, "gat2_empty", 1, slots, scores)
        turn_scores(nc, g, "gat2_turn", 1, scores, rows)
        max_pass(nc, g, "gat2_max", 1, rows, top)
        with nc.Block() as block:
            @block.vector
            def _(v):
                done = Chain(v, chain[1])
                r = rest[:, :, 0]
                tp = top[:, :, 0]
                done(v.tensor_copy(top_parts[:, :, 0], tp))
                done(v.tensor_tensor(r, tp, top_parts[:, :, 0], ALU.subtract))
                done(v.tensor_copy(top_parts[:, :, 1], r))
                done(v.tensor_tensor(top_parts[:, :, 2], r, top_parts[:, :, 1], ALU.subtract))
        sum_pass(nc, g, "gat2_sum", 1, scores, top_parts, l_parts, slots, total)
        with Stage(nc, "gat2_end") as s2:
            ps = s2.ps("ps", [LO, 512], F32)
            stat = s2.sb("stat", [LO, 2, D], F32)
            part = s2.sb("part", [LO, D], F32)
            ones = s2.sb("ones", [LO, LO], F32)
            weighed, lowered, summed = s2.sem("weighed"), s2.sem("lowered"), s2.sem("summed")
            parted, rooted = s2.sem("parted"), s2.sem("rooted")

            def over(a, shape):
                return a.rearrange("p (a f) -> p a f", a=1).to_broadcast(shape)

            S3 = [LO, CH, D]
            with nc.Block() as block:
                @block.tensor
                def _(pe):
                    for n in range(2):
                        pe.wait_ge(parted, n + 1)
                        pe.matmul(ps[:, n * D:(n + 1) * D], ones[:, :], part[:, :], start=True, stop=True
                                  ).then_inc(summed, 1)

                @block.scalar
                def _(act):
                    act.wait_ge(lowered, 1)
                    act.activation(own[:, :, 0], own[:, :, 0], ACT.Exp).then_inc(weighed, 1)
                    act.wait_ge(lowered, 2)
                    act.activation(stat[:, 1, :], stat[:, 1, :], ACT.Sqrt).then_inc(rooted, 1)

                @block.vector
                def _(v):
                    done = Chain(v, chain[2])
                    done(v.memset(ones[:, :], 1.0))
                    done(v.tensor_tensor(own[:, :, :], own[:, :, :], top[:, :, :], ALU.subtract))
                    v.sem_inc(lowered, 1)
                    v.wait_ge(weighed, 1)
                    done(v.tensor_tensor(rest[:, :, :], lr[:, :, 0:D], own[:, :, :].to_broadcast(S3), ALU.mult))
                    done(v.tensor_tensor(rest[:, :, :], rest[:, :, :], total[:, :, 0:D], ALU.add))
                    done(v.tensor_tensor(own[:, :, :], own[:, :, :], total[:, :, D:D + 1], ALU.add))
                    done(v.reciprocal(own[:, :, :], own[:, :, :]))
                    done(v.tensor_tensor(rest[:, :, :], rest[:, :, :], own[:, :, :].to_broadcast(S3), ALU.mult))
                    done(v.tensor_tensor(rest[:, :, :], rest[:, :, :], over(tail[:, 0, :], S3), ALU.add))
                    done(v.tensor_reduce(part[:, :], rest[:, :, :].rearrange("p c f -> p f c"), AX_X, ALU.add))
                    v.sem_inc(parted, 1)
                    v.wait_ge(summed, 1)
                    done(v.tensor_scalar(stat[:, 0, :], ps[:, 0:D], 1.0 / NODES, None, ALU.mult))
                    done(v.tensor_tensor(rest[:, :, :], rest[:, :, :], over(stat[:, 0, :], S3), ALU.subtract))
                    done(v.tensor_tensor(h[:, :, :], rest[:, :, :], rest[:, :, :], ALU.mult))
                    done(v.tensor_reduce(part[:, :], h[:, :, :].rearrange("p c f -> p f c"), AX_X, ALU.add))
                    v.sem_inc(parted, 1)
                    v.wait_ge(summed, 2)
                    done(v.tensor_scalar(stat[:, 1, :], ps[:, D:2 * D], 1.0 / NODES, 1e-5, ALU.mult, ALU.add))
                    v.sem_inc(lowered, 1)
                    v.wait_ge(rooted, 1)
                    done(v.reciprocal(stat[:, 1, :], stat[:, 1, :]))
                    done(v.tensor_tensor(stat[:, 1, :], stat[:, 1, :], tail[:, 1, :], ALU.mult))
                    done(v.tensor_tensor(rest[:, :, :], rest[:, :, :], over(stat[:, 1, :], S3), ALU.mult))
                    done(v.tensor_tensor(rest[:, :, :], rest[:, :, :], over(tail[:, 2, :], S3), ALU.add))
                    done(v.tensor_tensor(g.x[:, :, :], g.x[:, :, :], rest[:, :, :], ALU.add))


def layer_gat(nc, g, W):
    H = HEADS
    with Stage(nc, "gat") as st:
        slots = st.sb("slots", [P, 2, NT], BF16)
        g.row_src = st.sb("row_src", [NI, U, P], BF16)
        g.row_dst = st.sb("row_dst", [NI, U, P], BF16)
        h = st.sb("h", [LO, CH, D], F32)
        h_parts = st.sb("h_parts", [LO, CH, 3 * D], BF16)
        own = st.sb("own", [LO, CH, H], F32)
        top = st.sb("top", [LO, CH, H], F32)
        top_parts = st.sb("top_parts", [LO, CH, 3 * H], BF16)
        scores = st.sb("scores", [P, NT, H], F32)
        a_sd = st.sb("a_sd", [LO, CH, 2 * H], F32)
        rest4 = st.sb("rest4", [LO, CH, H], F32)
        a_parts = [st.sb(f"a_parts{k}", [LO, CH, 3, H], BF16) for k in range(2)]
        combined = st.sb("combined", [P, 2, D], F32)
        shift = st.sb("shift", [LO, D], F32)
        tail = st.sb("tail", [LO, 3, D], F32)
        chain = [st.sem(f"chain{k}") for k in range(6)]
        norm_relu(nc, g, "gat_norm", g.x, h[:, :, :])

        def row(ap, p, n):
            return ap.to_broadcast([p, n])

        with Stage(nc, "gat_w") as s2:
            w = s2.sb("w", [D, H * D], F32)
            att = s2.sb("att", [D, 2, H * D], F32)
            prod = s2.sb("prod", [D, 2, H * D], F32)
            vec = s2.sb("vec", [D, 2 * H], F32)
            wp = s2.sb("wp", [P, 2, D], F32)
            bias_col = s2.sb("bias_col", [P, 2], F32)
            diag = s2.sb("diag", [P, 2, P], F32)
            none = s2.sb("none", [LO, 2 * H], F32)
            ps_w = s2.ps("ps_w", [P, 512], F32)
            ps_c = s2.ps("ps_c", [P, 512], F32)
            ps_b = s2.ps("ps_b", [LO, 512], F32)
            w_in, turned, laid, mixed = s2.sem("w_in"), s2.sem("turned"), s2.sem("laid"), s2.sem("mixed")
            with nc.Block() as block:
                @block.sync
                def _(sp):
                    sp.dma_start(w[:, :], W["L3_gnn_W"]).then_inc(w_in, 16)
                    for n, name in enumerate(("L3_gnn_att_src", "L3_gnn_att_dst")):
                        sp.dma_start(att[:, n, :], row(W[name].rearrange("(a h) c -> a (h c)", a=1), D, H * D)
                                     ).then_inc(w_in, 16)
                    sp.dma_start(wp[:, :, :], W["L3_gnn_Wp"].rearrange("(b k) f -> k b f", b=2)).then_inc(w_in, 16)
                    sp.dma_start(bias_col[:, :], W["L3_gnn_bias"].rearrange("(b k) -> k b", b=2),
                                 allow_slow_non_contiguous=True).then_inc(w_in, 16)
                    for n, name in enumerate(("L3_gnn_bp", "L3_gnn_gamma", "L3_gnn_beta")):
                        sp.dma_start(tail[:, n, :], row(W[name].rearrange("(a f) -> a f", a=1), LO, D)).then_inc(w_in, 16)
                    sp.wait_ge(w_in, 16 * 8)

                @block.tensor
                def _(pe):
                    pe.wait_ge(w_in, 16 * 8)
                    for b in range(2):
                        pe.transpose(ps_w[:, b * D:(b + 1) * D], w[:, b * P:(b + 1) * P], g.ident[0:D, 0:D]
                                     ).then_inc(turned, 1)
                    pe.wait_ge(laid, 1)
                    for b in range(2):
                        pe.matmul(ps_c[:, b * D:(b + 1) * D], diag[:, b, :], wp[:, b, :], start=True, stop=True
                                  ).then_inc(mixed, 1)
                    for b in range(2):
                        pe.matmul(ps_b[:, 0:D], bias_col[:, b:b + 1].to_broadcast([P, LO]), wp[:, b, :],
                                  start=(b == 0), stop=(b == 1)).then_inc(mixed, 1)

                @block.vector
                def _(v):
                    done = Chain(v, chain[0])
                    v.memset(none[:, :], 0.0)
                    done(v.memset(diag[:, :, :], 0.0))
                    v.wait_ge(turned, 2)
                    for b in range(2):
                        for k in range(2):
                            half = slice(k * D, (k + 1) * D)
                            done(v.tensor_copy(diag[half, b, half], ps_w[half, b * D:(b + 1) * D]))
                    v.sem_inc(laid, 1)
                    v.wait_ge(w_in, 16 * 8)
                    done(v.tensor_tensor(prod[:, :, :], att[:, :, :],
                                         w[:, :].rearrange("p (a c) -> p a c", a=1).to_broadcast([D, 2, H * D]),
                                         ALU.mult))
                    done(v.tensor_reduce(vec[:, :], prod[:, :, :].rearrange("p n (h c) -> p (n h) c", h=H),
                                         AX_X, ALU.add))
                    v.wait_ge(mixed, 4)
                    done(v.tensor_copy(combined[:, :, :].rearrange("p b f -> p (b f)"), ps_c[:, 0:2 * D]))
                    done(v.tensor_tensor(shift[:, :], ps_b[:, 0:D], tail[:, 0, :], ALU.add))
            linear(nc, g, "gat_vec", h, D, [vec[:, :]], 2 * H, none[:, :], a_sd)

        with Stage(nc, "gat_attr") as s2:
            attr = s2.sb("attr", [P, GRP + NT, H], F32)
            attr_sum = s2.sb("attr_sum", [LO, GRP, CH, H], F32)
            inv = s2.sb("inv", [LO, CH], F32)
            rest = s2.sb("rest", [LO, CH, D], F32)
            load_slots(nc, g, "load3", slots, attr[:, GRP:, :])
            turn_slots(nc, g, "turn3", slots, g.row_src, g.row_dst)
            with nc.Block() as block:
                @block.vector
                def _(v):
                    done = Chain(v, chain[1])
                    v.memset(attr[:, 0:GRP, :], 0.0)
                    v.memset(attr_sum[:, :, :, :], 0.0)
                    split3(v, done, h[:, :, :], h_parts[:, :, :].rearrange("p c (s f) -> p c s f", s=3),
                           rest[:, :, :])
                    for k in range(2):
                        split3(v, done, a_sd[:, :, k * H:(k + 1) * H], a_parts[k], rest4[:, :, :])

            def finish(st2, ps_x, gathered, used):
                raw = [st2.sb(f"raw{k}", [P, GRP, H], F32) for k in range(2)]
                with_attr, scored = st2.sem("with_attr"), st2.sem("scored")

                def collect(v, i, n, k, b):
                    v.wait_ge(gathered, n + 3)
                    v.tensor_reduce(raw[b][:, :, :].rearrange("p t h -> p (t h)"),
                                    ps_x[b][:, 0:GRP * 3 * H].rearrange("p (t s h) -> p t h s", t=GRP, s=3),
                                    AX_X, ALU.add).then_inc(used, 1)

                def add_attr(v, i, n, k, b):
                    v.wait_ge(used, n + 3)
                    v.tensor_tensor(raw[b][:, :, :], raw[b][:, :, :], attr[:, bass.ds(i * U + k * GRP + GRP, GRP), :],
                                    ALU.add).then_inc(with_attr, 1)

                def bend(v, i, n, k, b):
                    v.wait_ge(with_attr, n + 1)
                    v.scalar_tensor_tensor(out=scores[:, bass.ds(i * U + k * GRP, GRP), :], in0=raw[b][:, :, :],
                                           scalar=0.2, in1=raw[b][:, :, :], op0=ALU.mult, op1=ALU.max
                                           ).then_inc(scored, 1)
                return collect, add_attr, bend

            score_pass(nc, g, "gat_score", a_parts[0][:, :, :, :].rearrange("p c s h -> p c (s h)"),
                       a_parts[1][:, :, :, :].rearrange("p c s h -> p c (s h)"), 3 * H, finish, slots, attr, attr_sum)
            empty_scores(nc, "gat_empty", H, slots, scores)
            with nc.Block() as block:
                @block.vector
                def _(v):
                    done = Chain(v, chain[2])
                    done(v.tensor_scalar(inv[:, :], g.degree[:, :], 1.0, None, ALU.max))
                    done(v.reciprocal(inv[:, :], inv[:, :]))
                    done(v.tensor_tensor(attr_sum[:, 0, :, :], attr_sum[:, 0, :, :],
                                         inv[:, :].rearrange("p (c a) -> p c a", a=1).to_broadcast([LO, CH, H]),
                                         ALU.mult))
                    done(v.tensor_tensor(own[:, :, :], a_sd[:, :, 0:H], a_sd[:, :, H:2 * H], ALU.add))
                    done(v.tensor_tensor(own[:, :, :], own[:, :, :], attr_sum[:, 0, :, :], ALU.add))
                    done(v.scalar_tensor_tensor(out=own[:, :, :], in0=own[:, :, :], scalar=0.2, in1=own[:, :, :],
                                                op0=ALU.mult, op1=ALU.max))
                    done(v.tensor_copy(top[:, :, :], own[:, :, :]))
        with Stage(nc, "gat_rows") as s2:
            rows = s2.sb("rows", [NI, U, H, 2, P], BF16)
            turn_scores(nc, g, "gat_turn", H, scores, rows)
            max_pass(nc, g, "gat_max", H, rows, top)
        total = st.sb("total", [LO, CH, H * D + H], F32)
        with nc.Block() as block:
            @block.vector
            def _(v):
                done = Chain(v, chain[3])
                v.memset(total[:, :, :], 0.0)
                split3(v, done, top[:, :, :], top_parts[:, :, :].rearrange("p c (s h) -> p c s h", s=3), rest4[:, :, :])
        sum_pass(nc, g, "gat_sum", H, scores, top_parts, h_parts, slots, total)
        with Stage(nc, "gat_end") as s2:
            agg = s2.sb("agg", [LO, CH, H * D], F32)
            proj = s2.sb("proj", [LO, CH, D], F32)
            neg = s2.sb("neg", [LO, CH, D], F32)
            mean = s2.sb("mean", [LO, CH], F32)
            lowered, weighed = s2.sem("lowered"), s2.sem("weighed")

            def over(a):
                return a[:, :].rearrange("p (c a) -> p c a", a=1).to_broadcast([LO, CH, D])

            def all_over(a):
                return a.rearrange("p (a f) -> p a f", a=1).to_broadcast([LO, CH, D])

            with nc.Block() as block:
                @block.scalar
                def _(act):
                    act.wait_ge(lowered, 1)
                    act.activation(own[:, :, :], own[:, :, :], ACT.Exp).then_inc(weighed, 1)

                @block.vector
                def _(v):
                    done = Chain(v, chain[4])
                    done(v.tensor_tensor(own[:, :, :], own[:, :, :], top[:, :, :], ALU.subtract))
                    v.sem_inc(lowered, 1)
                    v.wait_ge(weighed, 1)
                    done(v.tensor_tensor(rest4[:, :, :], own[:, :, :], total[:, :, H * D:], ALU.add))
                    done(v.reciprocal(rest4[:, :, :], rest4[:, :, :]))
                    for k in range(H):
                        part = agg[:, :, k * D:(k + 1) * D]
                        done(v.tensor_tensor(part, h[:, :, :], own[:, :, k:k + 1].to_broadcast([LO, CH, D]), ALU.mult))
                        done(v.tensor_tensor(part, part, total[:, :, k * D:(k + 1) * D], ALU.add))
                        done(v.tensor_tensor(part, part, rest4[:, :, k:k + 1].to_broadcast([LO, CH, D]), ALU.mult))
            linear(nc, g, "gat_proj", agg, P, [combined[:, 0, :], combined[:, 1, :]], D, shift[:, :], proj)
            minned, exped, varied, rooted = s2.sem("minned"), s2.sem("exped"), s2.sem("varied"), s2.sem("rooted")
            with nc.Block() as block:
                @block.scalar
                def _(act):
                    act.wait_ge(minned, 1)
                    act.activation(neg[:, :, :], neg[:, :, :], ACT.Exp).then_inc(exped, 1)
                    act.wait_ge(varied, 1)
                    act.activation(mean[:, :], mean[:, :], ACT.Sqrt).then_inc(rooted, 1)

                @block.vector
                def _(v):
                    done = Chain(v, chain[5])
                    done(v.tensor_scalar(neg[:, :, :], proj[:, :, :], 0.0, None, ALU.min))
                    v.sem_inc(minned, 1)
                    done(v.scalar_tensor_tensor(out=h[:, :, :], in0=proj[:, :, :], scalar=0.0, in1=h[:, :, :],
                                                op0=ALU.max, op1=ALU.add))
                    v.wait_ge(exped, 1)
                    done(v.scalar_tensor_tensor(out=h[:, :, :], in0=neg[:, :, :], scalar=-1.0, in1=h[:, :, :],
                                                op0=ALU.add, op1=ALU.add))
                    done(v.tensor_reduce(mean[:, :], h[:, :, :], AX_X, ALU.add))
                    done(v.tensor_scalar(mean[:, :], mean[:, :], 1.0 / D, None, ALU.mult))
                    done(v.tensor_tensor(h[:, :, :], h[:, :, :], over(mean), ALU.subtract))
                    done(v.tensor_tensor(proj[:, :, :], h[:, :, :], h[:, :, :], ALU.mult))
                    done(v.tensor_reduce(mean[:, :], proj[:, :, :], AX_X, ALU.add))
                    done(v.tensor_scalar(mean[:, :], mean[:, :], 1.0 / D, 1e-5, ALU.mult, ALU.add))
                    v.sem_inc(varied, 1)
                    v.wait_ge(rooted, 1)
                    done(v.reciprocal(mean[:, :], mean[:, :]))
                    done(v.tensor_tensor(h[:, :, :], h[:, :, :], over(mean), ALU.mult))
                    done(v.tensor_tensor(h[:, :, :], h[:, :, :], all_over(tail[:, 1, :]), ALU.mult))
                    done(v.tensor_tensor(h[:, :, :], h[:, :, :], all_over(tail[:, 2, :]), ALU.add))
                    done(v.tensor_tensor(g.x[:, :, :], g.x[:, :, :], h[:, :, :], ALU.add))


def empty_scores(nc, name, H, slots, scores):
    with Stage(nc, name) as st:
        low = st.sb("low", [P, NT], F32)
        chain = st.sem("chain")
        with nc.Block() as block:
            @block.vector
            def _(v):
                done = Chain(v, chain)
                done(v.tensor_scalar(low[:, :], slots[:, 0, :], 0.0, -BIG, ALU.is_lt, ALU.mult))
                for h in range(H):
                    done(v.tensor_tensor(scores[:, :, h], scores[:, :, h], low[:, :], ALU.add))


class Globals:
    pass


def program(nc, x, src, dst, ea16, w_edge, att_edge, out, **W):
    g = Globals()
    with Stage(nc, "g") as st:
        g.iota_free = st.sb("iota_free", [P, P], F32)
        g.iota_b = st.sb("iota_b", [P, P], BF16)
        g.ident = st.sb("ident", [P, P], F32)
        g.ident_h = st.sb("ident_h", [P, P], FP16)
        g.ident_b = st.sb("ident_b", [P, P], BF16)
        g.before = st.sb("before", [P, P], F32)
        g.after = st.sb("after", [P, P], F32)
        g.off_diag = st.sb("off_diag", [P, P], BF16)
        g.cleared = st.sem("cleared")
        g.scattered = [st.sem(f"scattered{k}") for k in range(2)]
        g.iota_part = st.sb("iota_part", [P, 1], F32)
        g.slots = nc.dram_tensor("slots", (P, NT, REC), F32, kind="Internal").ap()
        g.ends_dram = nc.dram_tensor("ends", (CH, CH), F32, kind="Internal").ap()
        g.pairs_dram = nc.dram_tensor("tile_pairs", (1, NT * 2), I32, kind="Internal").ap()
        g.dst_dram = nc.dram_tensor("tile_dst", (1, NT), I32, kind="Internal").ap()
        g.cell_dram = nc.dram_tensor("tile_cell", (1, NT), I32, kind="Internal").ap()
        g.counts_dram = nc.dram_tensor("countsd", (LO, CH * NODES), FP16, kind="Internal").ap()
        build_constants(nc, g)
        sort_edges(nc, g, src, dst, ea16, w_edge, att_edge)
        g.x = st.sb("x", [LO, CH, D], F32)
        g.degree = st.sb("degree", [LO, CH], F32)
        g.degree_out = st.sb("degree_out", [LO, CH], F32)
        x_in, saved, loaded = st.sem("x_in"), st.sem("saved"), st.sem("loaded")
        with Stage(nc, "first") as s2:
            counts = s2.sb("counts", [LO, CH * NODES], FP16)
            with Stage(nc, "slots0") as s3:
                slots = s3.sb("slots", [P, 2, NT], BF16)
                load_slots(nc, g, "load0", slots)
                build_counts(nc, g, counts, slots)
            with nc.Block() as block:
                @block.sync
                def _(sp):
                    sp.dma_start(g.x[:, :, :], x.rearrange("(p c) f -> p c f", p=LO)).then_inc(x_in, 16)
                    sp.wait_ge(x_in, 16)
                    sp.dma_start(g.counts_dram, counts[:, :]).then_inc(saved, 16)
            layer_sage(nc, g, W, counts)
            with nc.Block() as block:
                @block.sync
                def _(sp):
                    sp.wait_ge(saved, 16)
        layer_gat2(nc, g, W)
        with Stage(nc, "second") as s2:
            counts = s2.sb("counts", [LO, CH * NODES], FP16)
            with nc.Block() as block:
                @block.sync
                def _(sp):
                    sp.dma_start(counts[:, :], g.counts_dram).then_inc(loaded, 16)
            layer_appnp(nc, g, W, counts, loaded)
        layer_gat(nc, g, W)
        with nc.Block() as block:
            @block.sync
            def _(sp):
                sp.dma_start(out.rearrange("(p c) f -> p c f", p=LO), g.x[:, :, :]).then_inc(saved, 16)
                sp.wait_ge(saved, 32)


_INS = {"x": "x", "src": "src", "dst": "dst", "ea16": "edge_attr_16", "w_edge": "L3_gnn_W_edge",
        "att_edge": "L3_gnn_att_edge"}
_SAME = ["L0_gnn_Wl0", "L0_gnn_Wr0", "L0_gnn_b0", "L0_gnn_Wl1", "L0_gnn_Wr1", "L0_gnn_b1", "L0_gnn_Wl2",
         "L0_gnn_Wr2", "L0_gnn_b2", "L1_gnn_W_l", "L1_gnn_b_l", "L1_gnn_W_r", "L1_gnn_b_r", "L1_gnn_att",
         "L1_gnn_bias", "L1_gnn_gamma", "L1_gnn_beta", "L2_gnn_W", "L2_gnn_b", "L3_gnn_W", "L3_gnn_att_src",
         "L3_gnn_att_dst", "L3_gnn_bias", "L3_gnn_Wp", "L3_gnn_bp", "L3_gnn_gamma", "L3_gnn_beta"]


def kernel(**inputs):
    import numpy as _np
    import concourse.bacc as _bacc
    from concourse import mybir as _mybir
    from concourse.bass_utils import run_bass_kernel_spmd as _run

    nc = _bacc.Bacc("TRN2", target_bir_lowering=False, num_devices=1)
    arrays, args = {}, {}
    for arg, name in {**_INS, **{n: n for n in _SAME}}.items():
        a = _np.ascontiguousarray(inputs[name])
        arrays[f"in_{name}_dram"] = a
        args[arg] = nc.dram_tensor(f"in_{name}_dram", a.shape, _mybir.dt.from_np(a.dtype), kind="ExternalInput").ap()
    args["out"] = nc.dram_tensor("out_dram", (NODES, D), F32, kind="ExternalOutput").ap()
    program(nc, **args)
    r = _run(nc, [arrays], core_ids=[0])
    return r.results[0]["out_dram"]
```
